# Optimizing a Trainium2 kernel written in Bass

```python
import numpy as np
import jax
import jax.numpy as jnp

def _softmax(x, axis=-1):
    return jax.nn.softmax(x, axis=axis)

def _gelu(x):
    return jax.nn.gelu(x, approximate=True)

def _silu(x):
    return jax.nn.silu(x)

def _sigmoid(x):
    return jax.nn.sigmoid(x)

def _layernorm(x, axis=-1, eps=1e-05):
    m = jnp.mean(x, axis=axis, keepdims=True)
    v = jnp.var(x, axis=axis, keepdims=True)
    return (x - m) / jnp.sqrt(v + eps)

def _scatter_add(tgt, idx, src, axis=0):
    return tgt.at[idx].add(src)

def _segment_sum(src, seg, n):
    return jax.ops.segment_sum(src, seg, n)
kernel_name = 'mk_decoder_preln_d2_seqx_r8_fc5454'

def setup_inputs(seed: int=0):
    np.random.seed(seed)
    _w = jnp.asarray

    def _rec_inputs():
        import jax
        import jax.numpy as jnp
        _rk = jax.random.key(seed)
        x = -0.0002928 + 1 * jax.random.normal(jax.random.fold_in(_rk, 1), (4, 256, 256), jnp.float32)
        _lenS = 256 - jax.random.randint(jax.random.fold_in(_rk, 7), (4,), 0, max(1, 256 // 4) + 1, jnp.int32)
        _lenS2 = 256 - jax.random.randint(jax.random.fold_in(_rk, 8), (4,), 0, max(1, 256 // 4) + 1, jnp.int32)
        _ctx_512P = jax.random.normal(jax.random.fold_in(_rk, 11), (4, 16, 64), jnp.float32)
        _ctx_512c = jax.random.dirichlet(jax.random.fold_in(_rk, 511), 0.3 * jnp.ones((16,), jnp.float32), (4, 256))
        _ctx_512t = jnp.einsum('bsk,bkd->bsd', _ctx_512c, _ctx_512P)
        _ctx_512t = _ctx_512t * jax.lax.rsqrt(jnp.mean(jnp.square(_ctx_512t)) + 1e-12) * 0.953939
        ctx_512 = 0.000227908 + 0.99994 * (_ctx_512t + 0.3 * jax.random.normal(jax.random.fold_in(_rk, 611), (4, 256, 64), jnp.float32))
        return (x, ctx_512)
    x, ctx_512 = _rec_inputs()

    def _L0_attn_setup():
        import jax, jax.numpy as jnp
        import numpy as np
        DIM = 256
        HEADS = 16
        HEAD_DIM = DIM // HEADS
        RANK = 16
        ALPHA = 8.0
        SCALING = ALPHA / RANK
        SCALE = HEAD_DIM ** (-0.5)

        def lora_linear(x, W, b, Bm, Am):
            out = jnp.einsum('bld,od->blo', x, W) + b
            upd = jnp.einsum('blr,or->blo', jnp.einsum('bld,rd->blr', x, Bm), Am)
            return out + SCALING * upd

        def _split(t):
            B, L, D = t.shape
            return t.reshape(B, L, HEADS, HEAD_DIM).transpose(0, 2, 1, 3)
        key = jax.random.key(seed)
        ks = jax.random.split(key, 20)
        B, L = (4, 256)
        x = jax.random.normal(ks[0], (B, L, DIM), dtype=jnp.float32)
        s = 0.02
        inp = {'x': x}
        for i, name in enumerate(['q', 'k', 'v', 'o']):
            inp[f'W{name}'] = jax.random.normal(ks[1 + 4 * i], (DIM, DIM), jnp.float32) * s
            inp[f'b{name}'] = jax.random.normal(ks[2 + 4 * i], (DIM,), jnp.float32) * s
            inp[f'B{name}'] = jax.random.normal(ks[3 + 4 * i], (RANK, DIM), jnp.float32) * s
            inp[f'A{name}'] = jax.random.uniform(ks[4 + 4 * i], (DIM, RANK), jnp.float32, -0.1, 0.1)
        return inp
    _L0_attn_all = _L0_attn_setup()
    _L0_attn_in = {k: v for k, v in _L0_attn_all.items() if k in ('Wq', 'bq', 'Bq', 'Aq', 'Wk', 'bk', 'Bk', 'Ak', 'Wv', 'bv', 'Bv', 'Av', 'Wo', 'bo', 'Bo', 'Ao')}
    del _L0_attn_all

    def _L0_xattn_setup():
        import jax, jax.numpy as jnp
        import numpy as np
        B, S, L = (2, 128, 128)
        DIM_Q, H, K, D_C, D_CQ, R = (256, 16, 128, 64, 192, 64)

        def _rope_tables(length, dim):
            inv = 1.0 / 10000.0 ** (jnp.arange(0, dim, 2, dtype=jnp.float32) / dim)
            f = jnp.arange(length, dtype=jnp.float32)[:, None] * inv[None, :]
            sin = jnp.repeat(jnp.sin(f), 2, axis=-1)
            cos = jnp.repeat(jnp.cos(f), 2, axis=-1)
            return (sin, cos)

        def _rotate_half(x):
            half = x.shape[-1] // 2
            return jnp.concatenate([-x[..., half:], x[..., :half]], axis=-1)

        def _apply_rope(x, sin, cos):
            return x * cos + _rotate_half(x) * sin
        key = jax.random.key(seed)
        ks = jax.random.split(key, 8)
        return {'hidden_q': jax.random.normal(ks[0], (B, S, DIM_Q), jnp.float32), 'kv_c': jax.random.normal(ks[1], (B, L, D_C), jnp.float32), 'Wq': jax.random.normal(ks[2], (H * K, DIM_Q), jnp.float32) / np.sqrt(DIM_Q).astype(np.float32), 'w_kc_q': jax.random.normal(ks[3], (H, K, D_CQ), jnp.float32) / np.sqrt(K).astype(np.float32), 'w_kc_kv': jax.random.normal(ks[4], (H, K, D_C), jnp.float32) / np.sqrt(K).astype(np.float32), 'W_qr': jax.random.normal(ks[5], (H, D_CQ, R), jnp.float32) / np.float32(np.sqrt(D_CQ) * np.sqrt(R)), 'W_kr': jax.random.normal(ks[6], (H, D_C, R), jnp.float32) / np.sqrt(D_C).astype(np.float32), 'Wo': jax.random.normal(ks[7], (DIM_Q, H * K), jnp.float32) / np.sqrt(H * K).astype(np.float32)}
    _L0_xattn_all = _L0_xattn_setup()
    _L0_xattn_in = {k: v for k, v in _L0_xattn_all.items() if k in ('Wq', 'w_kc_q', 'w_kc_kv', 'W_qr', 'W_kr', 'Wo')}
    del _L0_xattn_all

    def _L0_ffn_setup():
        import jax, jax.numpy as jnp
        import numpy as np
        EPS = 1e-05
        RMS_EPS = 1e-06

        def activation_quant(x, num_bits=8):
            qn = -2 ** (num_bits - 1)
            qp = 2 ** (num_bits - 1) - 1
            xf = x.astype(jnp.float32)
            s = qp / jnp.clip(jnp.max(jnp.abs(xf), axis=-1, keepdims=True), EPS, None)
            return (jnp.clip(jnp.round(xf * s), qn, qp) / s).astype(x.dtype)

        def weight_quant(w):
            wf = w.astype(jnp.float32)
            s = 1.0 / jnp.clip(jnp.mean(jnp.abs(wf)), EPS, None)
            return (jnp.clip(jnp.round(wf * s), -1.0, 1.0) / s).astype(w.dtype)

        def bit_linear(x, w):
            qx = x + jax.lax.stop_gradient(activation_quant(x) - x)
            qw = w + jax.lax.stop_gradient(weight_quant(w) - w)
            return jnp.einsum('bsh,oh->bso', qx, qw)

        def rms_norm(x, weight, eps=RMS_EPS):
            xf = x.astype(jnp.float32)
            var = jnp.mean(xf * xf, axis=-1, keepdims=True)
            return weight * (xf * jax.lax.rsqrt(var + eps)).astype(x.dtype)
        key = jax.random.key(seed)
        k1, k2, k3, k4 = jax.random.split(key, 4)
        B, S, H, I = (2, 256, 256, 1024)
        scale = 1.0 / np.sqrt(H)
        return {'x': jax.random.normal(k1, (B, S, H), dtype=jnp.float32), 'w_gate': jax.random.normal(k2, (I, H), dtype=jnp.float32) * scale, 'w_up': jax.random.normal(k3, (I, H), dtype=jnp.float32) * scale, 'w_down': jax.random.normal(k4, (H, I), dtype=jnp.float32) * (1.0 / np.sqrt(I)), 'ln_weight': jnp.ones((I,), dtype=jnp.float32)}
    _L0_ffn_all = _L0_ffn_setup()
    _L0_ffn_in = {k: v for k, v in _L0_ffn_all.items() if k in ('w_gate', 'w_up', 'w_down', 'ln_weight')}
    del _L0_ffn_all

    def _L1_attn_setup():
        import jax, jax.numpy as jnp
        import numpy as np
        B, S, D, H = (2, 256, 256, 16)
        HD = D // H
        NEG = jnp.float32(-1000000000.0)
        key = jax.random.key(seed)
        ks = jax.random.split(key, 6)
        slopes = np.array([2 ** (-8.0 * (i + 1) / H) for i in range(H)], dtype=np.float32)
        return {'hidden_states': jax.random.normal(ks[0], (B, S, D), jnp.float32), 'qkv_w': jax.random.normal(ks[1], (3 * D, D), jnp.float32) * (1.0 / np.sqrt(D)), 'qkv_b': jax.random.normal(ks[2], (3 * D,), jnp.float32) * 0.01, 'out_w': jax.random.normal(ks[3], (D, D), jnp.float32) * (1.0 / np.sqrt(D)), 'out_b': jax.random.normal(ks[4], (D,), jnp.float32) * 0.01, 'alibi_slopes': jnp.asarray(slopes)}
    _L1_attn_all = _L1_attn_setup()
    _L1_attn_in = {k: v for k, v in _L1_attn_all.items() if k in ('qkv_w', 'qkv_b', 'out_w', 'out_b', 'alibi_slopes')}
    del _L1_attn_all

    def _L1_xattn_setup():
        import jax, jax.numpy as jnp
        import numpy as np
        B, S, E = (2, 256, 256)
        QH, KVH = (32, 8)
        D = E // QH
        G = QH // KVH
        DROPOUT = 1.0
        key = jax.random.key(seed)
        k1, k2, k3 = jax.random.split(key, 3)
        q = jax.random.normal(k1, (B, S, E), dtype=jnp.float32)
        k = jax.random.normal(k2, (B, S, E // G), dtype=jnp.float32)
        v = jax.random.normal(k3, (B, S, E // G), dtype=jnp.float32)
        return {'q': q, 'k': k, 'v': v}
    _L1_xattn_all = _L1_xattn_setup()
    _L1_xattn_in = {k: v for k, v in _L1_xattn_all.items() if k in ()}
    del _L1_xattn_all

    def _L1_ffn_setup():
        import jax, jax.numpy as jnp
        import numpy as np
        TOP_K = 2
        NUM_EXPERTS = 8
        ROUTE_SCALE = 1.0
        key = jax.random.key(seed)
        ks = jax.random.split(key, 8)
        bs, slen, dim, hidden, E = (4, 128, 256, 128, NUM_EXPERTS)
        s = 0.02
        return {'x': jax.random.normal(ks[0], (bs, slen, dim), jnp.float32), 'gate_w': jax.random.normal(ks[1], (E, dim), jnp.float32) * s, 'w1': jax.random.normal(ks[2], (E, hidden, dim), jnp.float32) * s, 'w2': jax.random.normal(ks[3], (E, dim, hidden), jnp.float32) * s, 'w3': jax.random.normal(ks[4], (E, hidden, dim), jnp.float32) * s, 'ws1': jax.random.normal(ks[5], (hidden, dim), jnp.float32) * s, 'ws2': jax.random.normal(ks[6], (dim, hidden), jnp.float32) * s, 'ws3': jax.random.normal(ks[7], (hidden, dim), jnp.float32) * s}
    _L1_ffn_all = _L1_ffn_setup()
    _L1_ffn_in = {k: v for k, v in _L1_ffn_all.items() if k in ('gate_w', 'w1', 'w2', 'w3', 'ws1', 'ws2', 'ws3')}
    del _L1_ffn_all
    return {'x': x, 'ctx_512': ctx_512, 'L0_attn_Wq': _L0_attn_in['Wq'], 'L0_attn_bq': _L0_attn_in['bq'], 'L0_attn_Bq': _L0_attn_in['Bq'], 'L0_attn_Aq': _L0_attn_in['Aq'], 'L0_attn_Wk': _L0_attn_in['Wk'], 'L0_attn_bk': _L0_attn_in['bk'], 'L0_attn_Bk': _L0_attn_in['Bk'], 'L0_attn_Ak': _L0_attn_in['Ak'], 'L0_attn_Wv': _L0_attn_in['Wv'], 'L0_attn_bv': _L0_attn_in['bv'], 'L0_attn_Bv': _L0_attn_in['Bv'], 'L0_attn_Av': _L0_attn_in['Av'], 'L0_attn_Wo': _L0_attn_in['Wo'], 'L0_attn_bo': _L0_attn_in['bo'], 'L0_attn_Bo': _L0_attn_in['Bo'], 'L0_attn_Ao': _L0_attn_in['Ao'], 'L0_xattn_Wq': _L0_xattn_in['Wq'], 'L0_xattn_w_kc_q': _L0_xattn_in['w_kc_q'], 'L0_xattn_w_kc_kv': _L0_xattn_in['w_kc_kv'], 'L0_xattn_W_qr': _L0_xattn_in['W_qr'], 'L0_xattn_W_kr': _L0_xattn_in['W_kr'], 'L0_xattn_Wo': _L0_xattn_in['Wo'], 'L0_ffn_w_gate': _L0_ffn_in['w_gate'], 'L0_ffn_w_up': _L0_ffn_in['w_up'], 'L0_ffn_w_down': _L0_ffn_in['w_down'], 'L0_ffn_ln_weight': _L0_ffn_in['ln_weight'], 'L1_attn_qkv_w': _L1_attn_in['qkv_w'], 'L1_attn_qkv_b': _L1_attn_in['qkv_b'], 'L1_attn_out_w': _L1_attn_in['out_w'], 'L1_attn_out_b': _L1_attn_in['out_b'], 'L1_attn_alibi_slopes': _L1_attn_in['alibi_slopes'], 'L1_ffn_gate_w': _L1_ffn_in['gate_w'], 'L1_ffn_w1': _L1_ffn_in['w1'], 'L1_ffn_w2': _L1_ffn_in['w2'], 'L1_ffn_w3': _L1_ffn_in['w3'], 'L1_ffn_ws1': _L1_ffn_in['ws1'], 'L1_ffn_ws2': _L1_ffn_in['ws2'], 'L1_ffn_ws3': _L1_ffn_in['ws3']}

def reference(x, ctx_512, L0_attn_Wq, L0_attn_bq, L0_attn_Bq, L0_attn_Aq, L0_attn_Wk, L0_attn_bk, L0_attn_Bk, L0_attn_Ak, L0_attn_Wv, L0_attn_bv, L0_attn_Bv, L0_attn_Av, L0_attn_Wo, L0_attn_bo, L0_attn_Bo, L0_attn_Ao, L0_xattn_Wq, L0_xattn_w_kc_q, L0_xattn_w_kc_kv, L0_xattn_W_qr, L0_xattn_W_kr, L0_xattn_Wo, L0_ffn_w_gate, L0_ffn_w_up, L0_ffn_w_down, L0_ffn_ln_weight, L1_attn_qkv_w, L1_attn_qkv_b, L1_attn_out_w, L1_attn_out_b, L1_attn_alibi_slopes, L1_ffn_gate_w, L1_ffn_w1, L1_ffn_w2, L1_ffn_w3, L1_ffn_ws1, L1_ffn_ws2, L1_ffn_ws3):
    import jax
    import jax.numpy as jnp

    def _L0_attn_ref(x, Wq, bq, Bq, Aq, Wk, bk, Bk, Ak, Wv, bv, Bv, Av, Wo, bo, Bo, Ao):
        import jax, jax.numpy as jnp
        import numpy as np
        DIM = 256
        HEADS = 16
        HEAD_DIM = DIM // HEADS
        RANK = 16
        ALPHA = 8.0
        SCALING = ALPHA / RANK
        SCALE = HEAD_DIM ** (-0.5)

        def lora_linear(x, W, b, Bm, Am):
            out = jnp.einsum('bld,od->blo', x, W) + b
            upd = jnp.einsum('blr,or->blo', jnp.einsum('bld,rd->blr', x, Bm), Am)
            return out + SCALING * upd

        def _split(t):
            B, L, D = t.shape
            return t.reshape(B, L, HEADS, HEAD_DIM).transpose(0, 2, 1, 3)
        q = _split(lora_linear(x, Wq, bq, Bq, Aq))
        k = _split(lora_linear(x, Wk, bk, Bk, Ak))
        v = _split(lora_linear(x, Wv, bv, Bv, Av))
        scores = jnp.einsum('bhqd,bhkd->bhqk', q, k) * SCALE
        attn = jax.nn.softmax(scores, axis=-1)
        out = jnp.einsum('bhqk,bhkd->bhqd', attn, v)
        B, H, L, hd = out.shape
        out = out.transpose(0, 2, 1, 3).reshape(B, L, H * hd)
        return lora_linear(out, Wo, bo, Bo, Ao)

    def _L0_xattn_ref(hidden_q, kv_c, Wq, w_kc_q, w_kc_kv, W_qr, W_kr, Wo):
        import jax, jax.numpy as jnp
        import numpy as np
        B, S, L = (2, 128, 128)
        DIM_Q, H, K, D_C, D_CQ, R = (256, 16, 128, 64, 192, 64)

        def _rope_tables(length, dim):
            inv = 1.0 / 10000.0 ** (jnp.arange(0, dim, 2, dtype=jnp.float32) / dim)
            f = jnp.arange(length, dtype=jnp.float32)[:, None] * inv[None, :]
            sin = jnp.repeat(jnp.sin(f), 2, axis=-1)
            cos = jnp.repeat(jnp.cos(f), 2, axis=-1)
            return (sin, cos)

        def _rotate_half(x):
            half = x.shape[-1] // 2
            return jnp.concatenate([-x[..., half:], x[..., :half]], axis=-1)

        def _apply_rope(x, sin, cos):
            return x * cos + _rotate_half(x) * sin
        Bv, Sv, _ = hidden_q.shape
        _, Lv, _ = kv_c.shape
        q_hk = (hidden_q @ Wq.T).reshape(Bv, Sv, H, K)
        q_big = jnp.einsum('bshk,hkq->bshq', q_hk, w_kc_q)
        sin_q, cos_q = _rope_tables(Sv, D_CQ)
        q_big = _apply_rope(q_big, sin_q[None, :, None, :], cos_q[None, :, None, :])
        sin_k, cos_k = _rope_tables(Lv, D_C)
        kv_r = _apply_rope(kv_c, sin_k[None], cos_k[None])
        q_r = jnp.einsum('bshq,hqr->bhsr', q_big, W_qr)
        k_r = jnp.einsum('bld,hdr->bhlr', kv_r, W_kr)
        scores = jnp.einsum('bhsr,bhlr->bhsl', q_r, k_r)
        attn = jax.nn.softmax(scores, axis=-1)
        ctx_c = jnp.einsum('bhsl,bld->bhsd', attn, kv_r)
        ctx_lat = jnp.einsum('bhsd,hkd->bhsk', ctx_c, w_kc_kv)
        ctx = ctx_lat.transpose(0, 2, 1, 3).reshape(Bv, Sv, H * K)
        return ctx @ Wo.T

    def _L0_ffn_ref(x, w_gate, w_up, w_down, ln_weight):
        import jax, jax.numpy as jnp
        import numpy as np
        EPS = 1e-05
        RMS_EPS = 1e-06

        def activation_quant(x, num_bits=8):
            qn = -2 ** (num_bits - 1)
            qp = 2 ** (num_bits - 1) - 1
            xf = x.astype(jnp.float32)
            s = qp / jnp.clip(jnp.max(jnp.abs(xf), axis=-1, keepdims=True), EPS, None)
            return (jnp.clip(jnp.round(xf * s), qn, qp) / s).astype(x.dtype)

        def weight_quant(w):
            wf = w.astype(jnp.float32)
            s = 1.0 / jnp.clip(jnp.mean(jnp.abs(wf)), EPS, None)
            return (jnp.clip(jnp.round(wf * s), -1.0, 1.0) / s).astype(w.dtype)

        def bit_linear(x, w):
            qx = x + jax.lax.stop_gradient(activation_quant(x) - x)
            qw = w + jax.lax.stop_gradient(weight_quant(w) - w)
            return jnp.einsum('bsh,oh->bso', qx, qw)

        def rms_norm(x, weight, eps=RMS_EPS):
            xf = x.astype(jnp.float32)
            var = jnp.mean(xf * xf, axis=-1, keepdims=True)
            return weight * (xf * jax.lax.rsqrt(var + eps)).astype(x.dtype)
        h = jax.nn.silu(bit_linear(x, w_gate)) * bit_linear(x, w_up)
        h = rms_norm(h, ln_weight)
        return bit_linear(h, w_down)

    def _L1_attn_ref(hidden_states, qkv_w, qkv_b, out_w, out_b, alibi_slopes):
        import jax, jax.numpy as jnp
        import numpy as np
        B, S, D, H = (2, 256, 256, 16)
        HD = D // H
        NEG = jnp.float32(-1000000000.0)
        b, s, d = hidden_states.shape
        qkv = hidden_states @ qkv_w.T + qkv_b
        q, k, v = jnp.split(qkv, 3, axis=-1)
        q = q.reshape(b, s, H, HD)
        k = k.reshape(b, s, H, HD)
        v = v.reshape(b, s, H, HD)
        scale = 1.0 / np.sqrt(HD)
        scores = jnp.einsum('bqhd,bkhd->bhqk', q, k) * scale
        pos = jnp.arange(s)
        rel = (pos[None, :] - pos[:, None]).astype(jnp.float32)
        bias = alibi_slopes[:, None, None] * rel
        causal = pos[None, :] <= pos[:, None]
        scores = jnp.where(causal[None, None], scores + bias[None], NEG)
        attn = jax.nn.softmax(scores, axis=-1)
        out = jnp.einsum('bhqk,bkhd->bqhd', attn, v).reshape(b, s, d)
        out = out @ out_w.T + out_b
        return out

    def _L1_xattn_ref(q, k, v):
        import jax, jax.numpy as jnp
        import numpy as np
        B, S, E = (2, 256, 256)
        QH, KVH = (32, 8)
        D = E // QH
        G = QH // KVH
        DROPOUT = 1.0
        b, s, _ = q.shape
        qh = q.reshape(b, s, KVH, G, D).transpose(0, 2, 3, 1, 4)
        kh = k.reshape(b, s, KVH, D).transpose(0, 2, 1, 3)
        vh = v.reshape(b, s, KVH, D).transpose(0, 2, 1, 3)
        scale = 1.0 / jnp.sqrt(jnp.float32(D))
        scores = jnp.einsum('bkgsd,bktd->bkgst', qh, kh) * scale
        attn = jax.nn.softmax(scores, axis=-1) / DROPOUT
        out = jnp.einsum('bkgst,bktd->bkgsd', attn, vh)
        return out.transpose(0, 3, 1, 2, 4).reshape(b, s, E)

    def _L1_ffn_ref(x, gate_w, w1, w2, w3, ws1, ws2, ws3):
        import jax, jax.numpy as jnp
        import numpy as np
        TOP_K = 2
        NUM_EXPERTS = 8
        ROUTE_SCALE = 1.0
        bs, slen, dim = x.shape
        xf = x.reshape(-1, dim)
        logits = (xf @ gate_w.T).astype(jnp.float32)
        scores = jax.nn.sigmoid(logits)
        top_scores, sel_idx = jax.lax.top_k(scores, TOP_K)
        top_scores = top_scores * ROUTE_SCALE
        routed = jnp.zeros_like(xf)
        for k in range(TOP_K):
            xs = xf * top_scores[:, k][:, None]
            h1 = jnp.einsum('td,ehd->teh', xs, w1)
            h3 = jnp.einsum('td,ehd->teh', xs, w3)
            h = jax.nn.silu(h1) * h3
            onehot = jax.nn.one_hot(sel_idx[:, k], NUM_EXPERTS, dtype=h.dtype)
            routed = routed + jnp.einsum('teh,te,edh->td', h, onehot, w2)
        shared = jax.nn.silu(xf @ ws1.T) * (xf @ ws3.T) @ ws2.T
        out = (shared + routed).reshape(bs, slen, dim)
        return out
    x = x + _L0_attn_ref(_layernorm(x, axis=-1), L0_attn_Wq, L0_attn_bq, L0_attn_Bq, L0_attn_Aq, L0_attn_Wk, L0_attn_bk, L0_attn_Bk, L0_attn_Ak, L0_attn_Wv, L0_attn_bv, L0_attn_Bv, L0_attn_Av, L0_attn_Wo, L0_attn_bo, L0_attn_Bo, L0_attn_Ao)
    x = x + _L0_xattn_ref(_layernorm(x, axis=-1), ctx_512, L0_xattn_Wq, L0_xattn_w_kc_q, L0_xattn_w_kc_kv, L0_xattn_W_qr, L0_xattn_W_kr, L0_xattn_Wo)
    x = x + _L0_ffn_ref(_layernorm(x, axis=-1), L0_ffn_w_gate, L0_ffn_w_up, L0_ffn_w_down, L0_ffn_ln_weight)
    x = x + _L1_attn_ref(_layernorm(x, axis=-1), L1_attn_qkv_w, L1_attn_qkv_b, L1_attn_out_w, L1_attn_out_b, L1_attn_alibi_slopes)
    x = x + _L1_xattn_ref(_layernorm(x, axis=-1), ctx_512, ctx_512)
    x = x + _L1_ffn_ref(_layernorm(x, axis=-1), L1_ffn_gate_w, L1_ffn_w1, L1_ffn_w2, L1_ffn_w3, L1_ffn_ws1, L1_ffn_ws2, L1_ffn_ws3)
    return x

_drawn_inputs = setup_inputs


def setup_inputs(seed=0):
    import zlib

    import numpy as np

    out = dict(_drawn_inputs(seed))
    spreads = {'L0_ffn_ln_weight': (1.0, 0.2)}
    factors = {'L0_attn_Wq': 6.514,
     'L0_attn_bq': 8.0,
     'L0_attn_Bq': 8.0,
     'L0_attn_Aq': 8.0,
     'L0_attn_Wk': 6.439,
     'L0_attn_bk': 8.0,
     'L0_attn_Bk': 8.0,
     'L0_attn_Ak': 8.0,
     'L0_attn_Wv': 3.879,
     'L0_attn_bv': 3.838,
     'L0_attn_Bv': 7.025,
     'L0_attn_Av': 7.454,
     'L0_attn_Wo': 3.37,
     'L0_attn_Bo': 6.846,
     'L0_attn_Ao': 6.782,
     'L1_attn_qkv_b': 6.39,
     'L1_attn_out_b': 8.0,
     'L1_ffn_gate_w': 8.0,
     'L1_ffn_w1': 8.0,
     'L1_ffn_w2': 8.0,
     'L1_ffn_w3': 8.0,
     'L1_ffn_ws1': 8.0,
     'L1_ffn_ws2': 8.0,
     'L1_ffn_ws3': 8.0}
    for name, (base, spread) in spreads.items():
        noise = np.random.default_rng([zlib.crc32(name.encode()), seed]).standard_normal(out[name].shape)
        drawn = base * np.exp(spread * noise) if base else spread * noise
        out[name] = jnp.asarray(drawn.astype(out[name].dtype))
    for name, factor in factors.items():
        out[name] = (out[name] * factor).astype(out[name].dtype)
    return out
```

```python
from contextlib import ExitStack

import numpy as np

import concourse.bass as bass
from concourse import mybir

F32 = mybir.dt.float32
BF16 = mybir.dt.bfloat16
U32 = mybir.dt.uint32
ALU = mybir.AluOpType
ACT = mybir.ActivationFunctionType
AX = mybir.AxisListType

P = 128
BATCH, SEQ, DIM = 4, 256, 256
CTX = 64
TOK = BATCH * SEQ
TT = TOK // P
DT = DIM // P
QT = SEQ // P
BANK = 512
HALF = TOK // BANK
LN_EPS = 1e-5
RMS_EPS = 1e-6
QUANT_EPS = 1e-5
INT8_MAX, INT8_MIN = 127.0, -128.0
ROUND = 1.5 * 2.0**23
NEG = -1.0e30
FFN = 1024
EXPERTS, TOPK, EH = 8, 2, 128
ITEMS = 8
TERMS = 6
SCOLS = 32


class Signal:

    def __init__(self, sem):
        self.sem = sem
        self.base = 0

    def at(self, n):
        return n + self.base

    def done(self, n):
        self.base += n


class Chip:

    def __init__(self, nc, ctx, io):
        self.nc, self.ctx, self.io = nc, ctx, io
        self.counters = {}

    def sbuf(self, name, shape, dtype=F32):
        return self.ctx.enter_context(self.nc.sbuf_tensor(name, shape, dtype))

    def counter(self, name):
        if name not in self.counters:
            self.counters[name] = Signal(self.ctx.enter_context(self.nc.semaphore(name)))
        return self.counters[name]



def load_stage(c):
    nc, io = c.nc, c.io
    c.ps = c.ctx.enter_context(nc.psum_tensor("ps", [P, 8, BANK], F32))
    c.x = c.sbuf("x", [P, TT, DIM])
    c.xnT = c.sbuf("xnT", [P, DT, TOK])
    c.ident = c.sbuf("ident", [P, P])
    c.identb = c.sbuf("identb", [P, P], BF16)
    c.qs = c.sbuf("qs", [P, ITEMS, 4, SEQ], BF16)
    c.ks = c.sbuf("ks", [P, ITEMS, 4, SEQ], BF16)
    cleared = c.counter("cleared")
    x_in = c.counter("x_in")
    const_in = c.counter("const_in")
    ident_cast = c.counter("ident_cast")

    with nc.Block() as block:

        @block.sync
        def _(sp):
            sp.dma_start(c.x[:, :, :], io["x"].rearrange("(t p) d -> p t d", p=P)).then_inc(x_in.sem, 16)
            sp.dma_start(c.ident[:, :], io["ident"]).then_inc(const_in.sem, 16)

        @block.gpsimd
        def _(pool):
            for k, (tile, value) in enumerate(((c.qs[:, :, :, :].bitcast(F32), 0.0),
                                               (c.ks[0:96, :, :, :].bitcast(F32), 0.0),
                                               (c.ks[96:P, :, :, :], 1.0),
                                               (c.ks[96:P - 2, :, :, :].bitcast(F32), 0.0))):
                pool.memset(tile, value).then_inc(cleared.sem, 1)
                pool.wait_ge(cleared.sem, cleared.at(k + 1))

        @block.vector
        def _(dve):
            dve.wait_ge(const_in.sem, 16)
            dve.wait_ge(x_in.sem, 16)
            dve.tensor_copy(c.identb[:, :], c.ident[:, :]).then_inc(ident_cast.sem, 1)
            dve.wait_ge(ident_cast.sem, 1)



def layer_norm(c, name, want_t=True):
    nc = c.nc
    with ExitStack() as st:
        stats = st.enter_context(nc.sbuf_tensor(f"{name}_stats", [P, TT, 6], F32))
        mv = st.enter_context(nc.sbuf_tensor(f"{name}_mv", [P, TT, 2], F32))
        std = st.enter_context(nc.sbuf_tensor(f"{name}_std", [P, TT], F32))
        rstd = st.enter_context(nc.sbuf_tensor(f"{name}_rstd", [P, TT], F32))
        stats_done, mv_done, var_done = c.counter("ln_stats"), c.counter("ln_mv"), c.counter("ln_var")
        std_done, rstd_done = c.counter("ln_std"), c.counter("ln_rstd")
        xn_done, tr_done, ev_done = c.counter("ln_xn"), c.counter("ln_tr"), c.counter("ln_ev")

        with nc.Block() as block:

            @block.vector
            def _(dve):
                for t in range(TT):
                    dve.bn_stats(stats[:, t, :], c.x[:, t, :]).then_inc(stats_done.sem, 1)
                for t in range(TT):
                    dve.wait_ge(stats_done.sem, stats_done.at(t + 1))
                    dve.bn_aggr(mv[:, t, :], stats[:, t, :]).then_inc(mv_done.sem, 1)
                dve.wait_ge(mv_done.sem, mv_done.at(TT))
                dve.tensor_scalar(std[:, :], mv[:, :, 1], LN_EPS, None, ALU.add).then_inc(var_done.sem, 1)
                dve.wait_ge(std_done.sem, std_done.at(1))
                dve.reciprocal(rstd[:, :], std[:, :]).then_inc(rstd_done.sem, 1)
                dve.wait_ge(rstd_done.sem, rstd_done.at(1))
                for t in range(TT):
                    dve.tensor_scalar(c.xn[:, t, :], c.x[:, t, :], mv[:, t, 0:1], rstd[:, t:t + 1],
                                      ALU.subtract, ALU.mult).then_inc(xn_done.sem, 1)
                if want_t:
                    for k in (1, 3):
                        dve.wait_ge(tr_done.sem, tr_done.at(k + 1))
                        dve.tensor_copy(c.xnT[:, k % 2, (k // 2) * BANK:(k // 2 + 1) * BANK],
                                        c.ps[:, k, :]).then_inc(ev_done.sem, 1)

            @block.scalar
            def _(act):
                act.wait_ge(var_done.sem, var_done.at(1))
                act.activation(std[:, :], std[:, :], ACT.Sqrt).then_inc(std_done.sem, 1)
                if want_t:
                    for k in (0, 2):
                        act.wait_ge(tr_done.sem, tr_done.at(k + 1))
                        act.activation(c.xnT[:, k % 2, (k // 2) * BANK:(k // 2 + 1) * BANK],
                                       c.ps[:, k, :], ACT.Copy).then_inc(ev_done.sem, 1)

            if want_t:
                @block.tensor
                def _(pe):
                    for k in range(4):
                        pe.wait_ge(xn_done.sem, xn_done.at(4 * (k // 2) + 4))
                        for j in range(4):
                            t = 4 * (k // 2) + j
                            mm = pe.transpose(c.ps[:, k, j * P:(j + 1) * P],
                                              c.xn[:, t, (k % 2) * P:(k % 2 + 1) * P], c.ident[:, :])
                        mm.then_inc(tr_done.sem, 1)

            @block.sync
            def _(sp):
                sp.wait_ge(xn_done.sem, xn_done.at(TT))
                if want_t:
                    sp.wait_ge(ev_done.sem, ev_done.at(4))

        for s, n in ((stats_done, TT), (mv_done, TT), (var_done, 1), (std_done, 1), (rstd_done, 1),
                     (xn_done, TT), (tr_done, 4 if want_t else 0), (ev_done, 4 if want_t else 0)):
            s.done(n)



def lora_fold(c, st, names):
    nc, io = c.nc, c.io
    rank = io["L0_B"].shape[1]
    wT = st.enter_context(nc.sbuf_tensor("lora_wT", [P, 4, DT, DIM], F32))
    lb = st.enter_context(nc.sbuf_tensor("lora_b", [rank, 4, DIM], F32))
    la = st.enter_context(nc.sbuf_tensor("lora_aT", [rank, 4, DIM], F32))
    loaded, prod, fold = c.counter("lora_in"), c.counter("lora_prod"), c.counter("lora_fold")
    with nc.Block() as block:

        @block.sync
        def _(sp):
            sp.dma_start(lb[:, :, :], io["L0_B"].rearrange("w r d -> r w d")).then_inc(loaded.sem, 16)
            sp.dma_start(la[:, :, :], io["L0_AT"].rearrange("w r d -> r w d")).then_inc(loaded.sem, 16)
            for w in range(4):
                sp.dma_start(wT[:, w, :, :], io["L0_WT"][w].rearrange("(t p) o -> p t o", p=P))\
                    .then_inc(loaded.sem, 16)
            sp.wait_ge(fold.sem, 4)

        @block.tensor
        def _(pe):
            pe.wait_ge(loaded.sem, 96)
            for w in range(4):
                for t in range(DT):
                    mm = pe.matmul(c.ps[:, w, t * DIM:(t + 1) * DIM], lb[:, w, t * P:(t + 1) * P],
                                   la[:, w, :], start=True, stop=True)
                mm.then_inc(prod.sem, 1)

        @block.vector
        def _(dve):
            for w in range(4):
                dve.wait_ge(prod.sem, w + 1)
                dve.scalar_tensor_tensor(wT[:, w, :, :], c.ps[:, w, :].rearrange("p (t o) -> p t o", t=DT),
                                         0.5, wT[:, w, :, :], ALU.mult, ALU.add).then_inc(fold.sem, 1)
    return wT


def store_stack(sp, w, dst, parts, stored):
    for k, part in enumerate(((0, 0, 0, 1, 1, 2), (0, 1, 2, 0, 1, 0))[w]):
        sp.dma_start(dst[:, k], parts[:, part, :]).then_inc(stored.sem, 16)



def qkv_stage(c, st, name, wq, wk, wv, bias_io, scr_q, scr_k):
    nc, io = c.nc, c.io
    v = st.enter_context(nc.sbuf_tensor(f"{name}_v", [P, TT, DIM], F32))
    with ExitStack() as tmp:
        parts = tmp.enter_context(nc.sbuf_tensor(f"{name}_parts", [P, 2, DT, 3, TOK], BF16))
        rest = tmp.enter_context(nc.sbuf_tensor(f"{name}_rest", [P, 2, BANK], F32))
        bcol = tmp.enter_context(nc.sbuf_tensor(f"{name}_bcol", [P, 2, DT], F32))
        bv = tmp.enter_context(nc.sbuf_tensor(f"{name}_bv", [P, DIM], F32))
        bias_in, proj = c.counter("qkv_bias"), c.counter("qkv_proj")
        hi_done, rest_done, mid_done, lo_done = (c.counter("qkv_hi"), c.counter("qkv_rest"),
                                                 c.counter("qkv_mid"), c.counter("qkv_lo"))
        vproj, v_done, stored = c.counter("qkv_vproj"), c.counter("qkv_v"), c.counter("qkv_stored")
        groups = [(w, ot, half) for w in range(2) for ot in range(DT) for half in range(HALF)]
        NG = len(groups)

        with nc.Block() as block:

            @block.sync
            def _(sp):
                sp.dma_start(bcol[:, :, :], io[bias_io + "_col"]).then_inc(bias_in.sem, 16)
                sp.dma_start(bv[:, :], io[bias_io][2:3, :].broadcast_to([P, DIM])).then_inc(bias_in.sem, 16)
                for k in range(2 * DT):
                    w, ot = divmod(k, DT)
                    sp.wait_ge(lo_done.sem, lo_done.at(HALF * (k + 1)))
                    store_stack(sp, w, (scr_q, scr_k)[w][8 * ot:8 * ot + 8], parts[:, w, ot, :, :],
                                stored)
                sp.wait_ge(stored.sem, stored.at(16 * TERMS * 2 * DT))
                sp.wait_ge(v_done.sem, v_done.at(TT // 2))

            @block.gpsimd
            def _(pool):
                for g, (w, ot, half) in enumerate(groups):
                    cols = slice(half * BANK, (half + 1) * BANK)
                    pool.wait_ge(mid_done.sem, mid_done.at(g + 1))
                    pool.tensor_tensor(parts[:, w, ot, 2, cols], rest[:, g % 2, :], parts[:, w, ot, 1, cols],
                                       ALU.subtract).then_inc(lo_done.sem, 1)

            @block.tensor
            def _(pe):
                for g, (w, ot, half) in enumerate(groups):
                    if g >= 4:
                        pe.wait_ge(rest_done.sem, rest_done.at(g - 3))
                    for dt in range(DT):
                        mm = pe.matmul(c.ps[:, g % 4, :], (wq, wk)[w][:, dt, ot * P:(ot + 1) * P],
                                       c.xnT[:, dt, half * BANK:(half + 1) * BANK],
                                       start=(dt == 0), stop=(dt == DT - 1))
                    mm.then_inc(proj.sem, 1)
                for t in range(TT):
                    for dt in range(DT):
                        mm = pe.matmul(c.ps[:, 4 + t // 2, (t % 2) * DIM:(t % 2 + 1) * DIM],
                                       c.xnT[:, dt, t * P:(t + 1) * P], wv[:, dt, :],
                                       start=(dt == 0), stop=(dt == DT - 1))
                    if t % 2:
                        mm.then_inc(vproj.sem, 1)

            @block.scalar
            def _(act):
                act.wait_ge(bias_in.sem, bias_in.at(32))
                for g, (w, ot, half) in enumerate(groups + [(None, None, None)]):
                    if g < NG:
                        act.wait_ge(proj.sem, proj.at(g + 1))
                        act.activation(parts[:, w, ot, 0, half * BANK:(half + 1) * BANK], c.ps[:, g % 4, :],
                                       ACT.Identity, bias=bcol[:, w, ot:ot + 1]).then_inc(hi_done.sem, 1)
                    if g >= 1:
                        w, ot, half = groups[g - 1]
                        act.wait_ge(rest_done.sem, rest_done.at(g))
                        act.activation(parts[:, w, ot, 1, half * BANK:(half + 1) * BANK],
                                       rest[:, (g - 1) % 2, :], ACT.Copy).then_inc(mid_done.sem, 1)

            @block.vector
            def _(dve):
                dve.wait_ge(bias_in.sem, bias_in.at(32))
                for g, (w, ot, half) in enumerate(groups):
                    dve.wait_ge(hi_done.sem, hi_done.at(g + 1))
                    if g >= 2:
                        dve.wait_ge(lo_done.sem, lo_done.at(g - 1))
                    dve.scalar_tensor_tensor(rest[:, g % 2, :], c.ps[:, g % 4, :], bcol[:, w, ot:ot + 1],
                                             parts[:, w, ot, 0, half * BANK:(half + 1) * BANK],
                                             ALU.add, ALU.subtract).then_inc(rest_done.sem, 1)
                for k in range(TT // 2):
                    dve.wait_ge(vproj.sem, vproj.at(k + 1))
                    dve.tensor_tensor(v[:, 2 * k:2 * k + 2, :],
                                      c.ps[:, 4 + k, :].rearrange("p (t o) -> p t o", t=2),
                                      bv[:, :].unsqueeze(1).broadcast_to([P, 2, DIM]), ALU.add)\
                        .then_inc(v_done.sem, 1)

        bias_in.done(32)
        for s in (proj, hi_done, rest_done, mid_done, lo_done):
            s.done(NG)
        vproj.done(TT // 2)
        v_done.done(TT // 2)
        stored.done(16 * TERMS * 2 * DT)
    return v



def attention_stage(c, name, hd, shared_k, scale, v, scr_q, scr_k, av_all, alibi=False):
    nc, io = c.nc, c.io
    rows = TERMS * hd
    s_rows = P - 2
    per_seq = 8 if shared_k else 4
    n_seq = ITEMS // per_seq
    NK = 1 if shared_k else 4
    N_ITER = BATCH // n_seq
    LAG = 2
    MAXR = 4 * QT * 2
    ST0, AV0, OUT0 = 2 * ITEMS, ITEMS, 1

    with ExitStack() as st:
        def sb(n, shape, dt=F32):
            return st.enter_context(nc.sbuf_tensor(f"{name}_{n}", shape, dt))

        qs = c.qs
        ks = c.ks[:, :, 0:NK, :]
        vs = sb("vs", [P, ITEMS, QT, NK, SCOLS])
        pt = sb("pt", [P, 2, QT, 4 * SEQ])
        one8 = sb("one8", [P, 4 * QT])
        nm = sb("nm", [P, ITEMS, 4 * QT])
        nms = sb("nms", [P, ITEMS, 2, 4 * QT], BF16)
        mT = sb("mT", [MAXR, ITEMS, P], BF16)
        if alibi:
            slope = sb("slope", [16, 2])
            wide = sb("wide", [16, 3, SEQ])
            pos = sb("pos", [16, SEQ])
            sl = sb("sl", [16, 9, SEQ], BF16)
            maskb = sb("maskb", [P, 3, BANK], BF16)
            maskf = sb("maskf", [P, 3, BANK])

        filled, fill_in = c.counter("at_filled"), c.counter("at_fill_in")
        al, al_in = c.counter("at_alibi"), c.counter("at_alibi_in")
        in_q = [c.counter(f"at_in{i}") for i in range(ITEMS)]
        m_in = [c.counter(f"at_m{i}") for i in range(ITEMS)]
        v_in = c.counter("at_v_in")
        s_done, mx_done = c.counter("at_s"), c.counter("at_mx")
        nh_done, nl_done = c.counter("at_nh"), c.counter("at_nl")
        tr_done, mt_done = c.counter("at_tr"), c.counter("at_mt")
        st_done, exp_done = c.counter("at_st"), c.counter("at_exp")
        av_done, out_done = c.counter("at_av"), c.counter("at_out")
        AL_STEPS = 10
        N_FILL = 2 * ITEMS // per_seq

        def seq_of(it, i):
            return it * n_seq + i // per_seq

        with nc.Block() as block:

            @block.sync
            def _(sp):
                if alibi:
                    sp.dma_start(slope[:, 0:1], io["slopes"]).then_inc(al_in.sem, 16)
                    sp.dma_start(pos[:, :], io["pos"].broadcast_to([16, SEQ])).then_inc(al_in.sem, 16)
                    sp.dma_start(maskf[:, :, :], io["masks"]).then_inc(al_in.sem, 16)
                    sp.wait_ge(al.sem, al.at(AL_STEPS))
                    sp.dma_start(c.scr_al.rearrange("k h q -> h k q"), sl[:, :, :]).then_inc(al_in.sem, 16)
                    sp.wait_ge(al_in.sem, al_in.at(64))
                    for i in range(0, ITEMS, per_seq):
                        slots = slice(i, i + per_seq)
                        for dst, first in ((qs, 0), (ks, 3)):
                            sp.dma_start(dst[rows:rows + 6, slots],
                                         c.scr_al[first:first + 6].rearrange("k (s h) q -> k s h q", s=per_seq))\
                                .then_inc(fill_in.sem, 16)
                with sp.Fori(0, N_ITER) as it:
                    for i in range(ITEMS):
                        n = it * ITEMS + i
                        toks = bass.ds(seq_of(it, i) * SEQ, SEQ)
                        hg = i % per_seq
                        sp.wait_ge(st_done.sem, st_done.at(2 * n + 2))
                        for dst, scr, heads in ((qs, scr_q, 4), (ks, scr_k, NK)):
                            sp.dma_start(dst[0:rows, i, :, :], scr[heads * hg:heads * (hg + 1), :, :, toks]
                                         .rearrange("h k d q -> (k d) h q")).then_inc(in_q[i].sem, 16)

            @block.gpsimd
            def _(pool):
                pool.memset(vs[:, :, :, :, :], 1.0).then_inc(filled.sem, 1)
                pool.memset(one8[:, :], 1.0).then_inc(filled.sem, 1)
                pool.wait_ge(filled.sem, filled.at(2))
                with pool.Fori(0, N_ITER) as it:
                    for i in range(ITEMS):
                        n = it * ITEMS + i
                        pool.wait_ge(av_done.sem, av_done.at(n + 1))
                        pool.wait_ge(filled.sem, filled.at(1))
                        hg = i % per_seq
                        pool.tensor_copy(vs[:, i, :, :, 0:hd],
                                         v[:, bass.ds(seq_of(it, i) * QT, QT), hg * NK * hd:(hg + 1) * NK * hd]
                                         .rearrange("p t (h d) -> p t h d", h=NK)).then_inc(v_in.sem, 1)
                        pool.wait_ge(mx_done.sem, mx_done.at(4 * n + 4))
                        pool.tensor_tensor(nms[:, i, 0, :], nm[:, i, :], one8[:, :], ALU.mult)\
                            .then_inc(nh_done.sem, 1)
                        pool.wait_ge(nh_done.sem, nh_done.at(n + 1))
                        pool.tensor_tensor(nms[:, i, 1, :], nm[:, i, :], nms[:, i, 0, :],
                                           ALU.subtract).then_inc(nl_done.sem, 1)

            @block.vector
            def _(dve):
                dve.sem_inc(st_done.sem, ST0)
                dve.sem_inc(av_done.sem, AV0)
                dve.sem_inc(out_done.sem, OUT0)
                if alibi:
                    dve.wait_ge(al_in.sem, al_in.at(48))
                    dve.tensor_copy(maskb[:, :, :], maskf[:, :, :]).then_inc(al.sem, 1)
                    dve.tensor_copy(sl[:, 3:6, :], pos[:, :].unsqueeze(1).broadcast_to([16, 3, SEQ]))\
                        .then_inc(al.sem, 1)
                    dve.tensor_scalar(slope[:, 1:2], slope[:, 0:1], 1.0 / scale, None, ALU.mult)\
                        .then_inc(al.sem, 1)
                    dve.wait_ge(al.sem, al.at(3))
                    dve.tensor_copy(wide[:, 0, :], slope[:, 1:2].broadcast_to([16, SEQ])).then_inc(al.sem, 1)
                    for k in range(3):
                        dve.wait_ge(al.sem, al.at(4 + 2 * k))
                        dve.tensor_copy(sl[:, k, :], wide[:, k, :]).then_inc(al.sem, 1)
                        if k < 2:
                            dve.wait_ge(al.sem, al.at(5 + 2 * k))
                            dve.tensor_tensor(wide[:, k + 1, :], wide[:, k, :], sl[:, k, :], ALU.subtract)\
                                .then_inc(al.sem, 1)
                    dve.wait_ge(al.sem, al.at(9))
                    dve.tensor_scalar(sl[:, 6:9, :], sl[:, 0:3, :], -1.0, None, ALU.mult).then_inc(al.sem, 1)

                def maxima(it, i):
                    for hh in range(4):
                        n = it * ITEMS + i
                        dve.wait_ge(s_done.sem, s_done.at(4 * n + hh + 1))
                        dve.tensor_reduce(nm[:, i, QT * hh:QT * hh + QT],
                                          c.ps[:, hh % 2, :].rearrange("p (t k) -> p t k", t=QT),
                                          AX.X, ALU.max, negate=True).then_inc(mx_done.sem, 1)

                def outputs(it, i):
                    n = it * ITEMS + i
                    dve.wait_ge(av_done.sem, av_done.at(AV0 + n + 1))
                    dve.tensor_scalar(av_all[:, i % per_seq, bass.ds(seq_of(it, i) * SEQ, SEQ)],
                                      c.ps[:, 6, 0:SEQ], 1.0, None, ALU.mult).then_inc(out_done.sem, 1)

                with dve.Fori(0, N_ITER) as it:
                    for i in range(LAG):
                        maxima(it, i)
                    for i in range(ITEMS + 1):
                        if i + LAG < ITEMS:
                            maxima(it, i + LAG)
                        if i >= 1:
                            outputs(it, i - 1)

            @block.scalar
            def _(act):
                def max_rows(it, i):
                    n = it * ITEMS + i
                    act.wait_ge(tr_done.sem, tr_done.at(n + 1))
                    act.activation(mT[:, i, :], c.ps[0:MAXR, 7, 0:P], ACT.Copy).then_inc(mt_done.sem, 1)
                    act.wait_ge(mt_done.sem, mt_done.at(n + 1))
                    for part in range(2):
                        act.dma_start(qs[s_rows + part:s_rows + part + 1, i, :, :],
                                      mT[4 * QT * part:4 * QT * (part + 1), i, :])\
                            .then_inc(m_in[i].sem, 16)

                with act.Fori(0, N_ITER) as it:
                    max_rows(it, 0)
                    for i in range(ITEMS):
                        n = it * ITEMS + i
                        if i + 1 < ITEMS:
                            max_rows(it, i + 1)
                        act.wait_ge(av_done.sem, av_done.at(AV0 + n - 1))
                        for kt in range(QT):
                            act.wait_ge(st_done.sem, st_done.at(ST0 + 2 * n + kt + 1))
                            act.activation(pt[:, i % 2, kt, :],
                                           c.ps[:, 2 + 2 * kt:4 + 2 * kt, :].rearrange("p b n -> p (b n)"),
                                           ACT.Exp, scale=scale).then_inc(exp_done.sem, 1)

            @block.tensor
            def _(pe):
                def scores(it, i):
                    n = it * ITEMS + i
                    pe.wait_ge(in_q[i].sem, in_q[i].at((it + 1) * 32))
                    for hh in range(4):
                        kh = 0 if shared_k else hh
                        if i > 0 or hh > 1:
                            pe.wait_ge(mx_done.sem, mx_done.at(4 * n + hh - 1))
                        if alibi:
                            pe.matmul(c.ps[:, hh % 2, :], c.identb[:, :], maskb[:, 0, :],
                                      start=True, stop=False)
                        for qt in range(QT):
                            mm = pe.matmul(c.ps[:, hh % 2, qt * SEQ:(qt + 1) * SEQ],
                                           qs[0:s_rows, i, hh, qt * P:(qt + 1) * P], ks[0:s_rows, i, kh, :],
                                           start=not alibi, stop=not alibi or qt == QT - 1)
                        mm.then_inc(s_done.sem, 1)

                def max_transpose(it, i):
                    n = it * ITEMS + i
                    if i > 0:
                        pe.wait_ge(mt_done.sem, mt_done.at(n))
                    pe.wait_ge(nl_done.sem, nl_done.at(n + 1))
                    pe.matmul(c.ps[0:MAXR, 7, 0:P], nms[:, i, :, :].rearrange("p a b -> p (a b)"),
                              c.identb[:, :], start=True, stop=True).then_inc(tr_done.sem, 1)

                def scores_t(it, i):
                    n = it * ITEMS + i
                    pe.wait_ge(m_in[i].sem, m_in[i].at((it + 1) * 32))
                    for kt in range(QT):
                        if i > 0:
                            pe.wait_ge(exp_done.sem, exp_done.at(2 * n - 1 + kt))
                        for hh in range(0, 4, 2):
                            bank = 2 + 2 * kt + hh // 2
                            if alibi:
                                pe.matmul(c.ps[:, bank, :], c.identb[:, :], maskb[:, 1 + kt, :],
                                          start=True, stop=False)
                            if shared_k:
                                mm = pe.matmul(c.ps[:, bank, :], ks[:, i, 0, kt * P:(kt + 1) * P],
                                               qs[:, i, hh:hh + 2, :].rearrange("p h q -> p (h q)"),
                                               start=True, stop=True)
                            else:
                                for h in range(hh, hh + 2):
                                    mm = pe.matmul(c.ps[:, bank, (h % 2) * SEQ:(h % 2 + 1) * SEQ],
                                                   ks[:, i, h, kt * P:(kt + 1) * P], qs[:, i, h, :],
                                                   start=not alibi, stop=not alibi or h % 2 == 1)
                        mm.then_inc(st_done.sem, 1)

                def product(it, i):
                    n = it * ITEMS + i
                    pe.wait_ge(v_in.sem, v_in.at(n + 1))
                    pe.wait_ge(out_done.sem, out_done.at(OUT0 + n))
                    for kt in range(QT):
                        pe.wait_ge(exp_done.sem, exp_done.at(2 * n + kt + 1))
                        for hh in range(4):
                            mm = pe.matmul(c.ps[SCOLS * hh:SCOLS * (hh + 1), 6, 0:SEQ],
                                           vs[:, i, kt, 0 if shared_k else hh, :],
                                           pt[:, i % 2, kt, hh * SEQ:(hh + 1) * SEQ],
                                           start=(kt == 0), stop=(kt == QT - 1))
                    mm.then_inc(av_done.sem, 1)

                if alibi:
                    pe.wait_ge(fill_in.sem, fill_in.at(16 * N_FILL))
                    pe.wait_ge(al.sem, al.at(1))
                with pe.Fori(0, N_ITER) as it:
                    for i in range(LAG):
                        scores(it, i)
                    max_transpose(it, 0)
                    for i in range(ITEMS + 1):
                        if i + LAG < ITEMS:
                            scores(it, i + LAG)
                        if i >= 1:
                            product(it, i - 1)
                        if i + 1 < ITEMS:
                            max_transpose(it, i + 1)
                        if i < ITEMS:
                            scores_t(it, i)

        n_items = N_ITER * ITEMS
        filled.done(2)
        if alibi:
            fill_in.done(16 * N_FILL)
            al.done(AL_STEPS)
            al_in.done(64)
        for s in in_q:
            s.done(32 * N_ITER)
        for s in m_in:
            s.done(32 * N_ITER)
        for s in (v_in, nh_done, nl_done, tr_done, mt_done):
            s.done(n_items)
        s_done.done(4 * n_items)
        mx_done.done(4 * n_items)
        st_done.done(ST0 + 2 * n_items)
        exp_done.done(2 * n_items)
        av_done.done(AV0 + n_items)
        out_done.done(OUT0 + n_items)


def normalise_stage(c, st, name, groups, hd, av_all, wo, bias_io):
    nc, io = c.nc, c.io
    heads = 4 * groups
    nb = groups * P // BANK
    with ExitStack() as tmp:
        def sb(n, shape, dt=F32):
            return tmp.enter_context(nc.sbuf_tensor(f"{name}_{n}", shape, dt))

        rec = sb("rec", [P, TT, heads])
        on = sb("on", [P, TT, heads, hd])
        onT = sb("onT", [P, DT, TOK])
        bo = sb("bo", [P, DIM])
        bias_in, tr_done, rec_done, on_done = (c.counter("no_bias"), c.counter("no_tr"), c.counter("no_rec"),
                                               c.counter("no_on"))
        t2_done, onT_done, y_done, x_done = (c.counter("no_t2"), c.counter("no_onT"), c.counter("no_y"),
                                             c.counter("no_x"))
        xb_done = c.counter("no_xb")

        def out_view(t):
            b0 = nb * (t % 2)
            return c.ps[:, b0:b0 + nb, :].rearrange("p b (h s) -> p (b h) s", s=SCOLS)

        with nc.Block() as block:

            @block.tensor
            def _(pe):
                def second(t):
                    pe.wait_ge(on_done.sem, on_done.at(t + 1))
                    if t >= 2:
                        pe.wait_ge(onT_done.sem, onT_done.at(t - 1))
                    for dt in range(DT):
                        mm = pe.transpose(c.ps[:, 4 + t % 2, dt * P:(dt + 1) * P],
                                          on[:, t, :, :].rearrange("p h d -> p (h d)")[:, dt * P:(dt + 1) * P],
                                          c.ident[:, :])
                    mm.then_inc(t2_done.sem, 1)

                def project(t):
                    pe.wait_ge(onT_done.sem, onT_done.at(t + 1))
                    if t >= 2:
                        pe.wait_ge(x_done.sem, x_done.at(t - 1))
                    for dt in range(DT):
                        mm = pe.matmul(c.ps[:, 6 + t % 2, 0:DIM], onT[:, dt, t * P:(t + 1) * P],
                                       wo[:, dt, :], start=(dt == 0), stop=(dt == DT - 1))
                    mm.then_inc(y_done.sem, 1)

                for t in range(TT + 2):
                    if t < TT:
                        if t >= 2:
                            pe.wait_ge(on_done.sem, on_done.at(t - 1))
                        for g in range(groups):
                            mm = pe.transpose(c.ps[:, nb * (t % 2) + g // 4, (g % 4) * P:(g % 4 + 1) * P],
                                              av_all[:, g, t * P:(t + 1) * P], c.ident[:, :])
                        mm.then_inc(tr_done.sem, 1)
                    if wo is not None and 1 <= t <= TT:
                        second(t - 1)
                    if wo is not None and t >= 2:
                        project(t - 2)

            @block.vector
            def _(dve):
                def residual(t):
                    dve.wait_ge(y_done.sem, y_done.at(t + 1))
                    dve.tensor_tensor(c.x[:, t, :], c.ps[:, 6 + t % 2, 0:DIM], c.x[:, t, :], ALU.add)\
                        .then_inc(x_done.sem, 1)

                if wo is not None:
                    dve.wait_ge(xb_done.sem, xb_done.at(1))
                for t in range(TT):
                    dve.wait_ge(tr_done.sem, tr_done.at(t + 1))
                    dve.reciprocal(rec[:, t, :], out_view(t)[:, :, hd:hd + 1].squeeze(2)).then_inc(rec_done.sem, 1)
                    dve.wait_ge(rec_done.sem, rec_done.at(t + 1))
                    dve.tensor_tensor(on[:, t, :, :], out_view(t)[:, :, 0:hd],
                                      rec[:, t, :].unsqueeze(2).broadcast_to([P, heads, hd]), ALU.mult)\
                        .then_inc(on_done.sem, 1)
                    if wo is None:
                        dve.wait_ge(on_done.sem, on_done.at(t + 1))
                        dve.tensor_tensor(c.x[:, t, :], on[:, t, :, :].rearrange("p h d -> p (h d)"),
                                          c.x[:, t, :], ALU.add).then_inc(x_done.sem, 1)
                    elif t >= 2:
                        residual(t - 2)
                if wo is not None:
                    residual(TT - 2)
                    residual(TT - 1)

            if wo is not None:
                @block.sync
                def _(sp):
                    sp.dma_start(bo[:, :], io[bias_io][3:4, :].broadcast_to([P, DIM])).then_inc(bias_in.sem, 16)

                @block.gpsimd
                def _(pool):
                    pool.wait_ge(bias_in.sem, bias_in.at(16))
                    pool.tensor_tensor(c.x[:, :, :], c.x[:, :, :],
                                       bo[:, :].unsqueeze(1).broadcast_to([P, TT, DIM]), ALU.add)\
                        .then_inc(xb_done.sem, 1)

                @block.scalar
                def _(act):
                    for t in range(TT):
                        act.wait_ge(t2_done.sem, t2_done.at(t + 1))
                        act.activation(onT[:, :, t * P:(t + 1) * P],
                                       c.ps[:, 4 + t % 2, 0:DIM].rearrange("p (t n) -> p t n", t=DT),
                                       ACT.Copy).then_inc(onT_done.sem, 1)

        for s in (tr_done, rec_done, on_done, x_done):
            s.done(TT)
        if wo is not None:
            for s in (t2_done, onT_done, y_done):
                s.done(TT)
            bias_in.done(16)
            xb_done.done(1)


PAIRS = 8
HK, DCQ, R = 128, 192, 64


def context_stage(c, st):
    nc, io = c.nc, c.io
    kvr = st.enter_context(nc.sbuf_tensor("m_kvr", [P, TT, CTX], F32))
    kvT = st.enter_context(nc.sbuf_tensor("m_kvT", [P, TOK], F32))
    with ExitStack() as tmp:
        def sb(n, shape, dt=F32):
            return tmp.enter_context(nc.sbuf_tensor(f"mc_{n}", shape, dt))

        raw = sb("raw", [P, TT, CTX])
        rot = sb("rot", [P, TT, CTX])
        tab = sb("tab", [P, 2, QT, CTX])
        t1 = sb("t1", [P, TT, CTX])
        loaded, step, tr = c.counter("mc_in"), c.counter("mc_step"), c.counter("mc_tr")
        half = CTX // 2
        with nc.Block() as block:

            @block.sync
            def _(sp):
                src = io["ctx"].rearrange("(t p) d -> p t d", p=P)
                sp.dma_start(raw[:, :, :], src).then_inc(loaded.sem, 16)
                sp.dma_start(rot[:, :, 0:half], src[:, :, half:CTX]).then_inc(loaded.sem, 16)
                sp.dma_start(rot[:, :, half:CTX], src[:, :, 0:half]).then_inc(loaded.sem, 16)
                sp.dma_start(tab[:, :, :, :], io["rope_k"]).then_inc(loaded.sem, 16)

            @block.vector
            def _(dve):
                def by_seq(a):
                    return a.rearrange("p (b t) d -> p b (t d)", t=QT)

                def table(k):
                    return tab[:, k, :, :].rearrange("p t d -> p (t d)").unsqueeze(1)\
                        .broadcast_to([P, BATCH, QT * CTX])

                dve.memset(kvT[:, :], 0.0).then_inc(step.sem, 1)
                dve.wait_ge(loaded.sem, 64)
                dve.tensor_tensor(by_seq(t1[:, :, :]), by_seq(raw[:, :, :]), table(0), ALU.mult)\
                    .then_inc(step.sem, 1)
                dve.tensor_tensor(by_seq(rot[:, :, :]), by_seq(rot[:, :, :]), table(1), ALU.mult)\
                    .then_inc(step.sem, 1)
                dve.wait_ge(step.sem, 3)
                dve.tensor_tensor(kvr[:, :, :], t1[:, :, :], rot[:, :, :], ALU.add).then_inc(step.sem, 1)
                dve.wait_ge(tr.sem, 1)
                dve.tensor_copy(kvT[0:CTX, :], c.ps[0:CTX, 0:2, :].rearrange("p b n -> p (b n)"))\
                    .then_inc(step.sem, 1)
                dve.wait_ge(step.sem, 5)

            @block.tensor
            def _(pe):
                pe.wait_ge(step.sem, 4)
                for t in range(TT):
                    mm = pe.transpose(c.ps[0:CTX, t // 4, (t % 4) * P:(t % 4 + 1) * P], kvr[:, t, :],
                                      c.ident[:, :])
                mm.then_inc(tr.sem, 1)
    return kvr, kvT


def mla_stages(c):
    nc, io = c.nc, c.io
    layer_norm(c, "ln2")
    with ExitStack() as st:
        kvr, kvT = context_stage(c, st)

        def sb(n, shape, dt=F32):
            return st.enter_context(nc.sbuf_tensor(f"m_{n}", shape, dt))

        ctxn = sb("ctxn", [P, PAIRS, TOK])
        nw = sb("nw", [P, PAIRS, DIM])
        with ExitStack() as tmp:
            mla_pairs(c, tmp, kvr, kvT, ctxn, nw)

        y_done, x_done = c.counter("mo_y"), c.counter("mo_x")
        with nc.Block() as block:

            @block.tensor
            def _(pe):
                for t in range(TT):
                    for p in range(PAIRS):
                        mm = pe.matmul(c.ps[:, t, 0:DIM], ctxn[:, p, t * P:(t + 1) * P], nw[:, p, :],
                                       start=(p == 0), stop=(p == PAIRS - 1))
                    mm.then_inc(y_done.sem, 1)

            @block.vector
            def _(dve):
                for t in range(TT):
                    dve.wait_ge(y_done.sem, t + 1)
                    dve.tensor_tensor(c.x[:, t, :], c.ps[:, t, 0:DIM], c.x[:, t, :], ALU.add)\
                        .then_inc(x_done.sem, 1)
                dve.wait_ge(x_done.sem, TT)


def mla_pairs(c, st, kvr, kvT, ctxn, nw):
    nc, io = c.nc, c.io

    def sb(n, shape, dt=F32):
        return st.enter_context(nc.sbuf_tensor(f"mp_{n}", shape, dt))

    wq2, wkq = sb("wq2", [P, 2, DIM]), sb("wkq", [P, 2, DCQ])
    wr = sb("wr", [P, 2, 3, 2 * R])
    wkr = sb("wkr", [P, 2 * R])
    wkv, wo = sb("wkv", [P, 2, CTX]), sb("wo", [P, 2, DIM])
    tab = sb("tab", [P, 2, 3, SEQ])
    mp = sb("mp", [P, DT, 2 * DCQ])
    qcs = sb("qcs", [P, HALF, 3, 2, BANK])
    qa = sb("qa", [P, 2, TOK])
    ks = sb("ks", [P, 2, TOK])
    zero = sb("zero", [1, TOK])
    nm = sb("nm", [P, 2, BATCH, QT])
    MR = 2 * BATCH * QT
    mT = sb("mT", [MR, P])
    pt = sb("pt", [P, 2, 2, QT, SEQ])
    ones = sb("ones", [P, R])
    cr, sm = sb("cr", [P, TOK]), sb("sm", [P, TOK])
    lns = sb("lns", [P, TOK])

    tab_in, prep = c.counter("mp_tab"), c.counter("mp_prep")
    w_a, w_k, w_r, w_n = (c.counter("mp_wa"), c.counter("mp_wk"), c.counter("mp_wr"), c.counter("mp_wn"))
    kr, k_ev = c.counter("mp_kr"), c.counter("mp_k_ev")
    a_done, mp_done = c.counter("mp_a"), c.counter("mp_mp")
    qb, rope, qr = c.counter("mp_qb"), c.counter("mp_rope"), c.counter("mp_qr")
    q_ev, q_ev2, z_in, m_in = (c.counter("mp_q_ev"), c.counter("mp_q_ev2"), c.counter("mp_z_in"),
                               c.counter("mp_m_in"))
    s_done, mx = c.counter("mp_s"), c.counter("mp_mx")
    tr, mt = c.counter("mp_tr"), c.counter("mp_mt")
    n_done, nw_done = c.counter("mp_n"), c.counter("mp_nw")
    stt, ex, av, out = c.counter("mp_st"), c.counter("mp_ex"), c.counter("mp_av"), c.counter("mp_out")
    ln_done, inv_done, cn = c.counter("mp_ln"), c.counter("mp_inv"), c.counter("mp_cn")
    OUT0, CN0, Z0 = 1, 1, 1
    TILE_ORDER = (1, 0, 2)
    QB_BANKS = (2, 3, 0, 1)

    def rows(h):
        return slice(R * h, R * h + R)

    def m_row(h):
        return slice(R * (1 - h), R * (1 - h) + 1)

    def half_cols(half):
        return slice(half * BANK, (half + 1) * BANK)

    with nc.Block() as block:

        @block.sync
        def _(sp):
            sp.dma_start(tab[:, :, :, :], io["rope_q"]).then_inc(tab_in.sem, 16)

            def load_k(p):
                sp.dma_start(wkr[:, :], io["m_wkr"][p]).then_inc(w_k.sem, 16)

            def load_a(p):
                sp.dma_start(wq2[:, :, :], io["m_wq"][p]).then_inc(w_a.sem, 16)
                sp.dma_start(wkq[:, :, :], io["m_wkq"][p]).then_inc(w_a.sem, 16)

            def load_r(p):
                sp.dma_start(wr[:, :, :, :], io["m_wr"][p]).then_inc(w_r.sem, 16)

            def load_n(p):
                sp.dma_start(wkv[:, :, :], io["m_wkv"][p]).then_inc(w_n.sem, 16)
                sp.dma_start(wo[:, :, :], io["m_wo"][p]).then_inc(w_n.sem, 16)

            load_k(0)
            load_a(0)
            load_r(0)
            load_n(0)
            with sp.Fori(1, PAIRS) as it:
                sp.wait_ge(kr.sem, it * 2)
                load_k(bass.ds(it, 1))
                sp.wait_ge(a_done.sem, it * 2)
                load_a(bass.ds(it, 1))
                sp.wait_ge(qr.sem, it * 2)
                load_r(bass.ds(it, 1))
                sp.wait_ge(n_done.sem, it * 1)
                load_n(bass.ds(it, 1))
                sp.wait_ge(stt.sem, it * 4)
                for h in range(2):
                    sp.dma_start(qa[m_row(h), h, :], zero[:, :]).then_inc(z_in.sem, 16)

        @block.gpsimd
        def _(pool):
            for tile, value in ((qa[:, :, :], 0.0), (ks[:, :, :], 0.0), (ones[:, :], 1.0), (zero[:, :], 0.0)):
                pool.memset(tile, value).then_inc(prep.sem, 1)
            pool.wait_ge(prep.sem, 4)
            for h in range(2):
                pool.memset(ks[m_row(h), h, :], 1.0).then_inc(prep.sem, 1)
            pool.wait_ge(prep.sem, 6)

        @block.vector
        def _(dve):
            dve.sem_inc(out.sem, OUT0)
            dve.sem_inc(cn.sem, CN0)
            dve.sem_inc(z_in.sem, Z0)
            dve.wait_ge(tab_in.sem, 16)
            dve.wait_ge(prep.sem, 6)
            with dve.Fori(0, PAIRS) as it:
                dve.wait_ge(a_done.sem, it * 2 + 2)
                dve.tensor_copy(mp[:, 1, :], c.ps[:, 1, 0:2 * DCQ]).then_inc(mp_done.sem, 1)
                for k in range(6):
                    half, tile = k // 3, TILE_ORDER[k % 3]
                    dve.wait_ge(qb.sem, it * 6 + (k + 1))
                    for cs in range(2):
                        dve.tensor_tensor(
                            qcs[:, half, tile, cs, :].rearrange("p (b q) -> p b q", q=SEQ),
                            c.ps[:, QB_BANKS[k % 4], :].rearrange("p (b q) -> p b q", q=SEQ),
                            tab[:, cs, tile, :].unsqueeze(1).broadcast_to([P, 2, SEQ]), ALU.mult)\
                            .then_inc(rope.sem, 1)
                for half in range(HALF):
                    dve.wait_ge(qr.sem, it * 2 + (half + 1))
                    dve.tensor_copy(qa[rows(1), 1, half_cols(half)], c.ps[rows(1), 4 + half, :])\
                        .then_inc(q_ev2.sem, 1)
                for k in range(8):
                    dve.wait_ge(s_done.sem, it * 8 + (k + 1))
                    dve.tensor_reduce(nm[:, k % 2, k // 2, :],
                                      c.ps[:, k % 2, :].rearrange("p (t k) -> p t k", t=QT),
                                      AX.X, ALU.max, negate=True).then_inc(mx.sem, 1)
                dve.wait_ge(n_done.sem, it + 1)
                dve.tensor_scalar(nw[:, bass.ds(it, 1), :].squeeze(1), c.ps[:, 5, 0:DIM], 1.0, None, ALU.mult)\
                    .then_inc(nw_done.sem, 1)
                dve.wait_ge(cn.sem, it + CN0)
                for b in range(BATCH):
                    dve.wait_ge(av.sem, it * 4 + (b + 1))
                    dve.tensor_copy(cr[:, b * SEQ:(b + 1) * SEQ], c.ps[:, 6, 0:SEQ]).then_inc(out.sem, 1)
                    dve.tensor_copy(sm[:, b * SEQ:(b + 1) * SEQ], c.ps[:, 6, SEQ:2 * SEQ]).then_inc(out.sem, 1)
                dve.wait_ge(out.sem, it * 8 + (OUT0 + 8))
                dve.wait_ge(inv_done.sem, it + 1)
                dve.tensor_tensor(ctxn[:, bass.ds(it, 1), :].squeeze(1), cr[:, :], sm[:, :], ALU.mult)\
                    .then_inc(cn.sem, 1)

        @block.scalar
        def _(act):
            act.wait_ge(prep.sem, 6)
            with act.Fori(0, PAIRS) as it:
                for half in range(HALF):
                    act.wait_ge(kr.sem, it * 2 + (half + 1))
                    for h in range(2):
                        act.activation(ks[rows(h), h, half_cols(half)], c.ps[rows(h), 6 + half, :], ACT.Copy)\
                            .then_inc(k_ev.sem, 1)
                act.wait_ge(a_done.sem, it * 2 + 1)
                act.activation(mp[:, 0, :], c.ps[:, 0, 0:2 * DCQ], ACT.Copy).then_inc(mp_done.sem, 1)
                for half in range(HALF):
                    act.wait_ge(qr.sem, it * 2 + (half + 1))
                    act.activation(qa[rows(0), 0, half_cols(half)], c.ps[rows(0), 4 + half, :], ACT.Copy)\
                        .then_inc(q_ev.sem, 1)
                act.wait_ge(tr.sem, it + 1)
                act.activation(mT[:, :], c.ps[0:MR, 7, 0:P], ACT.Copy).then_inc(mt.sem, 1)
                act.wait_ge(mt.sem, it + 1)
                for h in range(2):
                    act.dma_start(qa[m_row(h), h, :], mT[h * MR // 2:(h + 1) * MR // 2, :]).then_inc(m_in.sem, 16)
                for b in range(BATCH):
                    act.wait_ge(stt.sem, it * 4 + (b + 1))
                    if b >= 2:
                        act.wait_ge(av.sem, it * 4 + (b - 1))
                    act.activation(pt[:, b % 2, :, :, :].rearrange("p h t q -> p (h t q)"),
                                   c.ps[:, 2 + 2 * (b % 2):4 + 2 * (b % 2), :].rearrange("p b n -> p (b n)"),
                                   ACT.Exp).then_inc(ex.sem, 1)
                act.wait_ge(out.sem, it * 8 + (OUT0 + 8))
                act.activation(lns[:, :], sm[:, :], ACT.Ln).then_inc(ln_done.sem, 1)
                act.wait_ge(ln_done.sem, it + 1)
                act.activation(sm[:, :], lns[:, :], ACT.Exp, scale=-1.0).then_inc(inv_done.sem, 1)

        @block.tensor
        def _(pe):
            pe.wait_ge(prep.sem, 6)
            with pe.Fori(0, PAIRS) as it:
                pe.wait_ge(w_k.sem, it * 16 + 16)
                pe.wait_ge(out.sem, it * 8 + OUT0)
                for half in range(HALF):
                    pe.matmul(c.ps[:, 6 + half, :], wkr[:, :], kvT[:, half_cols(half)],
                              start=True, stop=True).then_inc(kr.sem, 1)
                pe.wait_ge(w_a.sem, it * 32 + 32)
                for dt in range(DT):
                    for h in range(2):
                        mm = pe.matmul(c.ps[:, dt, h * DCQ:(h + 1) * DCQ], wq2[:, h, dt * P:(dt + 1) * P],
                                       wkq[:, h, :], start=True, stop=True)
                    mm.then_inc(a_done.sem, 1)

                def packed(k):
                    half, tile = k // 3, TILE_ORDER[k % 3]
                    if k == 0:
                        pe.wait_ge(mp_done.sem, it * 2 + 2)
                    if k >= 4:
                        pe.wait_ge(rope.sem, it * 12 + 2 * (k - 3))
                    for dt in range(DT):
                        mm = pe.matmul(c.ps[:, QB_BANKS[k % 4], :], mp[:, dt, tile * P:(tile + 1) * P],
                                       c.xnT[:, dt, half_cols(half)], start=(dt == 0), stop=(dt == DT - 1))
                    mm.then_inc(qb.sem, 1)

                def scored_both(half):
                    pe.wait_ge(rope.sem, it * 12 + (6 * half + 2))
                    for cs in range(2):
                        pe.matmul(c.ps[:, 4 + half, :], wr[:, cs, 1, :], qcs[:, half, 1, cs, :],
                                  start=(cs == 0), stop=False, skip_group_check=True)

                def scored_own(half):
                    pe.wait_ge(rope.sem, it * 12 + (6 * half + 6))
                    for cs in range(2):
                        for h, tile in ((0, 0), (1, 2)):
                            mm = pe.matmul(c.ps[rows(h), 4 + half, :], wr[:, cs, tile, rows(h)],
                                           qcs[:, half, tile, cs, :], start=False, stop=(cs == 1),
                                           skip_group_check=True)
                    mm.then_inc(qr.sem, 1)

                pe.wait_ge(w_r.sem, it * 16 + 16)
                for k in range(4):
                    packed(k)
                scored_both(0)
                packed(4)
                scored_own(0)
                packed(5)
                scored_both(1)
                scored_own(1)

                pe.wait_ge(k_ev.sem, it * 4 + 4)
                pe.wait_ge(q_ev.sem, it * 2 + 2)
                pe.wait_ge(q_ev2.sem, it * 2 + 2)
                pe.wait_ge(z_in.sem, it * 32 + Z0)
                for k in range(8):
                    b, h = k // 2, k % 2
                    if k >= 2:
                        pe.wait_ge(mx.sem, it * 8 + (k - 1))
                    else:
                        pe.wait_ge(rope.sem, it * 12 + 12)
                    keys = ks[:, h, b * SEQ:(b + 1) * SEQ]
                    for qt in range(QT):
                        q0 = b * SEQ + qt * P
                        mm = pe.matmul(c.ps[:, k % 2, qt * SEQ:(qt + 1) * SEQ], qa[:, h, q0:q0 + P], keys,
                                       start=True, stop=True)
                    mm.then_inc(s_done.sem, 1)
                pe.wait_ge(w_n.sem, it * 32 + 32)
                for h in range(2):
                    mm = pe.matmul(c.ps[rows(h), 5, 0:DIM], wkv[:, h, :], wo[:, h, :], start=True, stop=True)
                mm.then_inc(n_done.sem, 1)
                pe.wait_ge(mx.sem, it * 8 + 8)
                pe.transpose(c.ps[0:MR, 7, 0:P], nm[:, :, :, :].rearrange("p h b t -> p (h b t)"),
                             c.ident[:, :]).then_inc(tr.sem, 1)
                pe.wait_ge(m_in.sem, it * 32 + 32)

                def scores_t(b):
                    if b == 1:
                        pe.wait_ge(nw_done.sem, it + 1)
                    if b >= 2:
                        pe.wait_ge(ex.sem, it * 4 + (b - 1))
                    for h in range(2):
                        bank = 2 + 2 * (b % 2) + h
                        queries = slice(b * SEQ, (b + 1) * SEQ)
                        for kt in range(QT):
                            keys = ks[:, h, b * SEQ + kt * P:b * SEQ + (kt + 1) * P]
                            dst = c.ps[:, bank, kt * SEQ:(kt + 1) * SEQ]
                            mm = pe.matmul(dst, keys, qa[:, h, queries], start=True, stop=True)
                    mm.then_inc(stt.sem, 1)

                def product(b):
                    pe.wait_ge(ex.sem, it * 4 + (b + 1))
                    pe.wait_ge(out.sem, it * 8 + (OUT0 + 2 * b))
                    for cols, lhs in ((slice(0, SEQ), None), (slice(SEQ, 2 * SEQ), ones)):
                        for kt in range(QT):
                            for h in range(2):
                                w = kvr[:, b * QT + kt, :] if lhs is None else ones[:, :]
                                mm = pe.matmul(c.ps[rows(h), 6, cols], w, pt[:, b % 2, h, kt, :],
                                               start=(kt == 0), stop=(kt == QT - 1))
                    mm.then_inc(av.sem, 1)

                scores_t(0)
                for b in range(1, BATCH):
                    scores_t(b)
                    product(b - 1)
                product(BATCH - 1)


FT = FFN // P


def ternary_weights(c, st):
    nc, io = c.nc, c.io
    wb = st.enter_context(nc.sbuf_tensor("f_wb", [P, 3, DT * FFN], BF16))
    mean = st.enter_context(nc.sbuf_tensor("f_mean", [P, 3], F32))
    with ExitStack() as tmp:
        def sb(n, shape, dt=F32):
            return tmp.enter_context(nc.sbuf_tensor(f"fw_{n}", shape, dt))

        w = sb("w", [P, 3, DT * FFN])
        junk = sb("junk", [P, DT * FFN])
        asum, inv, ones = sb("asum", [P, 3]), sb("inv", [P, 3]), sb("ones", [P, P])
        w_in = [c.counter(f"fw_in{k}") for k in range(3)]
        summed, total, step, q = c.counter("fw_sum"), c.counter("fw_total"), c.counter("fw_step"), c.counter("fw_q")
        with nc.Block() as block:

            @block.sync
            def _(sp):
                for k in range(3):
                    sp.dma_start(w[:, k, :], io["f_w"][k]).then_inc(w_in[k].sem, 16)

            @block.scalar
            def _(act):
                for k in range(3):
                    act.wait_ge(w_in[k].sem, 16)
                    if k:
                        act.wait_ge(summed.sem, k)
                    act.activation(junk[:, :], w[:, k, :], ACT.Abs, accum_out=asum[:, k:k + 1])\
                        .then_inc(summed.sem, 1)

            @block.tensor
            def _(pe):
                pe.wait_ge(step.sem, 1)
                pe.wait_ge(summed.sem, 3)
                pe.matmul(c.ps[:, 0, 0:3], ones[:, :], asum[:, :], start=True, stop=True)\
                    .then_inc(total.sem, 1)

            @block.vector
            def _(dve):
                dve.memset(ones[:, :], 1.0).then_inc(step.sem, 1)
                dve.wait_ge(total.sem, 1)
                dve.tensor_scalar(mean[:, :], c.ps[:, 0, 0:3], 1.0 / (FFN * DIM), QUANT_EPS, ALU.mult, ALU.max)\
                    .then_inc(step.sem, 1)
                dve.wait_ge(step.sem, 2)
                dve.reciprocal(inv[:, :], mean[:, :]).then_inc(step.sem, 1)
                dve.wait_ge(step.sem, 3)
                for k in range(3):
                    dve.tensor_scalar(w[:, k, :], w[:, k, :], inv[:, k:k + 1], ROUND, ALU.mult, ALU.add)\
                        .then_inc(q.sem, 1)
                for k in range(3):
                    dve.wait_ge(q.sem, k + 1)
                    dve.tensor_scalar(w[:, k, :], w[:, k, :], -ROUND, -1.0, ALU.add, ALU.max)\
                        .then_inc(q.sem, 1)
                for k in range(3):
                    dve.wait_ge(q.sem, 3 + k + 1)
                    dve.tensor_scalar(wb[:, k, :], w[:, k, :], 1.0, None, ALU.min).then_inc(q.sem, 1)
                dve.wait_ge(q.sem, 9)
    return wb, mean


def quantise(dve, tile, scale, out, sig, first, n):
    dve.tensor_scalar(tile, tile, scale, INT8_MAX, ALU.mult, ALU.min).then_inc(sig.sem, 1)
    dve.wait_ge(sig.sem, first + 1)
    dve.tensor_scalar(tile, tile, INT8_MIN, ROUND, ALU.max, ALU.add).then_inc(sig.sem, 1)
    dve.wait_ge(sig.sem, first + 2)
    dve.tensor_scalar(out, tile, -ROUND, None, ALU.add).then_inc(sig.sem, 1)


def ffn_stages(c):
    nc, io = c.nc, c.io
    with ExitStack() as st:
        wb, mean = ternary_weights(c, st)
        layer_norm(c, "ln3", want_t=False)

        def sb(n, shape, dt=F32):
            return st.enter_context(nc.sbuf_tensor(f"f_{n}", shape, dt))

        amax, qsc = sb("amax", [P, TT]), sb("qsc", [P, TT])
        deq = sb("deq", [P, 2, TT])
        xq = sb("xq", [P, TT, DIM], BF16)
        xqT = sb("xqT", [P, DT, TOK], BF16)
        h = sb("h", [P, TT, FFN])
        sg = sb("sg", [P, 2, FFN])
        a_s, q_s, tr, ev = c.counter("f_a"), c.counter("f_q"), c.counter("f_tr"), c.counter("f_ev")
        gu, silu, hd = c.counter("f_gu"), c.counter("f_silu"), c.counter("f_h")
        sq = c.counter("f_sq")
        ssq = sb("ssq", [P, TT])

        def bank16(k):
            return c.ps[:, k, :].bitcast(BF16)

        with nc.Block() as block:

            @block.vector
            def _(dve):
                dve.tensor_reduce(amax[:, :], c.xn[:, :, :], AX.X, ALU.max, apply_absolute_value=True)\
                    .then_inc(a_s.sem, 1)
                dve.wait_ge(a_s.sem, 1)
                dve.tensor_scalar(amax[:, :], amax[:, :], QUANT_EPS, None, ALU.max).then_inc(a_s.sem, 1)
                dve.wait_ge(a_s.sem, 2)
                dve.reciprocal(qsc[:, :], amax[:, :]).then_inc(a_s.sem, 1)
                dve.wait_ge(a_s.sem, 3)
                dve.tensor_scalar(qsc[:, :], qsc[:, :], INT8_MAX, None, ALU.mult).then_inc(a_s.sem, 1)
                for k in range(2):
                    dve.tensor_scalar(deq[:, k, :], amax[:, :], mean[:, k:k + 1], 1.0 / INT8_MAX,
                                      ALU.mult, ALU.mult).then_inc(a_s.sem, 1)
                dve.wait_ge(a_s.sem, 6)
                for t in range(TT):
                    quantise(dve, c.xn[:, t, :], qsc[:, t:t + 1], xq[:, t, :], q_s, 3 * t, TT)
                for t in range(TT):
                    dve.wait_ge(silu.sem, t + 1)
                    b = 4 * (t % 2) + 2
                    dve.scalar_tensor_tensor(h[:, t, :], c.ps[:, b:b + 2, :].rearrange("p b n -> p (b n)"),
                                             deq[:, 1, t:t + 1], sg[:, t % 2, :], ALU.mult, ALU.mult)\
                        .then_inc(hd.sem, 1)

            @block.tensor
            def _(pe):
                for t in range(TT):
                    pe.wait_ge(q_s.sem, 3 * t + 3)
                    for dt in range(DT):
                        mm = pe.transpose(bank16(dt)[:, t * P:(t + 1) * P], xq[:, t, dt * P:(dt + 1) * P],
                                          c.identb[:, :])
                mm.then_inc(tr.sem, 1)
                pe.wait_ge(ev.sem, 2)
                for t in range(TT):
                    if t >= 2:
                        pe.wait_ge(hd.sem, t - 1)
                    for k in range(2):
                        for n in range(FFN // BANK):
                            for dt in range(DT):
                                mm = pe.matmul(c.ps[:, 4 * (t % 2) + 2 * k + n, :], xqT[:, dt, t * P:(t + 1) * P],
                                               wb[:, k, dt * FFN + n * BANK:dt * FFN + (n + 1) * BANK],
                                               start=(dt == 0), stop=(dt == DT - 1))
                    mm.then_inc(gu.sem, 1)

            @block.scalar
            def _(act):
                act.wait_ge(tr.sem, 1)
                for dt in range(DT):
                    act.activation(xqT[:, dt, :], bank16(dt), ACT.Copy).then_inc(ev.sem, 1)
                for t in range(TT):
                    act.wait_ge(gu.sem, t + 1)
                    if t >= 2:
                        act.wait_ge(hd.sem, t - 1)
                    b = 4 * (t % 2)
                    act.activation(sg[:, t % 2, :], c.ps[:, b:b + 2, :].rearrange("p b n -> p (b n)"),
                                   ACT.Silu, scale=deq[:, 0, t:t + 1]).then_inc(silu.sem, 1)

        with ExitStack() as tmp:
            def sb2(n, shape, dt=F32):
                return tmp.enter_context(nc.sbuf_tensor(f"f2_{n}", shape, dt))

            lnw = sb2("lnw", [P, FFN])
            junk = sb2("junk", [P, FFN])
            rstd = sb2("rstd", [P, TT])
            am, qs2 = sb2("am", [P, TT]), sb2("qs2", [P, TT])
            dd = sb2("dd", [P, TT])
            hq = sb2("hq", [P, 2, FFN], BF16)
            hqT = sb2("hqT", [P, 2, FT, P], BF16)
            lnw_in, r_s, std_s = c.counter("f2_in"), c.counter("f2_r"), c.counter("f2_std")
            n_s, m_s, k_s = c.counter("f2_n"), c.counter("f2_m"), c.counter("f2_k")
            q2, tr2, ev2, y_s, x_s = (c.counter("f2_q"), c.counter("f2_tr"), c.counter("f2_ev"),
                                      c.counter("f2_y"), c.counter("f2_x"))
            with nc.Block() as block:

                @block.sync
                def _(sp):
                    sp.dma_start(lnw[:, :], io["f_ln"].broadcast_to([P, FFN])).then_inc(lnw_in.sem, 16)

                @block.scalar
                def _(act):
                    for t in range(TT):
                        if t:
                            act.wait_ge(sq.sem, t)
                        act.activation(junk[:, :], h[:, t, :], ACT.Square, accum_out=ssq[:, t:t + 1])\
                            .then_inc(sq.sem, 1)
                    act.wait_ge(r_s.sem, 1)
                    act.activation(rstd[:, :], rstd[:, :], ACT.Sqrt).then_inc(std_s.sem, 1)
                    for t in range(TT):
                        act.wait_ge(tr2.sem, t + 1)
                        if t >= 2:
                            act.wait_ge(y_s.sem, t - 1)
                        act.activation(hqT[:, t % 2, :, :].rearrange("p f n -> p (f n)"), bank16(t % 2), ACT.Copy)\
                            .then_inc(ev2.sem, 1)

                @block.vector
                def _(dve):
                    dve.wait_ge(sq.sem, TT)
                    dve.tensor_scalar(rstd[:, :], ssq[:, :], 1.0 / FFN, RMS_EPS, ALU.mult, ALU.add)\
                        .then_inc(r_s.sem, 1)
                    dve.wait_ge(std_s.sem, 1)
                    dve.reciprocal(rstd[:, :], rstd[:, :]).then_inc(r_s.sem, 1)
                    dve.wait_ge(r_s.sem, 2)
                    dve.wait_ge(lnw_in.sem, 16)

                    def residual(t):
                        dve.wait_ge(y_s.sem, t + 1)
                        dve.scalar_tensor_tensor(c.x[:, t, :], c.ps[:, 2 + t % 2, 0:DIM], dd[:, t:t + 1],
                                                 c.x[:, t, :], ALU.mult, ALU.add).then_inc(x_s.sem, 1)

                    for t in range(TT):
                        one = slice(t, t + 1)
                        dve.scalar_tensor_tensor(h[:, t, :], h[:, t, :], rstd[:, one], lnw[:, :], ALU.mult, ALU.mult)\
                            .then_inc(n_s.sem, 1)
                        dve.wait_ge(n_s.sem, t + 1)
                        dve.tensor_reduce(am[:, one], h[:, t, :], AX.X, ALU.max, apply_absolute_value=True)\
                            .then_inc(m_s.sem, 1)
                        dve.wait_ge(m_s.sem, t + 1)
                        dve.tensor_scalar(am[:, one], am[:, one], QUANT_EPS, None, ALU.max).then_inc(k_s.sem, 1)
                        dve.wait_ge(k_s.sem, 4 * t + 1)
                        dve.reciprocal(qs2[:, one], am[:, one]).then_inc(k_s.sem, 1)
                        dve.tensor_scalar(dd[:, one], am[:, one], mean[:, 2:3], 1.0 / INT8_MAX, ALU.mult, ALU.mult)\
                            .then_inc(k_s.sem, 1)
                        dve.wait_ge(k_s.sem, 4 * t + 2)
                        dve.tensor_scalar(qs2[:, one], qs2[:, one], INT8_MAX, None, ALU.mult).then_inc(k_s.sem, 1)
                        dve.wait_ge(k_s.sem, 4 * t + 4)
                        if t >= 2:
                            dve.wait_ge(tr2.sem, t - 1)
                        quantise(dve, h[:, t, :], qs2[:, one], hq[:, t % 2, :], q2, 3 * t, TT)
                        if t >= 1:
                            residual(t - 1)
                    residual(TT - 1)
                    dve.wait_ge(x_s.sem, TT)

                @block.tensor
                def _(pe):
                    for t in range(TT + 1):
                        if t < TT:
                            pe.wait_ge(q2.sem, 3 * t + 3)
                            if t >= 2:
                                pe.wait_ge(ev2.sem, t - 1)
                            for f in range(FT):
                                mm = pe.transpose(bank16(t % 2)[:, f * P:(f + 1) * P],
                                                  hq[:, t % 2, f * P:(f + 1) * P], c.identb[:, :])
                            mm.then_inc(tr2.sem, 1)
                        if t >= 1:
                            u = t - 1
                            pe.wait_ge(ev2.sem, u + 1)
                            if u >= 2:
                                pe.wait_ge(x_s.sem, u - 1)
                            for f in range(FT):
                                mm = pe.matmul(c.ps[:, 2 + u % 2, 0:DIM], hqT[:, u % 2, f, :],
                                               wb[:, 2, f * DIM:(f + 1) * DIM],
                                               start=(f == 0), stop=(f == FT - 1))
                            mm.then_inc(y_s.sem, 1)


def layer1_attentions(c, stages):
    nc, io = c.nc, c.io
    with ExitStack() as st:
        with ExitStack() as own:
            w = own.enter_context(nc.sbuf_tensor("a1_w", [P, 4, DT, DIM], F32))
            w_in = c.counter("a1_w_in")
            with nc.Block() as block:

                @block.sync
                def _(sp):
                    for k in range(4):
                        sp.dma_start(w[:, k, :, :], io["L1_WT"][k].rearrange("(t p) o -> p t o", p=P))\
                            .then_inc(w_in.sem, 16)
                    sp.wait_ge(w_in.sem, 64)
            layer_norm(c, "ln4")
            v = qkv_stage(c, own, "a1", w[:, 0], w[:, 1], w[:, 2], "L1_bias", c.scr_q, c.scr_k)
            av = own.enter_context(nc.sbuf_tensor("a1_av", [P, 4, TOK], F32))
            attention_stage(c, "a1", 16, False, 0.25, v, c.scr_q, c.scr_k, av, alibi=True)
            normalise_stage(c, own, "a1n", 4, 16, av, w[:, 3], "L1_bias")
        if stages < 5:
            return
        layer_norm(c, "ln5")
        with ExitStack() as own:
            v = own.enter_context(nc.sbuf_tensor("x1_v", [P, TT, CTX], F32))
            split_context(c, v)
            av = own.enter_context(nc.sbuf_tensor("x1_av", [P, 8, TOK], F32))
            attention_stage(c, "x1", 8, True, 8.0 ** -0.5, v, c.scr_xq, c.scr_xk, av)
            normalise_stage(c, own, "x1n", 8, 8, av, None, None)


def split_context(c, v):
    nc, io = c.nc, c.io
    with ExitStack() as tmp:
        def sb(n, shape, dt=F32):
            return tmp.enter_context(nc.sbuf_tensor(f"xs_{n}", shape, dt))

        qp = sb("qp", [P, DT, 3, TOK], BF16)
        kp = sb("kp", [CTX, 3, TOK], BF16)
        qrest, krest = sb("qrest", [P, DT, TOK]), sb("krest", [CTX, TOK])
        v_in, tr, k_s, qh, q_r, q_m, ql, stored, cleared = (
            c.counter("xs_v"), c.counter("xs_tr"), c.counter("xs_k"), c.counter("xs_qh"), c.counter("xs_qr"),
            c.counter("xs_qm"), c.counter("xs_ql"), c.counter("xs_st"), c.counter("xs_cleared"))
        kps = c.ps[0:CTX, 0:2, :].rearrange("p b n -> p (b n)")
        with nc.Block() as block:

            @block.sync
            def _(sp):
                sp.dma_start(v[:, :, :], io["ctx"].rearrange("(t p) d -> p t d", p=P)).then_inc(v_in.sem, 16)
                for dt in range(DT):
                    sp.wait_ge(ql.sem, dt + 1)
                    store_stack(sp, 0, c.scr_xq[16 * dt:16 * dt + 16], qp[:, dt, :, :], stored)
                sp.wait_ge(k_s.sem, 4)
                store_stack(sp, 1, c.scr_xk, kp[:, :, :], stored)
                sp.wait_ge(stored.sem, 16 * TERMS * (DT + 1))

            @block.gpsimd
            def _(pool):
                for k, (tile, first) in enumerate(((c.qs[:, :, :, :], 0), (c.ks[:, :, 0:1, :], 0),
                                                   (c.qs[:, :, :, :], 96), (c.ks[:, :, 0:1, :], 96))):
                    rows = slice(0, 96) if first == 0 else slice(96, P - 2)
                    pool.memset(tile[rows].bitcast(F32), 0.0).then_inc(cleared.sem, 1)
                    pool.wait_ge(cleared.sem, k + 1)

            @block.tensor
            def _(pe):
                pe.wait_ge(v_in.sem, 16)
                for t in range(TT):
                    mm = pe.transpose(c.ps[0:CTX, t // 4, (t % 4) * P:(t % 4 + 1) * P], v[:, t, :],
                                      c.ident[:, :])
                mm.then_inc(tr.sem, 1)

            @block.scalar
            def _(act):
                for dt in range(DT):
                    act.activation(qp[:, dt, 0, :], c.xnT[:, dt, :], ACT.Copy).then_inc(qh.sem, 1)
                act.wait_ge(tr.sem, 1)
                act.activation(kp[:, 0, :], kps, ACT.Copy).then_inc(k_s.sem, 1)
                for dt in range(DT):
                    act.wait_ge(q_r.sem, dt + 1)
                    act.activation(qp[:, dt, 1, :], qrest[:, dt, :], ACT.Copy).then_inc(q_m.sem, 1)
                act.wait_ge(k_s.sem, 2)
                act.activation(kp[:, 1, :], krest[:, :], ACT.Copy).then_inc(k_s.sem, 1)

            @block.vector
            def _(dve):
                for dt in range(DT):
                    dve.wait_ge(qh.sem, dt + 1)
                    dve.tensor_tensor(qrest[:, dt, :], c.xnT[:, dt, :], qp[:, dt, 0, :], ALU.subtract)\
                        .then_inc(q_r.sem, 1)
                dve.wait_ge(k_s.sem, 1)
                dve.tensor_tensor(krest[:, :], kps, kp[:, 0, :], ALU.subtract).then_inc(k_s.sem, 1)
                for dt in range(DT):
                    dve.wait_ge(q_m.sem, dt + 1)
                    dve.tensor_tensor(qp[:, dt, 2, :], qrest[:, dt, :], qp[:, dt, 1, :], ALU.subtract)\
                        .then_inc(ql.sem, 1)
                dve.wait_ge(k_s.sem, 3)
                dve.tensor_tensor(kp[:, 2, :], krest[:, :], kp[:, 1, :], ALU.subtract).then_inc(k_s.sem, 1)


def moe_stages(c):
    nc, io = c.nc, c.io
    layer_norm(c, "ln6")
    NX = EXPERTS + 1
    with ExitStack() as st:
        def sb(n, shape, dt=F32):
            return st.enter_context(nc.sbuf_tensor(f"x_{n}", shape, dt))

        gw = sb("gw", [P, DT, EXPERTS])
        iota = sb("iota", [P, EXPERTS])
        score = sb("score", [P, TT, EXPERTS])
        best = sb("best", [P, TT, 8])
        bidx = sb("bidx", [P, TT, 8], U32)
        bidf = sb("bidf", [P, TT, TOPK])
        hit = sb("hit", [P, TOPK, TT, EXPERTS])
        gate = sb("gate", [P, TT, NX])
        gT = sb("gT", [NX, TOK])
        g_in, logit, sc = c.counter("x_gate_in"), c.counter("x_logit"), c.counter("x_score")
        mxs, ids, st_s = c.counter("x_max"), c.counter("x_ids"), c.counter("x_step")
        gtr, gev, gst = c.counter("x_gtr"), c.counter("x_gev"), c.counter("x_gst")

        with nc.Block() as block:

            @block.sync
            def _(sp):
                sp.dma_start(gw[:, :, :], io["gate_wT"].rearrange("(t p) e -> p t e", p=P)).then_inc(g_in.sem, 16)
                sp.dma_start(iota[:, :], io["iota"].broadcast_to([P, EXPERTS])).then_inc(g_in.sem, 16)
                sp.wait_ge(gev.sem, 1)
                sp.dma_start(c.scr_g, gT[:, :]).then_inc(gst.sem, 16)
                sp.wait_ge(gst.sem, 16)

            @block.tensor
            def _(pe):
                pe.wait_ge(g_in.sem, 32)
                for t in range(TT):
                    for dt in range(DT):
                        mm = pe.matmul(c.ps[:, 0, t * EXPERTS:(t + 1) * EXPERTS], c.xnT[:, dt, t * P:(t + 1) * P],
                                       gw[:, dt, :], start=(dt == 0), stop=(dt == DT - 1))
                mm.then_inc(logit.sem, 1)
                pe.wait_ge(st_s.sem, 7)
                for t in range(TT):
                    mm = pe.transpose(c.ps[0:NX, 1 + t // 4, (t % 4) * P:(t % 4 + 1) * P], gate[:, t, :],
                                      c.ident[:, :])
                mm.then_inc(gtr.sem, 1)

            @block.scalar
            def _(act):
                act.wait_ge(logit.sem, 1)
                act.activation(score[:, :, :].rearrange("p t e -> p (t e)"), c.ps[:, 0, 0:TT * EXPERTS],
                               ACT.Sigmoid).then_inc(sc.sem, 1)
                act.wait_ge(gtr.sem, 1)
                act.activation(gT[:, :], c.ps[0:NX, 1:3, :].rearrange("p b n -> p (b n)"), ACT.Copy)\
                    .then_inc(gev.sem, 1)

            @block.vector
            def _(dve):
                dve.memset(gate[:, :, :], 1.0).then_inc(st_s.sem, 1)
                dve.wait_ge(sc.sem, 1)
                for t in range(TT):
                    dve.max(best[:, t, :], score[:, t, :]).then_inc(mxs.sem, 1)
                for t in range(TT):
                    dve.wait_ge(mxs.sem, t + 1)
                    dve.max_index(bidx[:, t, :], best[:, t, :], score[:, t, :]).then_inc(ids.sem, 1)
                dve.wait_ge(ids.sem, TT)
                dve.tensor_copy(bidf[:, :, :], bidx[:, :, 0:TOPK]).then_inc(st_s.sem, 1)
                dve.wait_ge(st_s.sem, 2)
                for k in range(TOPK):
                    dve.tensor_tensor(hit[:, k, :, :], iota[:, :].unsqueeze(1).broadcast_to([P, TT, EXPERTS]),
                                      bidf[:, :, k:k + 1].broadcast_to([P, TT, EXPERTS]), ALU.is_equal)\
                        .then_inc(st_s.sem, 1)
                for k in range(TOPK):
                    dve.wait_ge(st_s.sem, 3 + k)
                    dve.tensor_tensor(hit[:, k, :, :], hit[:, k, :, :],
                                      best[:, :, k:k + 1].broadcast_to([P, TT, EXPERTS]), ALU.mult)\
                        .then_inc(st_s.sem, 1)
                dve.wait_ge(st_s.sem, 6)
                dve.tensor_tensor(gate[:, :, 0:EXPERTS], hit[:, 0, :, :], hit[:, 1, :, :], ALU.add)\
                    .then_inc(st_s.sem, 1)

        BUF = 3
        w13 = sb("w13", [P, BUF, 2, DT, EH])
        w2 = sb("w2", [P, BUF, DIM])
        gb = sb("gb", [P, BUF, TOK])
        h1g = sb("h1g", [P, 2, BANK])
        sg = sb("sg", [P, 2, BANK])
        h3 = sb("h3", [P, 2, BANK])
        hT = sb("hT", [P, 2, BANK])
        w_in = [c.counter(f"e_in{b}") for b in range(BUF)]
        p13, gm, sl, m3, hd = c.counter("e_p13"), c.counter("e_gm"), c.counter("e_silu"), c.counter("e_m3"), c.counter("e_h")
        down, seeded, x_s = c.counter("e_down"), c.counter("e_seed"), c.counter("e_x")
        D0 = 2 * BUF
        with nc.Block() as block:

            @block.sync
            def _(sp):
                with sp.Fori(0, NX // BUF) as it:
                    for b in range(BUF):
                        e = it * BUF + b
                        sp.wait_ge(down.sem, e * 2 + 2)
                        one = bass.ds(e, 1)
                        sp.dma_start(w13[:, b], io["e_w13"][one]).then_inc(w_in[b].sem, 16)
                        sp.dma_start(w2[:, b], io["e_w2"][one]).then_inc(w_in[b].sem, 16)
                        sp.dma_start(gb[:, b], c.scr_g[one, :].broadcast_to([P, TOK])).then_inc(w_in[b].sem, 16)

            @block.vector
            def _(dve):
                dve.sem_inc(down.sem, D0)
                with dve.Fori(0, NX // BUF) as it:
                    for k in range(2 * BUF):
                        b, half = k // 2, k % 2
                        n = it * (2 * BUF) + k
                        cols = slice(half * BANK, (half + 1) * BANK)
                        dve.wait_ge(w_in[b].sem, it * 48 + 48)
                        dve.wait_ge(p13.sem, n * 2 + 1)
                        dve.tensor_tensor(h1g[:, half, :], c.ps[:, 4 + half, :], gb[:, b, cols], ALU.mult)\
                            .then_inc(gm.sem, 1)
                        dve.wait_ge(sl.sem, n + 1)
                        dve.wait_ge(p13.sem, n * 2 + 2)
                        dve.tensor_tensor(h3[:, half, :], c.ps[:, 6 + half, :], sg[:, half, :], ALU.mult)\
                            .then_inc(m3.sem, 1)
                for t in range(TT):
                    if t == 0:
                        dve.wait_ge(down.sem, D0 + 2 * NX)
                    dve.tensor_copy(c.x[:, t, :], c.ps[:, t // 2, (t % 2) * DIM:(t % 2 + 1) * DIM])\
                        .then_inc(x_s.sem, 1)
                dve.wait_ge(x_s.sem, TT)

            @block.scalar
            def _(act):
                with act.Fori(0, NX // BUF) as it:
                    for k in range(2 * BUF):
                        n = it * (2 * BUF) + k
                        act.wait_ge(gm.sem, n + 1)
                        act.activation(sg[:, k % 2, :], h1g[:, k % 2, :], ACT.Silu).then_inc(sl.sem, 1)

            @block.gpsimd
            def _(pool):
                with pool.Fori(0, NX // BUF) as it:
                    for k in range(2 * BUF):
                        b, half = k // 2, k % 2
                        n = it * (2 * BUF) + k
                        cols = slice(half * BANK, (half + 1) * BANK)
                        pool.wait_ge(down.sem, n + (D0 - 1))
                        pool.wait_ge(m3.sem, n + 1)
                        pool.tensor_tensor(hT[:, half, :], h3[:, half, :], gb[:, b, cols], ALU.mult)\
                            .then_inc(hd.sem, 1)

            @block.tensor
            def _(pe):
                for k in range(TT // 2):
                    pe.matmul(c.ps[:, k, :], c.ident[:, :], c.x[:, 2 * k:2 * k + 2, :].rearrange("p t d -> p (t d)"),
                              start=True, stop=True)

                def up(it, k):
                    b, half = k // 2, k % 2
                    n = it * (2 * BUF) + k
                    if half == 0:
                        pe.wait_ge(w_in[b].sem, it * 48 + 48)
                    if k >= 2:
                        pe.wait_ge(m3.sem, n - 1)
                    for j in range(2):
                        for dt in range(DT):
                            mm = pe.matmul(c.ps[:, 4 + 2 * j + half, :], w13[:, b, j, dt, :],
                                           c.xnT[:, dt, half * BANK:(half + 1) * BANK],
                                           start=(dt == 0), stop=(dt == DT - 1))
                        mm.then_inc(p13.sem, 1)

                def add(it, k):
                    b, half = k // 2, k % 2
                    n = it * (2 * BUF) + k
                    pe.wait_ge(hd.sem, n + 1)
                    for j in range(4):
                        t = 4 * half + j
                        mm = pe.matmul(c.ps[:, t // 2, (t % 2) * DIM:(t % 2 + 1) * DIM],
                                       hT[:, half, j * P:(j + 1) * P], w2[:, b, :],
                                       start=False, stop=True, skip_group_check=True)
                    mm.then_inc(down.sem, 1)

                with pe.Fori(0, NX // BUF) as it:
                    for k in range(2 * BUF + 1):
                        if k < 2 * BUF:
                            up(it, k)
                        if k >= 1:
                            add(it, k - 1)


def store_stage(c, out):
    nc = c.nc
    stored = c.counter("stored")
    with nc.Block() as block:

        @block.sync
        def _(sp):
            sp.dma_start(out.rearrange("(t p) d -> p t d", p=P), c.x[:, :, :]).then_inc(stored.sem, 16)
            sp.wait_ge(stored.sem, 16)


STAGES = 6


def build_program(nc, io, out):
    with ExitStack() as ctx:
        c = Chip(nc, ctx, io)
        load_stage(c)
        c.xn = c.sbuf("xn", [P, TT, DIM])
        c.scr_q = nc.dram_tensor("scr_q", (16, TERMS, 16, TOK), BF16, kind="Internal").ap()
        c.scr_k = nc.dram_tensor("scr_k", (16, TERMS, 16, TOK), BF16, kind="Internal").ap()
        c.scr_xq = nc.dram_tensor("scr_xq", (32, TERMS, 8, TOK), BF16, kind="Internal").ap()
        c.scr_xk = nc.dram_tensor("scr_xk", (8, TERMS, 8, TOK), BF16, kind="Internal").ap()
        c.scr_g = nc.dram_tensor("scr_g", (EXPERTS + 1, TOK), F32, kind="Internal").ap()
        c.scr_al = nc.dram_tensor("scr_al", (9, 16, SEQ), BF16, kind="Internal").ap()

        layer_norm(c, "ln1")
        with ExitStack() as st:
            wT = lora_fold(c, st, None)
            v = qkv_stage(c, st, "a0", wT[:, 0], wT[:, 1], wT[:, 2], "L0_bias", c.scr_q, c.scr_k)
            av = st.enter_context(nc.sbuf_tensor("a0_av", [P, 4, TOK], F32))
            attention_stage(c, "a0", 16, False, 0.25, v, c.scr_q, c.scr_k, av)
            normalise_stage(c, st, "a0n", 4, 16, av, wT[:, 3], "L0_bias")
        if STAGES >= 2:
            mla_stages(c)
        if STAGES >= 3:
            ffn_stages(c)
        if STAGES >= 4:
            layer1_attentions(c, STAGES)
        if STAGES >= 6:
            moe_stages(c)
        store_stage(c, out)



def _constants():
    q = np.arange(SEQ)
    causal = np.where(q[None, :] <= q[:, None], 0.0, NEG).astype(np.float32)
    masks = np.stack([
        causal.reshape(QT, P, SEQ).transpose(1, 0, 2).reshape(P, BANK),
        np.concatenate([causal.T[0:P]] * 2, 1),
        np.concatenate([causal.T[P:2 * P]] * 2, 1),
    ], 1)
    pos = q.astype(np.float32).reshape(1, SEQ)

    def rope(length, dim):
        inv = (np.float32(1.0) / np.float32(10000.0) ** (np.arange(0, dim, 2, dtype=np.float32) / np.float32(dim)))
        f = np.arange(length, dtype=np.float32)[:, None] * inv.astype(np.float32)[None, :]
        return np.repeat(np.sin(f), 2, -1).astype(np.float32), np.repeat(np.cos(f), 2, -1).astype(np.float32)

    sin_q, cos_q = rope(SEQ, DCQ)
    hq = DCQ // 2
    sin_moved = np.concatenate([sin_q[:, hq:], -sin_q[:, :hq]], 1)
    rope_q = np.stack([np.concatenate([t.T, t.T]).reshape(3, P, SEQ) for t in (cos_q, sin_moved)])
    sin_k, cos_k = rope(SEQ, CTX)
    hk = CTX // 2
    sin_signed = np.concatenate([-sin_k[:, :hk], sin_k[:, hk:]], 1)
    rope_k = np.stack([t.reshape(QT, P, CTX) for t in (cos_k, sin_signed)])
    return dict(ident=np.eye(P, dtype=np.float32), masks=masks, pos=pos,
                rope_q=rope_q.transpose(2, 0, 1, 3), rope_k=rope_k.transpose(2, 0, 1, 3))


def _columns(rows):
    return rows.reshape(len(rows), DT, P).transpose(2, 0, 1)


def _layout(inputs):
    k = _constants()
    c = np.ascontiguousarray
    a = {n: np.asarray(v) for n, v in inputs.items()}
    io = {
        "x": c(a["x"].reshape(TOK, DIM)),
        "ident": k["ident"], "masks": c(k["masks"]), "pos": c(k["pos"]),
        "L0_WT": np.stack([a[f"L0_attn_W{n}"].T for n in "qkvo"]),
        "L0_B": np.stack([a[f"L0_attn_B{n}"] for n in "qkvo"]),
        "L0_AT": np.stack([a[f"L0_attn_A{n}"].T for n in "qkvo"]),
        "L0_bias": np.stack([a[f"L0_attn_b{n}"] for n in "qkvo"]),
        "L0_bias_col": _columns(np.stack([a["L0_attn_bq"], a["L0_attn_bk"]])),
        "slopes": c(a["L1_attn_alibi_slopes"].reshape(16, 1)),
    }
    wqr = a["L0_xattn_W_qr"]
    wr = np.zeros((PAIRS, 2, 2 * DCQ, 2, R), np.float32)
    for h in range(2):
        for cs, moved in enumerate((wqr, np.roll(wqr, -(DCQ // 2), 1))):
            wr[:, cs, h * DCQ:(h + 1) * DCQ, h] = moved[h::2]
    wkr = np.zeros((PAIRS, P, 2, R), np.float32)
    for h in range(2):
        wkr[:, 0:CTX, h] = a["L0_xattn_W_kr"][h::2]
    pairs = lambda w, r: w.reshape(PAIRS, 2, P, r).transpose(0, 2, 1, 3)
    io.update({
        "ctx": a["ctx_512"].reshape(TOK, CTX),
        "rope_q": k["rope_q"], "rope_k": k["rope_k"],
        "m_wq": pairs(a["L0_xattn_Wq"], DIM), "m_wkq": pairs(a["L0_xattn_w_kc_q"], DCQ),
        "m_wr": wr.reshape(PAIRS, 2, 3, P, 2 * R).transpose(0, 3, 1, 2, 4),
        "m_wkr": wkr.reshape(PAIRS, P, 2 * R),
        "m_wkv": pairs(a["L0_xattn_w_kc_kv"], CTX), "m_wo": pairs(a["L0_xattn_Wo"].T, DIM),
    })
    tiles = lambda w: w.reshape(-1, P, w.shape[-1]).transpose(1, 0, 2).reshape(P, -1)
    qkv = a["L1_attn_qkv_w"].reshape(3, DIM, DIM)
    bias = np.concatenate([a["L1_attn_qkv_b"].reshape(3, DIM), a["L1_attn_out_b"][None]])
    w1 = np.concatenate([a["L1_ffn_w1"], a["L1_ffn_ws1"][None]])
    w3 = np.concatenate([a["L1_ffn_w3"], a["L1_ffn_ws3"][None]])
    w2 = np.concatenate([a["L1_ffn_w2"], a["L1_ffn_ws2"][None]])
    io.update({
        "f_w": np.stack([tiles(a["L0_ffn_w_gate"].T), tiles(a["L0_ffn_w_up"].T), tiles(a["L0_ffn_w_down"].T)]),
        "f_ln": a["L0_ffn_ln_weight"].reshape(1, FFN),
        "L1_WT": np.concatenate([qkv, a["L1_attn_out_w"][None]]).transpose(0, 2, 1),
        "L1_bias": bias, "L1_bias_col": _columns(bias[0:2]),
        "gate_wT": a["L1_ffn_gate_w"].T, "iota": np.arange(EXPERTS, dtype=np.float32).reshape(1, EXPERTS),
        "e_w13": np.stack([w1, w3], 1).reshape(EXPERTS + 1, 2, EH, DT, P).transpose(0, 4, 1, 3, 2),
        "e_w2": w2.transpose(0, 2, 1),
    })
    return {n: c(v) for n, v in io.items()}


def kernel(**inputs):
    import concourse.bacc as bacc
    from concourse.bass_utils import run_bass_kernel_spmd

    nc = bacc.Bacc("TRN2", target_bir_lowering=False, num_devices=1)
    arrays = _layout(inputs)
    io = {n: nc.dram_tensor(f"in_{n}", v.shape, mybir.dt.from_np(v.dtype), kind="ExternalInput").ap()
          for n, v in arrays.items()}
    out = nc.dram_tensor("out_x", (TOK, DIM), F32, kind="ExternalOutput").ap()
    build_program(nc, io, out)
    r = run_bass_kernel_spmd(nc, [{f"in_{n}": v for n, v in arrays.items()}], core_ids=[0])
    return r.results[0]["out_x"].reshape(BATCH, SEQ, DIM)
```

```python
from contextlib import ExitStack

import numpy as np

import concourse.bass as bass
from concourse import mybir

F32 = mybir.dt.float32
BF16 = mybir.dt.bfloat16
U32 = mybir.dt.uint32
ALU = mybir.AluOpType
ACT = mybir.ActivationFunctionType
AX = mybir.AxisListType

P = 128
BATCH, SEQ, DIM = 4, 256, 256
CTX = 64
TOK = BATCH * SEQ
TT = TOK // P
DT = DIM // P
QT = SEQ // P
BANK = 512
HALF = TOK // BANK
LN_EPS = 1e-5
RMS_EPS = 1e-6
QUANT_EPS = 1e-5
INT8_MAX, INT8_MIN = 127.0, -128.0
ROUND = 1.5 * 2.0**23
NEG = -1.0e30
FFN = 1024
EXPERTS, TOPK, EH = 8, 2, 128
ITEMS = 8
TERMS = 6
SCOLS = 32


class Signal:

    def __init__(self, sem):
        self.sem = sem
        self.base = 0

    def at(self, n):
        return n + self.base

    def done(self, n):
        self.base += n


class Chip:

    def __init__(self, nc, ctx, io):
        self.nc, self.ctx, self.io = nc, ctx, io
        self.counters = {}

    def sbuf(self, name, shape, dtype=F32):
        return self.ctx.enter_context(self.nc.sbuf_tensor(name, shape, dtype))

    def counter(self, name):
        if name not in self.counters:
            self.counters[name] = Signal(self.ctx.enter_context(self.nc.semaphore(name)))
        return self.counters[name]



def load_stage(c):
    nc, io = c.nc, c.io
    c.ps = c.ctx.enter_context(nc.psum_tensor("ps", [P, 8, BANK], F32))
    c.x = c.sbuf("x", [P, TT, DIM])
    c.xnT = c.sbuf("xnT", [P, DT, TOK])
    c.ident = c.sbuf("ident", [P, P])
    c.identb = c.sbuf("identb", [P, P], BF16)
    c.qs = c.sbuf("qs", [P, ITEMS, 4, SEQ], BF16)
    c.ks = c.sbuf("ks", [P, ITEMS, 4, SEQ], BF16)
    cleared = c.cleared = c.counter("cleared")
    c.fw = c.sbuf("fw", [P, 3, DT * FFN])
    c.wb = c.sbuf("wb", [P, 3, DT * FFN], BF16)
    c.fmean, c.finv = c.sbuf("fmean", [P, 3]), c.sbuf("finv", [P, 3])
    c.fw_in = [c.counter(f"fw_in{k}") for k in range(3)]
    x_in = c.counter("x_in")
    const_in = c.counter("const_in")
    ident_cast = c.counter("ident_cast")

    with nc.Block() as block:

        @block.sync
        def _(sp):
            sp.dma_start(c.x[:, :, :], io["x"].rearrange("(t p) d -> p t d", p=P)).then_inc(x_in.sem, 16)
            sp.dma_start(c.ident[:, :], io["ident"]).then_inc(const_in.sem, 16)

        @block.vector
        def _(dve):
            dve.memset(c.qs[:, :, :, :].bitcast(F32), 0.0).then_inc(cleared.sem, 1)
            dve.wait_ge(const_in.sem, 16)
            dve.wait_ge(x_in.sem, 16)
            dve.tensor_copy(c.identb[:, :], c.ident[:, :]).then_inc(ident_cast.sem, 1)
            dve.wait_ge(ident_cast.sem, 1)



def layer_norm(c, name, want_t=True):
    nc = c.nc
    with ExitStack() as st:
        stats = st.enter_context(nc.sbuf_tensor(f"{name}_stats", [P, TT, 6], F32))
        mv = st.enter_context(nc.sbuf_tensor(f"{name}_mv", [P, TT, 2], F32))
        std = st.enter_context(nc.sbuf_tensor(f"{name}_std", [P, TT], F32))
        rstd = st.enter_context(nc.sbuf_tensor(f"{name}_rstd", [P, TT], F32))
        stats_done, mv_done, var_done = c.counter("ln_stats"), c.counter("ln_mv"), c.counter("ln_var")
        std_done, rstd_done = c.counter("ln_std"), c.counter("ln_rstd")
        xn_done, tr_done, ev_done = c.counter("ln_xn"), c.counter("ln_tr"), c.counter("ln_ev")

        with nc.Block() as block:

            @block.vector
            def _(dve):
                for t in range(TT):
                    dve.bn_stats(stats[:, t, :], c.x[:, t, :]).then_inc(stats_done.sem, 1)
                for t in range(TT):
                    dve.wait_ge(stats_done.sem, stats_done.at(t + 1))
                    dve.bn_aggr(mv[:, t, :], stats[:, t, :]).then_inc(mv_done.sem, 1)
                dve.wait_ge(mv_done.sem, mv_done.at(TT))
                dve.tensor_scalar(std[:, :], mv[:, :, 1], LN_EPS, None, ALU.add).then_inc(var_done.sem, 1)
                dve.wait_ge(std_done.sem, std_done.at(1))
                dve.reciprocal(rstd[:, :], std[:, :]).then_inc(rstd_done.sem, 1)
                dve.wait_ge(rstd_done.sem, rstd_done.at(1))
                for t in range(TT):
                    dve.tensor_scalar(c.xn[:, t, :], c.x[:, t, :], mv[:, t, 0:1], rstd[:, t:t + 1],
                                      ALU.subtract, ALU.mult).then_inc(xn_done.sem, 1)
                if want_t:
                    for k in (1, 3):
                        dve.wait_ge(tr_done.sem, tr_done.at(k + 1))
                        dve.tensor_copy(c.xnT[:, k % 2, (k // 2) * BANK:(k // 2 + 1) * BANK],
                                        c.ps[:, k, :]).then_inc(ev_done.sem, 1)

            @block.scalar
            def _(act):
                act.wait_ge(var_done.sem, var_done.at(1))
                act.activation(std[:, :], std[:, :], ACT.Sqrt).then_inc(std_done.sem, 1)
                if want_t:
                    for k in (0, 2):
                        act.wait_ge(tr_done.sem, tr_done.at(k + 1))
                        act.activation(c.xnT[:, k % 2, (k // 2) * BANK:(k // 2 + 1) * BANK],
                                       c.ps[:, k, :], ACT.Copy).then_inc(ev_done.sem, 1)

            if want_t:
                @block.tensor
                def _(pe):
                    for k in range(4):
                        pe.wait_ge(xn_done.sem, xn_done.at(4 * (k // 2) + 4))
                        for j in range(4):
                            t = 4 * (k // 2) + j
                            mm = pe.transpose(c.ps[:, k, j * P:(j + 1) * P],
                                              c.xn[:, t, (k % 2) * P:(k % 2 + 1) * P], c.ident[:, :])
                        mm.then_inc(tr_done.sem, 1)

            @block.sync
            def _(sp):
                sp.wait_ge(xn_done.sem, xn_done.at(TT))
                if want_t:
                    sp.wait_ge(ev_done.sem, ev_done.at(4))

        for s, n in ((stats_done, TT), (mv_done, TT), (var_done, 1), (std_done, 1), (rstd_done, 1),
                     (xn_done, TT), (tr_done, 4 if want_t else 0), (ev_done, 4 if want_t else 0)):
            s.done(n)



def lora_fold(c, st, names):
    nc, io = c.nc, c.io
    rank = io["L0_B"].shape[1]
    wT = st.enter_context(nc.sbuf_tensor("lora_wT", [P, 4, DT, DIM], F32))
    lb = st.enter_context(nc.sbuf_tensor("lora_b", [rank, 4, DIM], F32))
    la = st.enter_context(nc.sbuf_tensor("lora_aT", [rank, 4, DIM], F32))
    loaded, prod, fold = c.counter("lora_in"), c.counter("lora_prod"), c.counter("lora_fold")
    with nc.Block() as block:

        @block.sync
        def _(sp):
            sp.dma_start(lb[:, :, :], io["L0_B"].rearrange("w r d -> r w d")).then_inc(loaded.sem, 16)
            sp.dma_start(la[:, :, :], io["L0_AT"].rearrange("w r d -> r w d")).then_inc(loaded.sem, 16)
            for w in range(4):
                sp.dma_start(wT[:, w, :, :], io["L0_WT"][w].rearrange("(t p) o -> p t o", p=P))\
                    .then_inc(loaded.sem, 16)
            for k in range(3):
                sp.dma_start(c.fw[:, k, :], io["f_w"][k]).then_inc(c.fw_in[k].sem, 16)
            sp.wait_ge(fold.sem, 4)

        @block.gpsimd
        def _(pool):
            for k, (tile, value) in enumerate(((c.ks[0:96, :, :, :].bitcast(F32), 0.0),
                                               (c.ks[96:P, :, :, :], 1.0),
                                               (c.ks[96:P - 2, :, :, :].bitcast(F32), 0.0))):
                pool.memset(tile, value).then_inc(c.cleared.sem, 1)
                pool.wait_ge(c.cleared.sem, k + 2)

        @block.tensor
        def _(pe):
            pe.wait_ge(loaded.sem, 96)
            for w in range(4):
                for t in range(DT):
                    mm = pe.matmul(c.ps[:, w, t * DIM:(t + 1) * DIM], lb[:, w, t * P:(t + 1) * P],
                                   la[:, w, :], start=True, stop=True)
                mm.then_inc(prod.sem, 1)

        @block.vector
        def _(dve):
            for w in range(4):
                dve.wait_ge(prod.sem, w + 1)
                dve.scalar_tensor_tensor(wT[:, w, :, :], c.ps[:, w, :].rearrange("p (t o) -> p t o", t=DT),
                                         0.5, wT[:, w, :, :], ALU.mult, ALU.add).then_inc(fold.sem, 1)
    return wT


def store_stack(sp, w, dst, parts, stored):
    for k, part in enumerate(((0, 0, 0, 1, 1, 2), (0, 1, 2, 0, 1, 0))[w]):
        sp.dma_start(dst[:, k], parts[:, part, :]).then_inc(stored.sem, 16)



def qkv_stage(c, st, name, wq, wk, wv, bias_io, scr_q, scr_k):
    nc, io = c.nc, c.io
    v = st.enter_context(nc.sbuf_tensor(f"{name}_v", [P, TT, DIM], F32))
    with ExitStack() as tmp:
        parts = tmp.enter_context(nc.sbuf_tensor(f"{name}_parts", [P, 2, DT, 3, TOK], BF16))
        rest = tmp.enter_context(nc.sbuf_tensor(f"{name}_rest", [P, 2, BANK], F32))
        bcol = tmp.enter_context(nc.sbuf_tensor(f"{name}_bcol", [P, 2, DT], F32))
        bv = tmp.enter_context(nc.sbuf_tensor(f"{name}_bv", [P, DIM], F32))
        bias_in, proj = c.counter("qkv_bias"), c.counter("qkv_proj")
        hi_done, rest_done, mid_done, lo_done = (c.counter("qkv_hi"), c.counter("qkv_rest"),
                                                 c.counter("qkv_mid"), c.counter("qkv_lo"))
        vproj, v_done, stored = c.counter("qkv_vproj"), c.counter("qkv_v"), c.counter("qkv_stored")
        groups = [(w, ot, half) for w in range(2) for ot in range(DT) for half in range(HALF)]
        NG = len(groups)

        with nc.Block() as block:

            @block.sync
            def _(sp):
                sp.dma_start(bcol[:, :, :], io[bias_io + "_col"]).then_inc(bias_in.sem, 16)
                sp.dma_start(bv[:, :], io[bias_io][2:3, :].broadcast_to([P, DIM])).then_inc(bias_in.sem, 16)
                for k in range(2 * DT):
                    w, ot = divmod(k, DT)
                    sp.wait_ge(lo_done.sem, lo_done.at(HALF * (k + 1)))
                    store_stack(sp, w, (scr_q, scr_k)[w][8 * ot:8 * ot + 8], parts[:, w, ot, :, :],
                                stored)
                sp.wait_ge(stored.sem, stored.at(16 * TERMS * 2 * DT))
                sp.wait_ge(v_done.sem, v_done.at(TT // 2))

            @block.gpsimd
            def _(pool):
                for g, (w, ot, half) in enumerate(groups):
                    cols = slice(half * BANK, (half + 1) * BANK)
                    pool.wait_ge(mid_done.sem, mid_done.at(g + 1))
                    pool.tensor_tensor(parts[:, w, ot, 2, cols], rest[:, g % 2, :], parts[:, w, ot, 1, cols],
                                       ALU.subtract).then_inc(lo_done.sem, 1)

            @block.tensor
            def _(pe):
                for g, (w, ot, half) in enumerate(groups):
                    if g >= 4:
                        pe.wait_ge(rest_done.sem, rest_done.at(g - 3))
                    for dt in range(DT):
                        mm = pe.matmul(c.ps[:, g % 4, :], (wq, wk)[w][:, dt, ot * P:(ot + 1) * P],
                                       c.xnT[:, dt, half * BANK:(half + 1) * BANK],
                                       start=(dt == 0), stop=(dt == DT - 1))
                    mm.then_inc(proj.sem, 1)
                for t in range(TT):
                    for dt in range(DT):
                        mm = pe.matmul(c.ps[:, 4 + t // 2, (t % 2) * DIM:(t % 2 + 1) * DIM],
                                       c.xnT[:, dt, t * P:(t + 1) * P], wv[:, dt, :],
                                       start=(dt == 0), stop=(dt == DT - 1))
                    if t % 2:
                        mm.then_inc(vproj.sem, 1)

            @block.scalar
            def _(act):
                act.wait_ge(bias_in.sem, bias_in.at(32))
                for g, (w, ot, half) in enumerate(groups + [(None, None, None)]):
                    if g < NG:
                        act.wait_ge(proj.sem, proj.at(g + 1))
                        act.activation(parts[:, w, ot, 0, half * BANK:(half + 1) * BANK], c.ps[:, g % 4, :],
                                       ACT.Identity, bias=bcol[:, w, ot:ot + 1]).then_inc(hi_done.sem, 1)
                    if g >= 1:
                        w, ot, half = groups[g - 1]
                        act.wait_ge(rest_done.sem, rest_done.at(g))
                        act.activation(parts[:, w, ot, 1, half * BANK:(half + 1) * BANK],
                                       rest[:, (g - 1) % 2, :], ACT.Copy).then_inc(mid_done.sem, 1)

            @block.vector
            def _(dve):
                dve.wait_ge(bias_in.sem, bias_in.at(32))
                for g, (w, ot, half) in enumerate(groups):
                    dve.wait_ge(hi_done.sem, hi_done.at(g + 1))
                    if g >= 2:
                        dve.wait_ge(lo_done.sem, lo_done.at(g - 1))
                    dve.scalar_tensor_tensor(rest[:, g % 2, :], c.ps[:, g % 4, :], bcol[:, w, ot:ot + 1],
                                             parts[:, w, ot, 0, half * BANK:(half + 1) * BANK],
                                             ALU.add, ALU.subtract).then_inc(rest_done.sem, 1)
                for k in range(TT // 2):
                    dve.wait_ge(vproj.sem, vproj.at(k + 1))
                    dve.tensor_tensor(v[:, 2 * k:2 * k + 2, :],
                                      c.ps[:, 4 + k, :].rearrange("p (t o) -> p t o", t=2),
                                      bv[:, :].unsqueeze(1).broadcast_to([P, 2, DIM]), ALU.add)\
                        .then_inc(v_done.sem, 1)

        bias_in.done(32)
        for s in (proj, hi_done, rest_done, mid_done, lo_done):
            s.done(NG)
        vproj.done(TT // 2)
        v_done.done(TT // 2)
        stored.done(16 * TERMS * 2 * DT)
    return v



def attention_stage(c, name, hd, shared_k, scale, v, scr_q, scr_k, av_all, alibi=False):
    nc, io = c.nc, c.io
    rows = TERMS * hd
    s_rows = P - 2
    per_seq = 8 if shared_k else 4
    n_seq = ITEMS // per_seq
    NK = 1 if shared_k else 4
    N_ITER = BATCH // n_seq
    LAG, TLAG = 4, 3
    MAXR = 4 * QT * 2
    ST0, AV0, OUT0, EX0 = 2 * ITEMS, ITEMS, 1, 2

    with ExitStack() as st:
        def sb(n, shape, dt=F32):
            return st.enter_context(nc.sbuf_tensor(f"{name}_{n}", shape, dt))

        qs = c.qs
        ks = c.ks[:, :, 0:NK, :]
        vs = sb("vs", [P, ITEMS, QT, NK, SCOLS])
        pt = sb("pt", [P, 2, QT, 4 * SEQ])
        one8 = sb("one8", [P, 4 * QT])
        nm = sb("nm", [P, ITEMS, 4 * QT])
        nms = sb("nms", [P, ITEMS, 2, 4 * QT], BF16)
        mT = sb("mT", [MAXR, ITEMS, P], BF16)
        if alibi:
            slope = sb("slope", [16, 2])
            wide = sb("wide", [16, 3, SEQ])
            pos = sb("pos", [16, SEQ])
            sl = sb("sl", [16, 9, SEQ], BF16)
            maskb = sb("maskb", [P, 3, BANK], BF16)
            maskf = sb("maskf", [P, 3, BANK])

        filled, fill_in = c.counter("at_filled"), c.counter("at_fill_in")
        al, al_in = c.counter("at_alibi"), c.counter("at_alibi_in")
        in_q = [c.counter(f"at_in{i}") for i in range(ITEMS)]
        m_in = [c.counter(f"at_m{i}") for i in range(ITEMS)]
        v_in = c.counter("at_v_in")
        s_done, mx_done = c.counter("at_s"), c.counter("at_mx")
        nh_done, nl_done = c.counter("at_nh"), c.counter("at_nl")
        tr_done, mt_done = c.counter("at_tr"), c.counter("at_mt")
        st_done, exp_done = c.counter("at_st"), c.counter("at_exp")
        av_done, out_done = c.counter("at_av"), c.counter("at_out")
        AL_STEPS = 10
        N_FILL = 2 * ITEMS // per_seq

        def seq_of(it, i):
            return it * n_seq + i // per_seq

        def ahead(step, it, i, last, *part):
            if i < ITEMS:
                step(it, i, *part)
            elif not last:
                step(it + 1, i - ITEMS, *part)

        def iterations(engine, body):
            with engine.Fori(0, N_ITER - 1) as it:
                body(it, False)
            body(N_ITER - 1, True)

        with nc.Block() as block:

            @block.sync
            def _(sp):
                if alibi:
                    sp.dma_start(slope[:, 0:1], io["slopes"]).then_inc(al_in.sem, 16)
                    sp.dma_start(pos[:, :], io["pos"].broadcast_to([16, SEQ])).then_inc(al_in.sem, 16)
                    sp.dma_start(maskf[:, :, :], io["masks"]).then_inc(al_in.sem, 16)
                    sp.wait_ge(al.sem, al.at(AL_STEPS))
                    sp.dma_start(c.scr_al.rearrange("k h q -> h k q"), sl[:, :, :]).then_inc(al_in.sem, 16)
                    sp.wait_ge(al_in.sem, al_in.at(64))
                    for i in range(0, ITEMS, per_seq):
                        slots = slice(i, i + per_seq)
                        for dst, first in ((qs, 0), (ks, 3)):
                            sp.dma_start(dst[rows:rows + 6, slots],
                                         c.scr_al[first:first + 6].rearrange("k (s h) q -> k s h q", s=per_seq))\
                                .then_inc(fill_in.sem, 16)
                with sp.Fori(0, N_ITER) as it:
                    for i in range(ITEMS):
                        n = it * ITEMS + i
                        toks = bass.ds(seq_of(it, i) * SEQ, SEQ)
                        hg = i % per_seq
                        sp.wait_ge(st_done.sem, st_done.at(2 * n + 2))
                        for dst, scr, heads in ((qs, scr_q, 4), (ks, scr_k, NK)):
                            sp.dma_start(dst[0:rows, i, :, :], scr[heads * hg:heads * (hg + 1), :, :, toks]
                                         .rearrange("h k d q -> (k d) h q")).then_inc(in_q[i].sem, 16)

            @block.gpsimd
            def _(pool):
                pool.memset(vs[:, :, :, :, :], 1.0).then_inc(filled.sem, 1)
                pool.memset(one8[:, :], 1.0).then_inc(filled.sem, 1)
                pool.wait_ge(filled.sem, filled.at(2))
                with pool.Fori(0, N_ITER) as it:
                    for i in range(ITEMS):
                        n = it * ITEMS + i
                        pool.wait_ge(av_done.sem, av_done.at(n + 1))
                        pool.wait_ge(filled.sem, filled.at(1))
                        hg = i % per_seq
                        pool.tensor_copy(vs[:, i, :, :, 0:hd],
                                         v[:, bass.ds(seq_of(it, i) * QT, QT), hg * NK * hd:(hg + 1) * NK * hd]
                                         .rearrange("p t (h d) -> p t h d", h=NK)).then_inc(v_in.sem, 1)
                        pool.wait_ge(mx_done.sem, mx_done.at(4 * n + 4))
                        pool.tensor_tensor(nms[:, i, 0, :], nm[:, i, :], one8[:, :], ALU.mult)\
                            .then_inc(nh_done.sem, 1)
                        pool.wait_ge(nh_done.sem, nh_done.at(n + 1))
                        pool.tensor_tensor(nms[:, i, 1, :], nm[:, i, :], nms[:, i, 0, :],
                                           ALU.subtract).then_inc(nl_done.sem, 1)

            @block.vector
            def _(dve):
                dve.sem_inc(st_done.sem, ST0)
                dve.sem_inc(av_done.sem, AV0)
                dve.sem_inc(out_done.sem, OUT0)
                if alibi:
                    dve.wait_ge(al_in.sem, al_in.at(48))
                    dve.tensor_copy(maskb[:, :, :], maskf[:, :, :]).then_inc(al.sem, 1)
                    dve.tensor_copy(sl[:, 3:6, :], pos[:, :].unsqueeze(1).broadcast_to([16, 3, SEQ]))\
                        .then_inc(al.sem, 1)
                    dve.tensor_scalar(slope[:, 1:2], slope[:, 0:1], 1.0 / scale, None, ALU.mult)\
                        .then_inc(al.sem, 1)
                    dve.wait_ge(al.sem, al.at(3))
                    dve.tensor_copy(wide[:, 0, :], slope[:, 1:2].broadcast_to([16, SEQ])).then_inc(al.sem, 1)
                    for k in range(3):
                        dve.wait_ge(al.sem, al.at(4 + 2 * k))
                        dve.tensor_copy(sl[:, k, :], wide[:, k, :]).then_inc(al.sem, 1)
                        if k < 2:
                            dve.wait_ge(al.sem, al.at(5 + 2 * k))
                            dve.tensor_tensor(wide[:, k + 1, :], wide[:, k, :], sl[:, k, :], ALU.subtract)\
                                .then_inc(al.sem, 1)
                    dve.wait_ge(al.sem, al.at(9))
                    dve.tensor_scalar(sl[:, 6:9, :], sl[:, 0:3, :], -1.0, None, ALU.mult).then_inc(al.sem, 1)

                def maximum(it, i, hh):
                    n = it * ITEMS + i
                    dve.wait_ge(s_done.sem, s_done.at(4 * n + hh + 1))
                    dve.tensor_reduce(nm[:, i, QT * hh:QT * hh + QT],
                                      c.ps[:, hh % 2, :].rearrange("p (t k) -> p t k", t=QT),
                                      AX.X, ALU.max, negate=True).then_inc(mx_done.sem, 1)

                def outputs(it, i):
                    n = it * ITEMS + i
                    dve.wait_ge(av_done.sem, av_done.at(AV0 + n + 1))
                    dve.tensor_scalar(av_all[:, i % per_seq, bass.ds(seq_of(it, i) * SEQ, SEQ)],
                                      c.ps[:, 6, 0:SEQ], 1.0, None, ALU.mult).then_inc(out_done.sem, 1)

                def body(it, last):
                    for i in range(ITEMS):
                        for hh in range(4):
                            ahead(maximum, it, i + LAG, last, hh)
                        outputs(it, i)

                dve.sem_inc(exp_done.sem, EX0)
                for i in range(LAG):
                    for hh in range(4):
                        maximum(0, i, hh)
                iterations(dve, body)

            @block.scalar
            def _(act):
                def max_rows(it, i):
                    n = it * ITEMS + i
                    act.wait_ge(tr_done.sem, tr_done.at(n + 1))
                    act.activation(mT[:, i, :], c.ps[0:MAXR, 7, 0:P], ACT.Copy)\
                        .then_inc(mt_done.sem, 1)
                    act.wait_ge(mt_done.sem, mt_done.at(n + 1))
                    act.dma_start(qs[s_rows:P, i, :, :], mT[:, i, :]).then_inc(m_in[i].sem, 16)

                def exponentials(it, i, kt):
                    n = it * ITEMS + i
                    act.wait_ge(av_done.sem, av_done.at(AV0 + n - 1))
                    act.wait_ge(st_done.sem, st_done.at(ST0 + 2 * n + kt + 1))
                    act.activation(pt[:, i % 2, kt, :],
                                   c.ps[:, 2 + 2 * kt:4 + 2 * kt, :].rearrange("p b n -> p (b n)"),
                                   ACT.Exp, scale=scale).then_inc(exp_done.sem, 1)

                def body(it, last):
                    for i in range(ITEMS):
                        ahead(exponentials, it, i + 1, last, 0)
                        ahead(max_rows, it, i + TLAG, last)
                        ahead(exponentials, it, i + 1, last, 1)

                for i in range(TLAG):
                    max_rows(0, i)
                for kt in range(QT):
                    exponentials(0, 0, kt)
                iterations(act, body)

            @block.tensor
            def _(pe):
                def is_first(it, i):
                    return isinstance(it, int) and it == 0 and i == 0

                def scores(it, i, hh):
                    n = it * ITEMS + i
                    kh = 0 if shared_k else hh
                    if hh == 0:
                        pe.wait_ge(in_q[i].sem, in_q[i].at((it + 1) * 32))
                    if not is_first(it, i) or hh > 1:
                        pe.wait_ge(mx_done.sem, mx_done.at(4 * n + hh - 1))
                    if alibi:
                        pe.matmul(c.ps[:, hh % 2, :], c.identb[:, :], maskb[:, 0, :],
                                  start=True, stop=False)
                    for qt in range(QT):
                        mm = pe.matmul(c.ps[:, hh % 2, qt * SEQ:(qt + 1) * SEQ],
                                       qs[0:s_rows, i, hh, qt * P:(qt + 1) * P], ks[0:s_rows, i, kh, :],
                                       start=not alibi, stop=not alibi or qt == QT - 1)
                    mm.then_inc(s_done.sem, 1)

                def max_transpose(it, i):
                    n = it * ITEMS + i
                    if not is_first(it, i):
                        pe.wait_ge(mt_done.sem, mt_done.at(n))
                    pe.wait_ge(nl_done.sem, nl_done.at(n + 1))
                    pe.matmul(c.ps[0:MAXR, 7, 0:P], nms[:, i, :, :].rearrange("p a b -> p (a b)"),
                              c.identb[:, :], start=True, stop=True).then_inc(tr_done.sem, 1)

                def scores_t(it, i, kt):
                    n = it * ITEMS + i
                    if kt == 0:
                        pe.wait_ge(m_in[i].sem, m_in[i].at((it + 1) * 16))
                    pe.wait_ge(exp_done.sem, exp_done.at(EX0 + 2 * n - 1 + kt))
                    for hh in range(0, 4, 2):
                        bank = 2 + 2 * kt + hh // 2
                        if alibi:
                            pe.matmul(c.ps[:, bank, :], c.identb[:, :], maskb[:, 1 + kt, :],
                                      start=True, stop=False)
                        if shared_k:
                            mm = pe.matmul(c.ps[:, bank, :], ks[:, i, 0, kt * P:(kt + 1) * P],
                                           qs[:, i, hh:hh + 2, :].rearrange("p h q -> p (h q)"),
                                           start=True, stop=True)
                        else:
                            for h in range(hh, hh + 2):
                                mm = pe.matmul(c.ps[:, bank, (h % 2) * SEQ:(h % 2 + 1) * SEQ],
                                               ks[:, i, h, kt * P:(kt + 1) * P], qs[:, i, h, :],
                                               start=not alibi, stop=not alibi or h % 2 == 1)
                    mm.then_inc(st_done.sem, 1)

                def product(it, i, kt):
                    n = it * ITEMS + i
                    if kt == 0:
                        pe.wait_ge(v_in.sem, v_in.at(n + 1))
                        pe.wait_ge(out_done.sem, out_done.at(OUT0 + n))
                    pe.wait_ge(exp_done.sem, exp_done.at(EX0 + 2 * n + kt + 1))
                    for hh in range(4):
                        mm = pe.matmul(c.ps[SCOLS * hh:SCOLS * (hh + 1), 6, 0:SEQ],
                                       vs[:, i, kt, 0 if shared_k else hh, :],
                                       pt[:, i % 2, kt, hh * SEQ:(hh + 1) * SEQ],
                                       start=(kt == 0), stop=(kt == QT - 1))
                    if kt == QT - 1:
                        mm.then_inc(av_done.sem, 1)

                if alibi:
                    pe.wait_ge(fill_in.sem, fill_in.at(16 * N_FILL))
                    pe.wait_ge(al.sem, al.at(1))
                for i in range(LAG):
                    for hh in range(4):
                        scores(0, i, hh)
                    if i >= LAG - TLAG:
                        max_transpose(0, i - (LAG - TLAG))
                for kt in range(QT):
                    scores_t(0, 0, kt)

                def body(it, last):
                    for i in range(ITEMS):
                        ahead(scores, it, i + LAG, last, 0)
                        ahead(scores_t, it, i + 1, last, 0)
                        ahead(scores, it, i + LAG, last, 1)
                        product(it, i, 0)
                        ahead(max_transpose, it, i + TLAG, last)
                        ahead(scores, it, i + LAG, last, 2)
                        product(it, i, 1)
                        ahead(scores, it, i + LAG, last, 3)
                        ahead(scores_t, it, i + 1, last, 1)

                iterations(pe, body)

        n_items = N_ITER * ITEMS
        filled.done(2)
        if alibi:
            fill_in.done(16 * N_FILL)
            al.done(AL_STEPS)
            al_in.done(64)
        for s in in_q:
            s.done(32 * N_ITER)
        for s in m_in:
            s.done(16 * N_ITER)
        for s in (v_in, nh_done, nl_done, tr_done, mt_done):
            s.done(n_items)
        s_done.done(4 * n_items)
        mx_done.done(4 * n_items)
        st_done.done(ST0 + 2 * n_items)
        exp_done.done(EX0 + 2 * n_items)
        av_done.done(AV0 + n_items)
        out_done.done(OUT0 + n_items)


def normalise_stage(c, st, name, groups, hd, av_all, wo, bias_io):
    nc, io = c.nc, c.io
    heads = 4 * groups
    nb = groups * P // BANK
    with ExitStack() as tmp:
        def sb(n, shape, dt=F32):
            return tmp.enter_context(nc.sbuf_tensor(f"{name}_{n}", shape, dt))

        rec = sb("rec", [P, TT, heads])
        on = sb("on", [P, TT, heads, hd])
        onT = sb("onT", [P, DT, TOK])
        bo = sb("bo", [P, DIM])
        bias_in, tr_done, rec_done, on_done = (c.counter("no_bias"), c.counter("no_tr"), c.counter("no_rec"),
                                               c.counter("no_on"))
        t2_done, onT_done, y_done, x_done = (c.counter("no_t2"), c.counter("no_onT"), c.counter("no_y"),
                                             c.counter("no_x"))
        xb_done = c.counter("no_xb")

        def out_view(t):
            b0 = nb * (t % 2)
            return c.ps[:, b0:b0 + nb, :].rearrange("p b (h s) -> p (b h) s", s=SCOLS)

        with nc.Block() as block:

            @block.tensor
            def _(pe):
                def second(t):
                    pe.wait_ge(on_done.sem, on_done.at(t + 1))
                    if t >= 2:
                        pe.wait_ge(onT_done.sem, onT_done.at(t - 1))
                    for dt in range(DT):
                        mm = pe.transpose(c.ps[:, 4 + t % 2, dt * P:(dt + 1) * P],
                                          on[:, t, :, :].rearrange("p h d -> p (h d)")[:, dt * P:(dt + 1) * P],
                                          c.ident[:, :])
                    mm.then_inc(t2_done.sem, 1)

                def project(t):
                    pe.wait_ge(onT_done.sem, onT_done.at(t + 1))
                    if t >= 2:
                        pe.wait_ge(x_done.sem, x_done.at(t - 1))
                    for dt in range(DT):
                        mm = pe.matmul(c.ps[:, 6 + t % 2, 0:DIM], onT[:, dt, t * P:(t + 1) * P],
                                       wo[:, dt, :], start=(dt == 0), stop=(dt == DT - 1))
                    mm.then_inc(y_done.sem, 1)

                for t in range(TT + 2):
                    if t < TT:
                        if t >= 2:
                            pe.wait_ge(on_done.sem, on_done.at(t - 1))
                        for g in range(groups):
                            mm = pe.transpose(c.ps[:, nb * (t % 2) + g // 4, (g % 4) * P:(g % 4 + 1) * P],
                                              av_all[:, g, t * P:(t + 1) * P], c.ident[:, :])
                        mm.then_inc(tr_done.sem, 1)
                    if wo is not None and 1 <= t <= TT:
                        second(t - 1)
                    if wo is not None and t >= 2:
                        project(t - 2)

            @block.vector
            def _(dve):
                def residual(t):
                    dve.wait_ge(y_done.sem, y_done.at(t + 1))
                    dve.tensor_tensor(c.x[:, t, :], c.ps[:, 6 + t % 2, 0:DIM], c.x[:, t, :], ALU.add)\
                        .then_inc(x_done.sem, 1)

                if wo is not None:
                    dve.wait_ge(xb_done.sem, xb_done.at(1))
                for t in range(TT):
                    dve.wait_ge(tr_done.sem, tr_done.at(t + 1))
                    dve.reciprocal(rec[:, t, :], out_view(t)[:, :, hd:hd + 1].squeeze(2)).then_inc(rec_done.sem, 1)
                    dve.wait_ge(rec_done.sem, rec_done.at(t + 1))
                    dve.tensor_tensor(on[:, t, :, :], out_view(t)[:, :, 0:hd],
                                      rec[:, t, :].unsqueeze(2).broadcast_to([P, heads, hd]), ALU.mult)\
                        .then_inc(on_done.sem, 1)
                    if wo is None:
                        dve.wait_ge(on_done.sem, on_done.at(t + 1))
                        dve.tensor_tensor(c.x[:, t, :], on[:, t, :, :].rearrange("p h d -> p (h d)"),
                                          c.x[:, t, :], ALU.add).then_inc(x_done.sem, 1)
                    elif t >= 2:
                        residual(t - 2)
                if wo is not None:
                    residual(TT - 2)
                    residual(TT - 1)

            if wo is not None:
                @block.sync
                def _(sp):
                    sp.dma_start(bo[:, :], io[bias_io][3:4, :].broadcast_to([P, DIM])).then_inc(bias_in.sem, 16)

                @block.gpsimd
                def _(pool):
                    pool.wait_ge(bias_in.sem, bias_in.at(16))
                    pool.tensor_tensor(c.x[:, :, :], c.x[:, :, :],
                                       bo[:, :].unsqueeze(1).broadcast_to([P, TT, DIM]), ALU.add)\
                        .then_inc(xb_done.sem, 1)

                @block.scalar
                def _(act):
                    for t in range(TT):
                        act.wait_ge(t2_done.sem, t2_done.at(t + 1))
                        act.activation(onT[:, :, t * P:(t + 1) * P],
                                       c.ps[:, 4 + t % 2, 0:DIM].rearrange("p (t n) -> p t n", t=DT),
                                       ACT.Copy).then_inc(onT_done.sem, 1)

        for s in (tr_done, rec_done, on_done, x_done):
            s.done(TT)
        if wo is not None:
            for s in (t2_done, onT_done, y_done):
                s.done(TT)
            bias_in.done(16)
            xb_done.done(1)


PAIRS = 8
HK, DCQ, R = 128, 192, 64


def context_stage(c, st):
    nc, io = c.nc, c.io
    kvr = st.enter_context(nc.sbuf_tensor("m_kvr", [P, TT, CTX], F32))
    kvT = st.enter_context(nc.sbuf_tensor("m_kvT", [P, TOK], F32))
    with ExitStack() as tmp:
        def sb(n, shape, dt=F32):
            return tmp.enter_context(nc.sbuf_tensor(f"mc_{n}", shape, dt))

        raw = sb("raw", [P, TT, CTX])
        rot = sb("rot", [P, TT, CTX])
        tab = sb("tab", [P, 2, QT, CTX])
        t1 = sb("t1", [P, TT, CTX])
        junk, ones = sb("junk", [P, DT * FFN]), sb("ones", [P, P])
        asum = sb("asum", [P, 3])
        summed, total, scales = c.counter("fw_sum"), c.counter("fw_total"), c.counter("fw_step")
        loaded, step, tr = c.counter("mc_in"), c.counter("mc_step"), c.counter("mc_tr")
        half = CTX // 2
        with nc.Block() as block:

            @block.sync
            def _(sp):
                src = io["ctx"].rearrange("(t p) d -> p t d", p=P)
                sp.dma_start(raw[:, :, :], src).then_inc(loaded.sem, 16)
                sp.dma_start(rot[:, :, 0:half], src[:, :, half:CTX]).then_inc(loaded.sem, 16)
                sp.dma_start(rot[:, :, half:CTX], src[:, :, 0:half]).then_inc(loaded.sem, 16)
                sp.dma_start(tab[:, :, :, :], io["rope_k"]).then_inc(loaded.sem, 16)

            @block.vector
            def _(dve):
                def by_seq(a):
                    return a.rearrange("p (b t) d -> p b (t d)", t=QT)

                def table(k):
                    return tab[:, k, :, :].rearrange("p t d -> p (t d)").unsqueeze(1)\
                        .broadcast_to([P, BATCH, QT * CTX])

                dve.memset(kvT[:, :], 0.0).then_inc(step.sem, 1)
                dve.wait_ge(loaded.sem, 64)
                dve.tensor_tensor(by_seq(t1[:, :, :]), by_seq(raw[:, :, :]), table(0), ALU.mult)\
                    .then_inc(step.sem, 1)
                dve.tensor_tensor(by_seq(rot[:, :, :]), by_seq(rot[:, :, :]), table(1), ALU.mult)\
                    .then_inc(step.sem, 1)
                dve.wait_ge(step.sem, 3)
                dve.tensor_tensor(kvr[:, :, :], t1[:, :, :], rot[:, :, :], ALU.add).then_inc(step.sem, 1)
                dve.wait_ge(tr.sem, 1)
                dve.tensor_copy(kvT[0:CTX, :], c.ps[0:CTX, 0:2, :].rearrange("p b n -> p (b n)"))\
                    .then_inc(step.sem, 1)
                dve.wait_ge(total.sem, 1)
                dve.tensor_scalar(c.fmean[:, :], c.ps[:, 3, 0:3], 1.0 / (FFN * DIM), QUANT_EPS, ALU.mult, ALU.max)\
                    .then_inc(scales.sem, 1)
                dve.wait_ge(scales.sem, 2)
                dve.reciprocal(c.finv[:, :], c.fmean[:, :]).then_inc(scales.sem, 1)
                dve.wait_ge(scales.sem, 3)
                dve.wait_ge(step.sem, 5)

            @block.gpsimd
            def _(pool):
                pool.memset(ones[:, :], 1.0).then_inc(scales.sem, 1)

            @block.scalar
            def _(act):
                for k in range(3):
                    act.wait_ge(c.fw_in[k].sem, 16)
                    if k:
                        act.wait_ge(summed.sem, k)
                    act.activation(junk[:, :], c.fw[:, k, :], ACT.Abs, accum_out=asum[:, k:k + 1])\
                        .then_inc(summed.sem, 1)

            @block.tensor
            def _(pe):
                pe.wait_ge(scales.sem, 1)
                pe.wait_ge(summed.sem, 3)
                pe.matmul(c.ps[:, 3, 0:3], ones[:, :], asum[:, :], start=True, stop=True).then_inc(total.sem, 1)
                pe.wait_ge(step.sem, 4)
                for t in range(TT):
                    mm = pe.transpose(c.ps[0:CTX, t // 4, (t % 4) * P:(t % 4 + 1) * P], kvr[:, t, :],
                                      c.ident[:, :])
                mm.then_inc(tr.sem, 1)
    return kvr, kvT


def mla_stages(c):
    nc, io = c.nc, c.io
    layer_norm(c, "ln2")
    with ExitStack() as st:
        kvr, kvT = context_stage(c, st)

        def sb(n, shape, dt=F32):
            return st.enter_context(nc.sbuf_tensor(f"m_{n}", shape, dt))

        ctxn = sb("ctxn", [P, PAIRS, TOK])
        nw = sb("nw", [P, PAIRS, DIM])
        with ExitStack() as tmp:
            mla_pairs(c, tmp, kvr, kvT, ctxn, nw)

        y_done, x_done = c.counter("mo_y"), c.counter("mo_x")
        with nc.Block() as block:

            @block.tensor
            def _(pe):
                for t in range(TT):
                    for p in range(PAIRS):
                        mm = pe.matmul(c.ps[:, t, 0:DIM], ctxn[:, p, t * P:(t + 1) * P], nw[:, p, :],
                                       start=(p == 0), stop=(p == PAIRS - 1))
                    mm.then_inc(y_done.sem, 1)

            @block.vector
            def _(dve):
                for t in range(TT):
                    dve.wait_ge(y_done.sem, t + 1)
                    dve.tensor_tensor(c.x[:, t, :], c.ps[:, t, 0:DIM], c.x[:, t, :], ALU.add)\
                        .then_inc(x_done.sem, 1)
                dve.wait_ge(x_done.sem, TT)


def mla_pairs(c, st, kvr, kvT, ctxn, nw):
    nc, io = c.nc, c.io

    def sb(n, shape, dt=F32):
        return st.enter_context(nc.sbuf_tensor(f"mp_{n}", shape, dt))

    wq2, wkq = sb("wq2", [P, 2, DIM]), sb("wkq", [P, 2, DCQ])
    wr = sb("wr", [P, 2, 3, 2 * R])
    wkr = sb("wkr", [P, 2 * R])
    wkv, wo = sb("wkv", [P, 2, CTX]), sb("wo", [P, 2, DIM])
    tab = sb("tab", [P, 2, 3, SEQ])
    mp = sb("mp", [P, DT, 2 * DCQ])
    qcs = sb("qcs", [P, HALF, 3, 2, BANK])
    qa = c.xn[:, :, :].rearrange("p (h t) d -> p h (t d)", h=2)
    ks = sb("ks", [P, 2, TOK])
    zero = sb("zero", [1, TOK])
    nm = sb("nm", [P, HALF, 2, BATCH // HALF, QT])
    MR = 2 * BATCH // HALF * QT
    mT = sb("mT", [MR, HALF, P])
    pt = sb("pt", [P, 2, 2, QT, SEQ])
    ones = sb("ones", [P, R])
    inv = sb("inv", [P, 2, SEQ])

    tab_in, prep, tern = c.counter("mp_tab"), c.counter("mp_prep"), c.counter("mp_tern")
    w_a, w_k, w_r, w_n = (c.counter("mp_wa"), c.counter("mp_wk"), c.counter("mp_wr"), c.counter("mp_wn"))
    kr, k_ev = c.counter("mp_kr"), c.counter("mp_k_ev")
    a_done, mp_done = c.counter("mp_a"), c.counter("mp_mp")
    qb, rope, qr = c.counter("mp_qb"), c.counter("mp_rope"), c.counter("mp_qr")
    q_ev, q_ev2, z_in = c.counter("mp_q_ev"), c.counter("mp_q_ev2"), c.counter("mp_z_in")
    m_in = [c.counter(f"mp_m_in{half}") for half in range(HALF)]
    s_done, mx = c.counter("mp_s"), c.counter("mp_mx")
    tr, mt = c.counter("mp_tr"), c.counter("mp_mt")
    n_done, nw_done = c.counter("mp_n"), c.counter("mp_nw")
    stt, ex, av = c.counter("mp_st"), c.counter("mp_ex"), c.counter("mp_av")
    inv_done, out = c.counter("mp_inv"), c.counter("mp_out")
    OUT0, Z0 = 2, 1
    TILE_ORDER = (1, 0, 2)
    QB_BANKS = (2, 3, 0, 1)
    S_BANKS = (0, 1, 0, 1, 2, 3, 0, 1)

    def rows(h):
        return slice(R * h, R * h + R)

    def m_row(h):
        return slice(R * (1 - h), R * (1 - h) + 1)

    def half_cols(half):
        return slice(half * BANK, (half + 1) * BANK)

    def pairs(engine, body):
        with engine.Fori(0, PAIRS - 1) as it:
            body(it, False)
        body(PAIRS - 1, True)

    with nc.Block() as block:

        @block.sync
        def _(sp):
            def load_k(p):
                sp.dma_start(wkr[:, :], io["m_wkr"][p]).then_inc(w_k.sem, 16)

            def load_a(p):
                sp.dma_start(wq2[:, :, :], io["m_wq"][p]).then_inc(w_a.sem, 16)
                sp.dma_start(wkq[:, :, :], io["m_wkq"][p]).then_inc(w_a.sem, 16)

            def load_r(p):
                sp.dma_start(wr[:, :, :, :], io["m_wr"][p]).then_inc(w_r.sem, 16)

            def load_n(p):
                sp.dma_start(wkv[:, :, :], io["m_wkv"][p]).then_inc(w_n.sem, 16)
                sp.dma_start(wo[:, :, :], io["m_wo"][p]).then_inc(w_n.sem, 16)

            load_k(0)
            load_a(0)
            sp.dma_start(tab[:, :, :, :], io["rope_q"]).then_inc(tab_in.sem, 16)
            load_r(0)
            load_n(0)
            with sp.Fori(1, PAIRS) as it:
                sp.wait_ge(kr.sem, it * 2)
                load_k(bass.ds(it, 1))
                sp.wait_ge(a_done.sem, it * 1)
                load_a(bass.ds(it, 1))
                sp.wait_ge(qr.sem, it * 2)
                load_r(bass.ds(it, 1))
                sp.wait_ge(n_done.sem, it * 1)
                load_n(bass.ds(it, 1))
                sp.wait_ge(stt.sem, it * 4)
                for h in range(2):
                    sp.dma_start(qa[m_row(h), h, :], zero[:, :]).then_inc(z_in.sem, 16)

        @block.gpsimd
        def _(pool):
            for tile, value in ((ks[:, :, :], 0.0), (qa[:, :, :], 0.0), (ones[:, :], 1.0), (zero[:, :], 0.0)):
                pool.memset(tile, value).then_inc(prep.sem, 1)
            pool.wait_ge(prep.sem, 4)
            for h in range(2):
                pool.memset(ks[m_row(h), h, :], 1.0).then_inc(prep.sem, 1)
            pool.wait_ge(prep.sem, 6)
            for k in range(3):
                w = c.fw[:, k, :]
                pool.tensor_scalar(w, w, c.finv[:, k:k + 1], ROUND, ALU.mult, ALU.add).then_inc(tern.sem, 1)
                pool.wait_ge(tern.sem, 3 * k + 1)
                pool.tensor_scalar(w, w, -ROUND, -1.0, ALU.add, ALU.max).then_inc(tern.sem, 1)
                pool.wait_ge(tern.sem, 3 * k + 2)
                pool.tensor_scalar(c.wb[:, k, :], w, 1.0, None, ALU.min).then_inc(tern.sem, 1)
            pool.wait_ge(tern.sem, 9)

        @block.vector
        def _(dve):
            def rotate(it, k):
                half, tile = k // 3, TILE_ORDER[k % 3]
                dve.wait_ge(qb.sem, it * 6 + (k + 1))
                for cs in range(2):
                    dve.tensor_tensor(
                        qcs[:, half, tile, cs, :].rearrange("p (b q) -> p b q", q=SEQ),
                        c.ps[:, QB_BANKS[k % 4], :].rearrange("p (b q) -> p b q", q=SEQ),
                        tab[:, cs, tile, :].unsqueeze(1).broadcast_to([P, 2, SEQ]), ALU.mult)\
                        .then_inc(rope.sem, 1)

            def queries(it, half):
                dve.wait_ge(qr.sem, it * 2 + (half + 1))
                dve.tensor_copy(qa[rows(1), 1, half_cols(half)], c.ps[rows(1), 4 + half, :])\
                    .then_inc(q_ev2.sem, 1)

            def maximum(it, k):
                b, h = k // 2, k % 2
                dve.wait_ge(s_done.sem, it * 8 + (k + 1))
                dve.tensor_reduce(nm[:, b // 2, h, b % 2, :],
                                  c.ps[:, S_BANKS[k], :].rearrange("p (t k) -> p t k", t=QT),
                                  AX.X, ALU.max, negate=True).then_inc(mx.sem, 1)

            def outputs(it, b):
                dve.wait_ge(av.sem, it * 4 + (b + 1))
                cols = slice(b * SEQ, (b + 1) * SEQ)
                dve.reciprocal(inv[:, b % 2, :], c.ps[:, 6 + b % 2, SEQ:2 * SEQ]).then_inc(inv_done.sem, 1)
                dve.wait_ge(inv_done.sem, it * 4 + (b + 1))
                dve.tensor_tensor(ctxn[:, bass.ds(it, 1), cols].squeeze(1), c.ps[:, 6 + b % 2, 0:SEQ],
                                  inv[:, b % 2, :], ALU.mult).then_inc(out.sem, 1)

            def body(it, last):
                for k in range(5):
                    rotate(it, k)
                queries(it, 0)
                rotate(it, 5)
                for k in range(4):
                    maximum(it, k)
                queries(it, 1)
                for k in range(4, 8):
                    maximum(it, k)
                dve.wait_ge(n_done.sem, it + 1)
                dve.tensor_scalar(nw[:, bass.ds(it, 1), :].squeeze(1), c.ps[:, 5, 0:DIM], 1.0, None, ALU.mult)\
                    .then_inc(nw_done.sem, 1)
                for b in range(BATCH):
                    outputs(it, b)

            dve.sem_inc(out.sem, OUT0)
            dve.sem_inc(z_in.sem, Z0)
            dve.wait_ge(tab_in.sem, 16)
            dve.wait_ge(prep.sem, 6)
            pairs(dve, body)

        @block.scalar
        def _(act):
            def keys(p):
                for half in range(HALF):
                    act.wait_ge(kr.sem, p * 2 + (half + 1))
                    for h in range(2):
                        act.activation(ks[rows(h), h, half_cols(half)], c.ps[rows(h), half, :], ACT.Copy)\
                            .then_inc(k_ev.sem, 1)

            def folded(p):
                act.wait_ge(a_done.sem, p + 1)
                act.activation(mp[:, :, :], c.ps[:, 0:2, 0:2 * DCQ], ACT.Copy).then_inc(mp_done.sem, 1)

            def queries(it, half):
                act.wait_ge(qr.sem, it * 2 + (half + 1))
                act.activation(qa[rows(0), 0, half_cols(half)], c.ps[rows(0), 4 + half, :], ACT.Copy)\
                    .then_inc(q_ev.sem, 1)

            def max_rows(it, half):
                act.wait_ge(tr.sem, it * 2 + (half + 1))
                act.activation(mT[:, half, :], c.ps[0:MR, 7, 0:P], ACT.Copy).then_inc(mt.sem, 1)
                act.wait_ge(mt.sem, it * 2 + (half + 1))
                for h in range(2):
                    act.dma_start(qa[m_row(h), h, half_cols(half)], mT[h * MR // 2:(h + 1) * MR // 2, half, :])\
                        .then_inc(m_in[half].sem, 16)

            def exponentials(it, b):
                act.wait_ge(stt.sem, it * 4 + (b + 1))
                if b >= 2:
                    act.wait_ge(av.sem, it * 4 + (b - 1))
                act.activation(pt[:, b % 2, :, :, :].rearrange("p h t q -> p (h t q)"),
                               c.ps[:, 2 + 2 * (b % 2):4 + 2 * (b % 2), :].rearrange("p b n -> p (b n)"),
                               ACT.Exp).then_inc(ex.sem, 1)

            def body(it, last):
                queries(it, 0)
                queries(it, 1)
                max_rows(it, 0)
                exponentials(it, 0)
                max_rows(it, 1)
                exponentials(it, 1)
                if not last:
                    folded(it + 1)
                exponentials(it, 2)
                exponentials(it, 3)
                if not last:
                    keys(it + 1)

            folded(0)
            act.wait_ge(prep.sem, 6)
            keys(0)
            pairs(act, body)

        @block.tensor
        def _(pe):
            def keys(p):
                pe.wait_ge(w_k.sem, p * 16 + 16)
                pe.wait_ge(mp_done.sem, p + 1)
                for half in range(HALF):
                    pe.matmul(c.ps[:, half, :], wkr[:, :], kvT[:, half_cols(half)],
                              start=True, stop=True).then_inc(kr.sem, 1)

            def fold(p):
                pe.wait_ge(w_a.sem, p * 32 + 32)
                for dt in range(DT):
                    for h in range(2):
                        mm = pe.matmul(c.ps[:, dt, h * DCQ:(h + 1) * DCQ], wq2[:, h, dt * P:(dt + 1) * P],
                                       wkq[:, h, :], start=True, stop=True)
                mm.then_inc(a_done.sem, 1)

            def packed(it, k):
                half, tile = k // 3, TILE_ORDER[k % 3]
                if k == 0:
                    pe.wait_ge(mp_done.sem, it + 1)
                if k == 2:
                    pe.wait_ge(k_ev.sem, it * 4 + 4)
                if k >= 4:
                    pe.wait_ge(rope.sem, it * 12 + 2 * (k - 3))
                for dt in range(DT):
                    mm = pe.matmul(c.ps[:, QB_BANKS[k % 4], :], mp[:, dt, tile * P:(tile + 1) * P],
                                   c.xnT[:, dt, half_cols(half)], start=(dt == 0), stop=(dt == DT - 1))
                mm.then_inc(qb.sem, 1)

            def scored_both(it, half):
                if half == 0:
                    pe.wait_ge(w_r.sem, it * 16 + 16)
                pe.wait_ge(rope.sem, it * 12 + (6 * half + 2))
                for cs in range(2):
                    pe.matmul(c.ps[:, 4 + half, :], wr[:, cs, 1, :], qcs[:, half, 1, cs, :],
                              start=(cs == 0), stop=False, skip_group_check=True)

            def scored_own(it, half):
                pe.wait_ge(rope.sem, it * 12 + (6 * half + 6))
                for cs in range(2):
                    for h, tile in ((0, 0), (1, 2)):
                        mm = pe.matmul(c.ps[rows(h), 4 + half, :], wr[:, cs, tile, rows(h)],
                                       qcs[:, half, tile, cs, :], start=False, stop=(cs == 1),
                                       skip_group_check=True)
                mm.then_inc(qr.sem, 1)

            def scores(it, k):
                b, h = k // 2, k % 2
                if k == 0:
                    pe.wait_ge(rope.sem, it * 12 + 8)
                    pe.wait_ge(z_in.sem, it * 32 + Z0)
                if k % 4 == 0:
                    pe.wait_ge(q_ev.sem, it * 2 + (k // 4 + 1))
                    pe.wait_ge(q_ev2.sem, it * 2 + (k // 4 + 1))
                if k in (2, 3):
                    pe.wait_ge(mx.sem, it * 8 + (k - 1))
                if k in (6, 7):
                    pe.wait_ge(mx.sem, it * 8 + (k - 3))
                for qt in range(QT):
                    q0 = b * SEQ + qt * P
                    mm = pe.matmul(c.ps[:, S_BANKS[k], qt * SEQ:(qt + 1) * SEQ], qa[:, h, q0:q0 + P],
                                   ks[:, h, b * SEQ:(b + 1) * SEQ], start=True, stop=True)
                mm.then_inc(s_done.sem, 1)

            def max_transpose(it, half):
                pe.wait_ge(mx.sem, it * 8 + 4 * (half + 1))
                if half == 0:
                    pe.wait_ge(out.sem, it * 4 + OUT0)
                else:
                    pe.wait_ge(mt.sem, it * 2 + 1)
                pe.transpose(c.ps[0:MR, 7, 0:P], nm[:, half, :, :, :].rearrange("p h b t -> p (h b t)"),
                             c.ident[:, :]).then_inc(tr.sem, 1)

            def output_weight(it):
                pe.wait_ge(w_n.sem, it * 32 + 32)
                for h in range(2):
                    mm = pe.matmul(c.ps[rows(h), 5, 0:DIM], wkv[:, h, :], wo[:, h, :], start=True, stop=True)
                mm.then_inc(n_done.sem, 1)

            def scores_t(it, b):
                if b % 2 == 0:
                    pe.wait_ge(m_in[b // 2].sem, it * 32 + 32)
                if b == 0:
                    pe.wait_ge(mx.sem, it * 8 + 6)
                if b == 1:
                    pe.wait_ge(nw_done.sem, it + 1)
                if b >= 2:
                    pe.wait_ge(ex.sem, it * 4 + (b - 1))
                for h in range(2):
                    for kt in range(QT):
                        mm = pe.matmul(c.ps[:, 2 + 2 * (b % 2) + h, kt * SEQ:(kt + 1) * SEQ],
                                       ks[:, h, b * SEQ + kt * P:b * SEQ + (kt + 1) * P],
                                       qa[:, h, b * SEQ:(b + 1) * SEQ], start=True, stop=True)
                mm.then_inc(stt.sem, 1)

            def product(it, b):
                pe.wait_ge(ex.sem, it * 4 + (b + 1))
                pe.wait_ge(out.sem, it * 4 + (OUT0 - 1 + b))
                if b == 1:
                    pe.wait_ge(mt.sem, it * 2 + 2)
                for part in range(2):
                    for kt in range(QT):
                        for h in range(2):
                            mm = pe.matmul(c.ps[rows(h), 6 + b % 2, part * SEQ:(part + 1) * SEQ],
                                           (kvr[:, b * QT + kt, :], ones[:, :])[part], pt[:, b % 2, h, kt, :],
                                           start=(kt == 0), stop=(kt == QT - 1))
                mm.then_inc(av.sem, 1)

            def body(it, last):
                for k in range(4):
                    packed(it, k)
                scored_both(it, 0)
                packed(it, 4)
                scored_own(it, 0)
                packed(it, 5)
                for k in range(4):
                    scores(it, k)
                scored_both(it, 1)
                scored_own(it, 1)
                max_transpose(it, 0)
                for k in range(4, 8):
                    scores(it, k)
                output_weight(it)
                scores_t(it, 0)
                max_transpose(it, 1)
                scores_t(it, 1)
                product(it, 0)
                if not last:
                    fold(it + 1)
                scores_t(it, 2)
                product(it, 1)
                scores_t(it, 3)
                if not last:
                    keys(it + 1)
                product(it, 2)
                product(it, 3)

            pe.wait_ge(prep.sem, 6)
            fold(0)
            keys(0)
            pairs(pe, body)


FT = FFN // P


def quantise(dve, tile, scale, out, sig, first, n):
    dve.tensor_scalar(tile, tile, scale, INT8_MAX, ALU.mult, ALU.min).then_inc(sig.sem, 1)
    dve.wait_ge(sig.sem, first + 1)
    dve.tensor_scalar(tile, tile, INT8_MIN, ROUND, ALU.max, ALU.add).then_inc(sig.sem, 1)
    dve.wait_ge(sig.sem, first + 2)
    dve.tensor_scalar(out, tile, -ROUND, None, ALU.add).then_inc(sig.sem, 1)


def ffn_stages(c):
    nc, io = c.nc, c.io
    with ExitStack() as st:
        wb, mean = c.wb, c.fmean
        layer_norm(c, "ln3", want_t=False)

        def sb(n, shape, dt=F32):
            return st.enter_context(nc.sbuf_tensor(f"f_{n}", shape, dt))

        amax, qsc = sb("amax", [P, TT]), sb("qsc", [P, TT])
        deq = sb("deq", [P, 2, TT])
        xq = sb("xq", [P, TT, DIM], BF16)
        xqT = sb("xqT", [P, DT, TOK], BF16)
        h = sb("h", [P, TT, FFN])
        sg = sb("sg", [P, 2, FFN])
        a_s, q_s, tr, ev = c.counter("f_a"), c.counter("f_q"), c.counter("f_tr"), c.counter("f_ev")
        gu, silu, hd = c.counter("f_gu"), c.counter("f_silu"), c.counter("f_h")
        sq = c.counter("f_sq")
        ssq = sb("ssq", [P, TT])
        junk = sb("junk", [P, FFN])

        def bank16(k):
            return c.ps[:, k, :].bitcast(BF16)

        with nc.Block() as block:

            @block.vector
            def _(dve):
                dve.tensor_reduce(amax[:, :], c.xn[:, :, :], AX.X, ALU.max, apply_absolute_value=True)\
                    .then_inc(a_s.sem, 1)
                dve.wait_ge(a_s.sem, 1)
                dve.tensor_scalar(amax[:, :], amax[:, :], QUANT_EPS, None, ALU.max).then_inc(a_s.sem, 1)
                dve.wait_ge(a_s.sem, 2)
                dve.reciprocal(qsc[:, :], amax[:, :]).then_inc(a_s.sem, 1)
                dve.wait_ge(a_s.sem, 3)
                dve.tensor_scalar(qsc[:, :], qsc[:, :], INT8_MAX, None, ALU.mult).then_inc(a_s.sem, 1)
                for k in range(2):
                    dve.tensor_scalar(deq[:, k, :], amax[:, :], mean[:, k:k + 1], 1.0 / INT8_MAX,
                                      ALU.mult, ALU.mult).then_inc(a_s.sem, 1)
                dve.wait_ge(a_s.sem, 6)
                for t in range(TT):
                    dve.tensor_scalar(c.xn[:, t, :], c.xn[:, t, :], qsc[:, t:t + 1], INT8_MAX, ALU.mult, ALU.min)\
                        .then_inc(q_s.sem, 1)
                for g in range(HALF):
                    some = slice(g * TT // 2, (g + 1) * TT // 2)
                    dve.wait_ge(q_s.sem, 2 * g + TT)
                    dve.tensor_scalar(c.xn[:, some, :], c.xn[:, some, :], INT8_MIN, ROUND, ALU.max, ALU.add)\
                        .then_inc(q_s.sem, 1)
                    dve.wait_ge(q_s.sem, 2 * g + TT + 1)
                    dve.tensor_scalar(xq[:, some, :], c.xn[:, some, :], -ROUND, None, ALU.add).then_inc(q_s.sem, 1)
                for t in range(TT):
                    dve.wait_ge(silu.sem, t + 1)
                    b = 4 * (t % 2) + 2
                    dve.scalar_tensor_tensor(h[:, t, :], c.ps[:, b:b + 2, :].rearrange("p b n -> p (b n)"),
                                             deq[:, 1, t:t + 1], sg[:, t % 2, :], ALU.mult, ALU.mult)\
                        .then_inc(hd.sem, 1)

            @block.tensor
            def _(pe):
                for t in range(TT):
                    if t % (TT // 2) == 0:
                        pe.wait_ge(q_s.sem, TT + 2 + 2 * (t // (TT // 2)))
                    for dt in range(DT):
                        mm = pe.transpose(bank16(dt)[:, t * P:(t + 1) * P], xq[:, t, dt * P:(dt + 1) * P],
                                          c.identb[:, :])
                mm.then_inc(tr.sem, 1)
                pe.wait_ge(ev.sem, 2)
                for t in range(TT):
                    if t >= 2:
                        pe.wait_ge(hd.sem, t - 1)
                    for k in range(2):
                        for n in range(FFN // BANK):
                            for dt in range(DT):
                                mm = pe.matmul(c.ps[:, 4 * (t % 2) + 2 * k + n, :], xqT[:, dt, t * P:(t + 1) * P],
                                               wb[:, k, dt * FFN + n * BANK:dt * FFN + (n + 1) * BANK],
                                               start=(dt == 0), stop=(dt == DT - 1))
                    mm.then_inc(gu.sem, 1)

            def square(act, t):
                act.wait_ge(hd.sem, t + 1)
                if t:
                    act.wait_ge(sq.sem, t)
                act.activation(junk[:, :], h[:, t, :], ACT.Square, accum_out=ssq[:, t:t + 1]).then_inc(sq.sem, 1)

            @block.scalar
            def _(act):
                act.wait_ge(tr.sem, 1)
                for dt in range(DT):
                    act.activation(xqT[:, dt, :], bank16(dt), ACT.Copy).then_inc(ev.sem, 1)
                for t in range(TT):
                    act.wait_ge(gu.sem, t + 1)
                    if t >= 2:
                        act.wait_ge(hd.sem, t - 1)
                    b = 4 * (t % 2)
                    act.activation(sg[:, t % 2, :], c.ps[:, b:b + 2, :].rearrange("p b n -> p (b n)"),
                                   ACT.Silu, scale=deq[:, 0, t:t + 1]).then_inc(silu.sem, 1)
                    if t >= 1:
                        square(act, t - 1)
                square(act, TT - 1)

        with ExitStack() as tmp:
            def sb2(n, shape, dt=F32):
                return tmp.enter_context(nc.sbuf_tensor(f"f2_{n}", shape, dt))

            lnw = sb2("lnw", [P, FFN])
            rstd = sb2("rstd", [P, TT])
            am, qs2 = sb2("am", [P, TT]), sb2("qs2", [P, TT])
            dd = sb2("dd", [P, TT])
            hq = sb2("hq", [P, 2, FFN], BF16)
            hqT = sb2("hqT", [P, 2, FT, P], BF16)
            lnw_in, r_s, std_s = c.counter("f2_in"), c.counter("f2_r"), c.counter("f2_std")
            v_s, n_s, m_s, k_s = c.counter("f2_v"), c.counter("f2_n"), c.counter("f2_m"), c.counter("f2_k")
            q2, tr2, ev2, y_s, x_s = (c.counter("f2_q"), c.counter("f2_tr"), c.counter("f2_ev"),
                                      c.counter("f2_y"), c.counter("f2_x"))
            with nc.Block() as block:

                @block.sync
                def _(sp):
                    sp.dma_start(lnw[:, :], io["f_ln"].broadcast_to([P, FFN])).then_inc(lnw_in.sem, 16)

                @block.scalar
                def _(act):
                    act.wait_ge(r_s.sem, 1)
                    act.activation(rstd[:, :], rstd[:, :], ACT.Sqrt).then_inc(std_s.sem, 1)

                    def normalise(t):
                        act.activation(h[:, t, :], h[:, t, :], ACT.Copy, scale=rstd[:, t:t + 1]).then_inc(v_s.sem, 1)

                    act.wait_ge(r_s.sem, 2)
                    for t in range(3):
                        normalise(t)
                    for t in range(TT):
                        act.wait_ge(tr2.sem, t + 1)
                        if t >= 2:
                            act.wait_ge(y_s.sem, t - 1)
                        act.activation(hqT[:, t % 2, :, :].rearrange("p f n -> p (f n)"), bank16(t % 2), ACT.Copy)\
                            .then_inc(ev2.sem, 1)
                        if t + 3 < TT:
                            normalise(t + 3)

                @block.gpsimd
                def _(pool):
                    pool.wait_ge(lnw_in.sem, 16)
                    for t in range(TT):
                        pool.wait_ge(v_s.sem, t + 1)
                        pool.tensor_tensor(h[:, t, :], h[:, t, :], lnw[:, :], ALU.mult).then_inc(n_s.sem, 1)

                @block.vector
                def _(dve):
                    dve.tensor_scalar(rstd[:, :], ssq[:, :], 1.0 / FFN, RMS_EPS, ALU.mult, ALU.add)\
                        .then_inc(r_s.sem, 1)
                    dve.wait_ge(std_s.sem, 1)
                    dve.reciprocal(rstd[:, :], rstd[:, :]).then_inc(r_s.sem, 1)

                    def residual(t):
                        dve.wait_ge(y_s.sem, t + 1)
                        dve.scalar_tensor_tensor(c.x[:, t, :], c.ps[:, 2 + t % 2, 0:DIM], dd[:, t:t + 1],
                                                 c.x[:, t, :], ALU.mult, ALU.add).then_inc(x_s.sem, 1)

                    for t in range(TT):
                        one = slice(t, t + 1)
                        dve.wait_ge(n_s.sem, t + 1)
                        dve.tensor_reduce(am[:, one], h[:, t, :], AX.X, ALU.max, apply_absolute_value=True)\
                            .then_inc(m_s.sem, 1)
                        dve.wait_ge(m_s.sem, t + 1)
                        dve.tensor_scalar(am[:, one], am[:, one], QUANT_EPS, None, ALU.max).then_inc(k_s.sem, 1)
                        dve.wait_ge(k_s.sem, 4 * t + 1)
                        dve.reciprocal(qs2[:, one], am[:, one]).then_inc(k_s.sem, 1)
                        dve.tensor_scalar(dd[:, one], am[:, one], mean[:, 2:3], 1.0 / INT8_MAX, ALU.mult, ALU.mult)\
                            .then_inc(k_s.sem, 1)
                        dve.wait_ge(k_s.sem, 4 * t + 2)
                        dve.tensor_scalar(qs2[:, one], qs2[:, one], INT8_MAX, None, ALU.mult).then_inc(k_s.sem, 1)
                        dve.wait_ge(k_s.sem, 4 * t + 4)
                        if t >= 2:
                            dve.wait_ge(tr2.sem, t - 1)
                        quantise(dve, h[:, t, :], qs2[:, one], hq[:, t % 2, :], q2, 3 * t, TT)
                        if t >= 1:
                            residual(t - 1)
                    residual(TT - 1)
                    dve.wait_ge(x_s.sem, TT)

                @block.tensor
                def _(pe):
                    for t in range(TT + 1):
                        if t >= 1:
                            u = t - 1
                            pe.wait_ge(ev2.sem, u + 1)
                            if u >= 2:
                                pe.wait_ge(x_s.sem, u - 1)
                            for f in range(FT):
                                mm = pe.matmul(c.ps[:, 2 + u % 2, 0:DIM], hqT[:, u % 2, f, :],
                                               wb[:, 2, f * DIM:(f + 1) * DIM],
                                               start=(f == 0), stop=(f == FT - 1))
                            mm.then_inc(y_s.sem, 1)
                        if t < TT:
                            pe.wait_ge(q2.sem, 3 * t + 3)
                            if t >= 2:
                                pe.wait_ge(ev2.sem, t - 1)
                            for f in range(FT):
                                mm = pe.transpose(bank16(t % 2)[:, f * P:(f + 1) * P],
                                                  hq[:, t % 2, f * P:(f + 1) * P], c.identb[:, :])
                            mm.then_inc(tr2.sem, 1)


def layer1_attentions(c, stages):
    nc, io = c.nc, c.io
    with ExitStack() as st:
        with ExitStack() as own:
            w = own.enter_context(nc.sbuf_tensor("a1_w", [P, 4, DT, DIM], F32))
            w_in = c.counter("a1_w_in")
            with nc.Block() as block:

                @block.sync
                def _(sp):
                    for k in range(4):
                        sp.dma_start(w[:, k, :, :], io["L1_WT"][k].rearrange("(t p) o -> p t o", p=P))\
                            .then_inc(w_in.sem, 16)
                    sp.wait_ge(w_in.sem, 64)
            layer_norm(c, "ln4")
            v = qkv_stage(c, own, "a1", w[:, 0], w[:, 1], w[:, 2], "L1_bias", c.scr_q, c.scr_k)
            av = own.enter_context(nc.sbuf_tensor("a1_av", [P, 4, TOK], F32))
            attention_stage(c, "a1", 16, False, 0.25, v, c.scr_q, c.scr_k, av, alibi=True)
            normalise_stage(c, own, "a1n", 4, 16, av, w[:, 3], "L1_bias")
        if stages < 5:
            return
        layer_norm(c, "ln5")
        with ExitStack() as own:
            v = own.enter_context(nc.sbuf_tensor("x1_v", [P, TT, CTX], F32))
            split_context(c, v)
            av = own.enter_context(nc.sbuf_tensor("x1_av", [P, 8, TOK], F32))
            attention_stage(c, "x1", 8, True, 8.0 ** -0.5, v, c.scr_xq, c.scr_xk, av)
            normalise_stage(c, own, "x1n", 8, 8, av, None, None)


def split_context(c, v):
    nc, io = c.nc, c.io
    with ExitStack() as tmp:
        def sb(n, shape, dt=F32):
            return tmp.enter_context(nc.sbuf_tensor(f"xs_{n}", shape, dt))

        qp = sb("qp", [P, DT, 3, TOK], BF16)
        kp = sb("kp", [CTX, 3, TOK], BF16)
        qrest, krest = sb("qrest", [P, DT, TOK]), sb("krest", [CTX, TOK])
        v_in, tr, k_s, qh, q_r, q_m, ql, stored, cleared = (
            c.counter("xs_v"), c.counter("xs_tr"), c.counter("xs_k"), c.counter("xs_qh"), c.counter("xs_qr"),
            c.counter("xs_qm"), c.counter("xs_ql"), c.counter("xs_st"), c.counter("xs_cleared"))
        kps = c.ps[0:CTX, 0:2, :].rearrange("p b n -> p (b n)")
        with nc.Block() as block:

            @block.sync
            def _(sp):
                sp.dma_start(v[:, :, :], io["ctx"].rearrange("(t p) d -> p t d", p=P)).then_inc(v_in.sem, 16)
                for dt in range(DT):
                    sp.wait_ge(ql.sem, dt + 1)
                    store_stack(sp, 0, c.scr_xq[16 * dt:16 * dt + 16], qp[:, dt, :, :], stored)
                sp.wait_ge(k_s.sem, 4)
                store_stack(sp, 1, c.scr_xk, kp[:, :, :], stored)
                sp.wait_ge(stored.sem, 16 * TERMS * (DT + 1))

            @block.gpsimd
            def _(pool):
                for k, (tile, first) in enumerate(((c.qs[:, :, :, :], 0), (c.ks[:, :, 0:1, :], 0),
                                                   (c.qs[:, :, :, :], 96), (c.ks[:, :, 0:1, :], 96))):
                    rows = slice(0, 96) if first == 0 else slice(96, P - 2)
                    pool.memset(tile[rows].bitcast(F32), 0.0).then_inc(cleared.sem, 1)
                    pool.wait_ge(cleared.sem, k + 1)

            @block.tensor
            def _(pe):
                pe.wait_ge(v_in.sem, 16)
                for t in range(TT):
                    mm = pe.transpose(c.ps[0:CTX, t // 4, (t % 4) * P:(t % 4 + 1) * P], v[:, t, :],
                                      c.ident[:, :])
                mm.then_inc(tr.sem, 1)

            @block.scalar
            def _(act):
                for dt in range(DT):
                    act.activation(qp[:, dt, 0, :], c.xnT[:, dt, :], ACT.Copy).then_inc(qh.sem, 1)
                act.wait_ge(tr.sem, 1)
                act.activation(kp[:, 0, :], kps, ACT.Copy).then_inc(k_s.sem, 1)
                for dt in range(DT):
                    act.wait_ge(q_r.sem, dt + 1)
                    act.activation(qp[:, dt, 1, :], qrest[:, dt, :], ACT.Copy).then_inc(q_m.sem, 1)
                act.wait_ge(k_s.sem, 2)
                act.activation(kp[:, 1, :], krest[:, :], ACT.Copy).then_inc(k_s.sem, 1)

            @block.vector
            def _(dve):
                for dt in range(DT):
                    dve.wait_ge(qh.sem, dt + 1)
                    dve.tensor_tensor(qrest[:, dt, :], c.xnT[:, dt, :], qp[:, dt, 0, :], ALU.subtract)\
                        .then_inc(q_r.sem, 1)
                dve.wait_ge(k_s.sem, 1)
                dve.tensor_tensor(krest[:, :], kps, kp[:, 0, :], ALU.subtract).then_inc(k_s.sem, 1)
                for dt in range(DT):
                    dve.wait_ge(q_m.sem, dt + 1)
                    dve.tensor_tensor(qp[:, dt, 2, :], qrest[:, dt, :], qp[:, dt, 1, :], ALU.subtract)\
                        .then_inc(ql.sem, 1)
                dve.wait_ge(k_s.sem, 3)
                dve.tensor_tensor(kp[:, 2, :], krest[:, :], kp[:, 1, :], ALU.subtract).then_inc(k_s.sem, 1)


def moe_stages(c):
    nc, io = c.nc, c.io
    layer_norm(c, "ln6")
    NX = EXPERTS + 1
    with ExitStack() as st:
        def sb(n, shape, dt=F32):
            return st.enter_context(nc.sbuf_tensor(f"x_{n}", shape, dt))

        gw = sb("gw", [P, DT, EXPERTS])
        iota = sb("iota", [P, EXPERTS])
        score = sb("score", [P, TT, EXPERTS])
        best = sb("best", [P, TT, 8])
        bidx = sb("bidx", [P, TT, 8], U32)
        bidf = sb("bidf", [P, TT, TOPK])
        hit = sb("hit", [P, TOPK, TT, EXPERTS])
        gate = sb("gate", [P, TT, NX])
        gT = sb("gT", [NX, TOK])
        g_in, logit, sc = c.counter("x_gate_in"), c.counter("x_logit"), c.counter("x_score")
        mxs, ids, st_s = c.counter("x_max"), c.counter("x_ids"), c.counter("x_step")
        gtr, gev, gst = c.counter("x_gtr"), c.counter("x_gev"), c.counter("x_gst")

        with nc.Block() as block:

            @block.sync
            def _(sp):
                sp.dma_start(gw[:, :, :], io["gate_wT"].rearrange("(t p) e -> p t e", p=P)).then_inc(g_in.sem, 16)
                sp.dma_start(iota[:, :], io["iota"].broadcast_to([P, EXPERTS])).then_inc(g_in.sem, 16)
                sp.wait_ge(gev.sem, 1)
                sp.dma_start(c.scr_g, gT[:, :]).then_inc(gst.sem, 16)
                sp.wait_ge(gst.sem, 16)

            @block.tensor
            def _(pe):
                pe.wait_ge(g_in.sem, 32)
                for t in range(TT):
                    for dt in range(DT):
                        mm = pe.matmul(c.ps[:, 0, t * EXPERTS:(t + 1) * EXPERTS], c.xnT[:, dt, t * P:(t + 1) * P],
                                       gw[:, dt, :], start=(dt == 0), stop=(dt == DT - 1))
                mm.then_inc(logit.sem, 1)
                pe.wait_ge(st_s.sem, 7)
                for t in range(TT):
                    mm = pe.transpose(c.ps[0:NX, 1 + t // 4, (t % 4) * P:(t % 4 + 1) * P], gate[:, t, :],
                                      c.ident[:, :])
                mm.then_inc(gtr.sem, 1)

            @block.scalar
            def _(act):
                act.wait_ge(logit.sem, 1)
                act.activation(score[:, :, :].rearrange("p t e -> p (t e)"), c.ps[:, 0, 0:TT * EXPERTS],
                               ACT.Sigmoid).then_inc(sc.sem, 1)
                act.wait_ge(gtr.sem, 1)
                act.activation(gT[:, :], c.ps[0:NX, 1:3, :].rearrange("p b n -> p (b n)"), ACT.Copy)\
                    .then_inc(gev.sem, 1)

            @block.vector
            def _(dve):
                dve.memset(gate[:, :, :], 1.0).then_inc(st_s.sem, 1)
                dve.wait_ge(sc.sem, 1)
                for t in range(TT):
                    dve.max(best[:, t, :], score[:, t, :]).then_inc(mxs.sem, 1)
                for t in range(TT):
                    dve.wait_ge(mxs.sem, t + 1)
                    dve.max_index(bidx[:, t, :], best[:, t, :], score[:, t, :]).then_inc(ids.sem, 1)
                dve.wait_ge(ids.sem, TT)
                dve.tensor_copy(bidf[:, :, :], bidx[:, :, 0:TOPK]).then_inc(st_s.sem, 1)
                dve.wait_ge(st_s.sem, 2)
                for k in range(TOPK):
                    dve.tensor_tensor(hit[:, k, :, :], iota[:, :].unsqueeze(1).broadcast_to([P, TT, EXPERTS]),
                                      bidf[:, :, k:k + 1].broadcast_to([P, TT, EXPERTS]), ALU.is_equal)\
                        .then_inc(st_s.sem, 1)
                for k in range(TOPK):
                    dve.wait_ge(st_s.sem, 3 + k)
                    dve.tensor_tensor(hit[:, k, :, :], hit[:, k, :, :],
                                      best[:, :, k:k + 1].broadcast_to([P, TT, EXPERTS]), ALU.mult)\
                        .then_inc(st_s.sem, 1)
                dve.wait_ge(st_s.sem, 6)
                dve.tensor_tensor(gate[:, :, 0:EXPERTS], hit[:, 0, :, :], hit[:, 1, :, :], ALU.add)\
                    .then_inc(st_s.sem, 1)

        BUF = 3
        w13 = sb("w13", [P, BUF, 2, DT, EH])
        w2 = sb("w2", [P, BUF, DIM])
        gb = sb("gb", [P, BUF, TOK])
        h1g = sb("h1g", [P, 2, BANK])
        sg = sb("sg", [P, 2, BANK])
        h3 = sb("h3", [P, 2, BANK])
        hT = sb("hT", [P, 2, BANK])
        w_in = [c.counter(f"e_in{b}") for b in range(BUF)]
        p13, gm, sl, m3, hd = c.counter("e_p13"), c.counter("e_gm"), c.counter("e_silu"), c.counter("e_m3"), c.counter("e_h")
        down, seeded, x_s = c.counter("e_down"), c.counter("e_seed"), c.counter("e_x")
        D0 = 2 * BUF
        with nc.Block() as block:

            @block.sync
            def _(sp):
                with sp.Fori(0, NX // BUF) as it:
                    for b in range(BUF):
                        e = it * BUF + b
                        sp.wait_ge(down.sem, e * 2 + 2)
                        one = bass.ds(e, 1)
                        sp.dma_start(w13[:, b], io["e_w13"][one]).then_inc(w_in[b].sem, 16)
                        sp.dma_start(w2[:, b], io["e_w2"][one]).then_inc(w_in[b].sem, 16)
                        sp.dma_start(gb[:, b], c.scr_g[one, :].broadcast_to([P, TOK])).then_inc(w_in[b].sem, 16)

            @block.vector
            def _(dve):
                dve.sem_inc(down.sem, D0)
                with dve.Fori(0, NX // BUF) as it:
                    for k in range(2 * BUF):
                        b, half = k // 2, k % 2
                        n = it * (2 * BUF) + k
                        cols = slice(half * BANK, (half + 1) * BANK)
                        dve.wait_ge(w_in[b].sem, it * 48 + 48)
                        dve.wait_ge(p13.sem, n * 2 + 1)
                        dve.tensor_tensor(h1g[:, half, :], c.ps[:, 4 + half, :], gb[:, b, cols], ALU.mult)\
                            .then_inc(gm.sem, 1)
                        dve.wait_ge(sl.sem, n + 1)
                        dve.wait_ge(p13.sem, n * 2 + 2)
                        dve.tensor_tensor(h3[:, half, :], c.ps[:, 6 + half, :], sg[:, half, :], ALU.mult)\
                            .then_inc(m3.sem, 1)
                for t in range(TT):
                    if t == 0:
                        dve.wait_ge(down.sem, D0 + 2 * NX)
                    dve.tensor_copy(c.x[:, t, :], c.ps[:, t // 2, (t % 2) * DIM:(t % 2 + 1) * DIM])\
                        .then_inc(x_s.sem, 1)
                dve.wait_ge(x_s.sem, TT)

            @block.scalar
            def _(act):
                with act.Fori(0, NX // BUF) as it:
                    for k in range(2 * BUF):
                        n = it * (2 * BUF) + k
                        act.wait_ge(gm.sem, n + 1)
                        act.activation(sg[:, k % 2, :], h1g[:, k % 2, :], ACT.Silu).then_inc(sl.sem, 1)

            @block.gpsimd
            def _(pool):
                with pool.Fori(0, NX // BUF) as it:
                    for k in range(2 * BUF):
                        b, half = k // 2, k % 2
                        n = it * (2 * BUF) + k
                        cols = slice(half * BANK, (half + 1) * BANK)
                        pool.wait_ge(down.sem, n + (D0 - 1))
                        pool.wait_ge(m3.sem, n + 1)
                        pool.tensor_tensor(hT[:, half, :], h3[:, half, :], gb[:, b, cols], ALU.mult)\
                            .then_inc(hd.sem, 1)

            @block.tensor
            def _(pe):
                for k in range(TT // 2):
                    pe.matmul(c.ps[:, k, :], c.ident[:, :], c.x[:, 2 * k:2 * k + 2, :].rearrange("p t d -> p (t d)"),
                              start=True, stop=True)

                def up(it, k):
                    b, half = k // 2, k % 2
                    n = it * (2 * BUF) + k
                    if half == 0:
                        pe.wait_ge(w_in[b].sem, it * 48 + 48)
                    if k >= 2:
                        pe.wait_ge(m3.sem, n - 1)
                    for j in range(2):
                        for dt in range(DT):
                            mm = pe.matmul(c.ps[:, 4 + 2 * j + half, :], w13[:, b, j, dt, :],
                                           c.xnT[:, dt, half * BANK:(half + 1) * BANK],
                                           start=(dt == 0), stop=(dt == DT - 1))
                        mm.then_inc(p13.sem, 1)

                def add(it, k):
                    b, half = k // 2, k % 2
                    n = it * (2 * BUF) + k
                    pe.wait_ge(hd.sem, n + 1)
                    for j in range(4):
                        t = 4 * half + j
                        mm = pe.matmul(c.ps[:, t // 2, (t % 2) * DIM:(t % 2 + 1) * DIM],
                                       hT[:, half, j * P:(j + 1) * P], w2[:, b, :],
                                       start=False, stop=True, skip_group_check=True)
                    mm.then_inc(down.sem, 1)

                with pe.Fori(0, NX // BUF) as it:
                    for k in range(2 * BUF + 1):
                        if k < 2 * BUF:
                            up(it, k)
                        if k >= 1:
                            add(it, k - 1)


def store_stage(c, out):
    nc = c.nc
    stored = c.counter("stored")
    with nc.Block() as block:

        @block.sync
        def _(sp):
            sp.dma_start(out.rearrange("(t p) d -> p t d", p=P), c.x[:, :, :]).then_inc(stored.sem, 16)
            sp.wait_ge(stored.sem, 16)


STAGES = 6


def build_program(nc, io, out):
    with ExitStack() as ctx:
        c = Chip(nc, ctx, io)
        load_stage(c)
        c.xn = c.sbuf("xn", [P, TT, DIM])
        c.scr_q = nc.dram_tensor("scr_q", (16, TERMS, 16, TOK), BF16, kind="Internal").ap()
        c.scr_k = nc.dram_tensor("scr_k", (16, TERMS, 16, TOK), BF16, kind="Internal").ap()
        c.scr_xq = nc.dram_tensor("scr_xq", (32, TERMS, 8, TOK), BF16, kind="Internal").ap()
        c.scr_xk = nc.dram_tensor("scr_xk", (8, TERMS, 8, TOK), BF16, kind="Internal").ap()
        c.scr_g = nc.dram_tensor("scr_g", (EXPERTS + 1, TOK), F32, kind="Internal").ap()
        c.scr_al = nc.dram_tensor("scr_al", (9, 16, SEQ), BF16, kind="Internal").ap()

        layer_norm(c, "ln1")
        with ExitStack() as st:
            wT = lora_fold(c, st, None)
            v = qkv_stage(c, st, "a0", wT[:, 0], wT[:, 1], wT[:, 2], "L0_bias", c.scr_q, c.scr_k)
            av = st.enter_context(nc.sbuf_tensor("a0_av", [P, 4, TOK], F32))
            attention_stage(c, "a0", 16, False, 0.25, v, c.scr_q, c.scr_k, av)
            normalise_stage(c, st, "a0n", 4, 16, av, wT[:, 3], "L0_bias")
        if STAGES >= 2:
            mla_stages(c)
        if STAGES >= 3:
            ffn_stages(c)
        if STAGES >= 4:
            layer1_attentions(c, STAGES)
        if STAGES >= 6:
            moe_stages(c)
        store_stage(c, out)



def _constants():
    q = np.arange(SEQ)
    causal = np.where(q[None, :] <= q[:, None], 0.0, NEG).astype(np.float32)
    masks = np.stack([
        causal.reshape(QT, P, SEQ).transpose(1, 0, 2).reshape(P, BANK),
        np.concatenate([causal.T[0:P]] * 2, 1),
        np.concatenate([causal.T[P:2 * P]] * 2, 1),
    ], 1)
    pos = q.astype(np.float32).reshape(1, SEQ)

    def rope(length, dim):
        inv = (np.float32(1.0) / np.float32(10000.0) ** (np.arange(0, dim, 2, dtype=np.float32) / np.float32(dim)))
        f = np.arange(length, dtype=np.float32)[:, None] * inv.astype(np.float32)[None, :]
        return np.repeat(np.sin(f), 2, -1).astype(np.float32), np.repeat(np.cos(f), 2, -1).astype(np.float32)

    sin_q, cos_q = rope(SEQ, DCQ)
    hq = DCQ // 2
    sin_moved = np.concatenate([sin_q[:, hq:], -sin_q[:, :hq]], 1)
    rope_q = np.stack([np.concatenate([t.T, t.T]).reshape(3, P, SEQ) for t in (cos_q, sin_moved)])
    sin_k, cos_k = rope(SEQ, CTX)
    hk = CTX // 2
    sin_signed = np.concatenate([-sin_k[:, :hk], sin_k[:, hk:]], 1)
    rope_k = np.stack([t.reshape(QT, P, CTX) for t in (cos_k, sin_signed)])
    return dict(ident=np.eye(P, dtype=np.float32), masks=masks, pos=pos,
                rope_q=rope_q.transpose(2, 0, 1, 3), rope_k=rope_k.transpose(2, 0, 1, 3))


def _columns(rows):
    return rows.reshape(len(rows), DT, P).transpose(2, 0, 1)


def _layout(inputs):
    k = _constants()
    c = np.ascontiguousarray
    a = {n: np.asarray(v) for n, v in inputs.items()}
    io = {
        "x": c(a["x"].reshape(TOK, DIM)),
        "ident": k["ident"], "masks": c(k["masks"]), "pos": c(k["pos"]),
        "L0_WT": np.stack([a[f"L0_attn_W{n}"].T for n in "qkvo"]),
        "L0_B": np.stack([a[f"L0_attn_B{n}"] for n in "qkvo"]),
        "L0_AT": np.stack([a[f"L0_attn_A{n}"].T for n in "qkvo"]),
        "L0_bias": np.stack([a[f"L0_attn_b{n}"] for n in "qkvo"]),
        "L0_bias_col": _columns(np.stack([a["L0_attn_bq"], a["L0_attn_bk"]])),
        "slopes": c(a["L1_attn_alibi_slopes"].reshape(16, 1)),
    }
    wqr = a["L0_xattn_W_qr"]
    wr = np.zeros((PAIRS, 2, 2 * DCQ, 2, R), np.float32)
    for h in range(2):
        for cs, moved in enumerate((wqr, np.roll(wqr, -(DCQ // 2), 1))):
            wr[:, cs, h * DCQ:(h + 1) * DCQ, h] = moved[h::2]
    wkr = np.zeros((PAIRS, P, 2, R), np.float32)
    for h in range(2):
        wkr[:, 0:CTX, h] = a["L0_xattn_W_kr"][h::2]
    pairs = lambda w, r: w.reshape(PAIRS, 2, P, r).transpose(0, 2, 1, 3)
    io.update({
        "ctx": a["ctx_512"].reshape(TOK, CTX),
        "rope_q": k["rope_q"], "rope_k": k["rope_k"],
        "m_wq": pairs(a["L0_xattn_Wq"], DIM), "m_wkq": pairs(a["L0_xattn_w_kc_q"], DCQ),
        "m_wr": wr.reshape(PAIRS, 2, 3, P, 2 * R).transpose(0, 3, 1, 2, 4),
        "m_wkr": wkr.reshape(PAIRS, P, 2 * R),
        "m_wkv": pairs(a["L0_xattn_w_kc_kv"], CTX), "m_wo": pairs(a["L0_xattn_Wo"].T, DIM),
    })
    tiles = lambda w: w.reshape(-1, P, w.shape[-1]).transpose(1, 0, 2).reshape(P, -1)
    qkv = a["L1_attn_qkv_w"].reshape(3, DIM, DIM)
    bias = np.concatenate([a["L1_attn_qkv_b"].reshape(3, DIM), a["L1_attn_out_b"][None]])
    w1 = np.concatenate([a["L1_ffn_w1"], a["L1_ffn_ws1"][None]])
    w3 = np.concatenate([a["L1_ffn_w3"], a["L1_ffn_ws3"][None]])
    w2 = np.concatenate([a["L1_ffn_w2"], a["L1_ffn_ws2"][None]])
    io.update({
        "f_w": np.stack([tiles(a["L0_ffn_w_gate"].T), tiles(a["L0_ffn_w_up"].T), tiles(a["L0_ffn_w_down"].T)]),
        "f_ln": a["L0_ffn_ln_weight"].reshape(1, FFN),
        "L1_WT": np.concatenate([qkv, a["L1_attn_out_w"][None]]).transpose(0, 2, 1),
        "L1_bias": bias, "L1_bias_col": _columns(bias[0:2]),
        "gate_wT": a["L1_ffn_gate_w"].T, "iota": np.arange(EXPERTS, dtype=np.float32).reshape(1, EXPERTS),
        "e_w13": np.stack([w1, w3], 1).reshape(EXPERTS + 1, 2, EH, DT, P).transpose(0, 4, 1, 3, 2),
        "e_w2": w2.transpose(0, 2, 1),
    })
    return {n: c(v) for n, v in io.items()}


def kernel(**inputs):
    import concourse.bacc as bacc
    from concourse.bass_utils import run_bass_kernel_spmd

    nc = bacc.Bacc("TRN2", target_bir_lowering=False, num_devices=1)
    arrays = _layout(inputs)
    io = {n: nc.dram_tensor(f"in_{n}", v.shape, mybir.dt.from_np(v.dtype), kind="ExternalInput").ap()
          for n, v in arrays.items()}
    out = nc.dram_tensor("out_x", (TOK, DIM), F32, kind="ExternalOutput").ap()
    build_program(nc, io, out)
    r = run_bass_kernel_spmd(nc, [{f"in_{n}": v for n, v in arrays.items()}], core_ids=[0])
    return r.results[0]["out_x"].reshape(BATCH, SEQ, DIM)
```

```python
from contextlib import ExitStack

import numpy as np

import concourse.bass as bass
from concourse import mybir

F32 = mybir.dt.float32
F32R = mybir.dt.float32r
BF16 = mybir.dt.bfloat16
U32 = mybir.dt.uint32
ALU = mybir.AluOpType
ACT = mybir.ActivationFunctionType
AX = mybir.AxisListType

P = 128
BATCH, SEQ, DIM = 4, 256, 256
CTX = 64
TOK = BATCH * SEQ
TT = TOK // P
DT = DIM // P
QT = SEQ // P
BANK = 512
HALF = TOK // BANK
LN_EPS = 1e-5
RMS_EPS = 1e-6
QUANT_EPS = 1e-5
INT8_MAX, INT8_MIN = 127.0, -128.0
ROUND = 1.5 * 2.0**23
NEG = -1.0e30
FFN = 1024
EXPERTS, TOPK, EH = 8, 2, 128
ITEMS = 8
TERMS = 6
SCOLS = 32


class Signal:

    def __init__(self, sem):
        self.sem = sem
        self.base = 0

    def at(self, n):
        return n + self.base

    def done(self, n):
        self.base += n


class Chip:

    def __init__(self, nc, ctx, io):
        self.nc, self.ctx, self.io = nc, ctx, io
        self.counters = {}

    def sbuf(self, name, shape, dtype=F32):
        return self.ctx.enter_context(self.nc.sbuf_tensor(name, shape, dtype))

    def counter(self, name):
        if name not in self.counters:
            self.counters[name] = Signal(self.ctx.enter_context(self.nc.semaphore(name)))
        return self.counters[name]



def permanent_buffers(c):
    nc = c.nc
    c.ps = c.ctx.enter_context(nc.psum_tensor("ps", [P, 8, BANK], F32))
    c.x = c.sbuf("x", [P, TT, DIM])
    c.xnT = c.sbuf("xnT", [P, DT, TOK])
    c.ident = c.sbuf("ident", [P, P])
    c.identb = c.sbuf("identb", [P, P], BF16)
    c.fw = c.sbuf("fw", [P, 3, DT * FFN])
    c.wb = c.sbuf("wb", [P, 3, DT * FFN], BF16)
    c.fmean, c.finv = c.sbuf("fmean", [P, 3]), c.sbuf("finv", [P, 3])
    c.fw_in = [c.counter(f"fw_in{k}") for k in range(3)]
    c.xn = c.sbuf("xn", [P, TT, DIM])
    c.cleared = c.counter("cleared")


def stack_slots(c, st, name):
    c.qs = st.enter_context(c.nc.sbuf_tensor(f"{name}_qs", [P, ITEMS, 4, SEQ], BF16))
    c.ks = st.enter_context(c.nc.sbuf_tensor(f"{name}_ks", [P, ITEMS, 4, SEQ], BF16))


def clear_keys(c, pool, steps=range(3)):
    tiles = ((c.ks[0:96, :, :, :].bitcast(F32), 0.0), (c.ks[96:P, :, :, :], 1.0),
             (c.ks[96:P - 2, :, :, :].bitcast(F32), 0.0))
    for k in steps:
        pool.memset(tiles[k][0], tiles[k][1]).then_inc(c.cleared.sem, 1)
        pool.wait_ge(c.cleared.sem, c.cleared.at(k + 2))


def load_stage(c):
    nc, io = c.nc, c.io
    wT, lb, la = c.lora
    x_in, lora_in = c.counter("x_in"), c.counter("lora_in")
    const_in = c.counter("const_in")
    ident_cast = c.counter("ident_cast")

    with nc.Block() as block:

        @block.sync
        def _(sp):
            sp.dma_start(c.x[:, :, :], io["x"].rearrange("(t p) d -> p t d", p=P)).then_inc(x_in.sem, 16)
            sp.dma_start(c.ident[:, :], io["ident"]).then_inc(const_in.sem, 16)
            sp.dma_start(lb[:, :, :], io["L0_B"].rearrange("w r d -> r w d")).then_inc(lora_in.sem, 16)
            sp.dma_start(la[:, :, :], io["L0_AT"].rearrange("w r d -> r w d")).then_inc(lora_in.sem, 16)
            for w in range(4):
                sp.dma_start(wT[:, w, :, :], io["L0_WT"][w].rearrange("(t p) o -> p t o", p=P))\
                    .then_inc(lora_in.sem, 16)

        @block.vector
        def _(dve):
            dve.memset(c.qs[:, :, :, :].bitcast(F32), 0.0).then_inc(c.cleared.sem, 1)
            dve.wait_ge(const_in.sem, 16)
            dve.wait_ge(x_in.sem, 16)
            dve.tensor_copy(c.identb[:, :], c.ident[:, :]).then_inc(ident_cast.sem, 1)
            dve.wait_ge(ident_cast.sem, 1)



def layer_norm(c, name, want_t=True, beside=None):
    nc = c.nc
    with ExitStack() as st:
        stats = st.enter_context(nc.sbuf_tensor(f"{name}_stats", [P, TT, 6], F32))
        mv = st.enter_context(nc.sbuf_tensor(f"{name}_mv", [P, TT, 2], F32))
        std = st.enter_context(nc.sbuf_tensor(f"{name}_std", [P, TT], F32))
        rstd = st.enter_context(nc.sbuf_tensor(f"{name}_rstd", [P, TT], F32))
        stats_done, mv_done, var_done = c.counter("ln_stats"), c.counter("ln_mv"), c.counter("ln_var")
        std_done, rstd_done = c.counter("ln_std"), c.counter("ln_rstd")
        xn_done, tr_done, ev_done = c.counter("ln_xn"), c.counter("ln_tr"), c.counter("ln_ev")

        with nc.Block() as block:

            @block.vector
            def _(dve):
                for t in range(TT):
                    dve.bn_stats(stats[:, t, :], c.x[:, t, :]).then_inc(stats_done.sem, 1)
                for t in range(TT):
                    dve.wait_ge(stats_done.sem, stats_done.at(t + 1))
                    dve.bn_aggr(mv[:, t, :], stats[:, t, :]).then_inc(mv_done.sem, 1)
                dve.wait_ge(mv_done.sem, mv_done.at(TT))
                dve.tensor_scalar(std[:, :], mv[:, :, 1], LN_EPS, None, ALU.add).then_inc(var_done.sem, 1)
                dve.wait_ge(std_done.sem, std_done.at(1))
                dve.reciprocal(rstd[:, :], std[:, :]).then_inc(rstd_done.sem, 1)
                dve.wait_ge(rstd_done.sem, rstd_done.at(1))
                for t in range(TT):
                    dve.tensor_scalar(c.xn[:, t, :], c.x[:, t, :], mv[:, t, 0:1], rstd[:, t:t + 1],
                                      ALU.subtract, ALU.mult).then_inc(xn_done.sem, 1)
                if want_t:
                    for k in (1, 3):
                        dve.wait_ge(tr_done.sem, tr_done.at(k + 1))
                        dve.tensor_copy(c.xnT[:, k % 2, (k // 2) * BANK:(k // 2 + 1) * BANK],
                                        c.ps[:, k, :]).then_inc(ev_done.sem, 1)

            @block.scalar
            def _(act):
                act.wait_ge(var_done.sem, var_done.at(1))
                act.activation(std[:, :], std[:, :], ACT.Sqrt).then_inc(std_done.sem, 1)
                if want_t:
                    for k in (0, 2):
                        act.wait_ge(tr_done.sem, tr_done.at(k + 1))
                        act.activation(c.xnT[:, k % 2, (k // 2) * BANK:(k // 2 + 1) * BANK],
                                       c.ps[:, k, :], ACT.Copy).then_inc(ev_done.sem, 1)

            if beside is not None:
                @block.gpsimd
                def _(pool):
                    beside(pool)

            if want_t:
                @block.tensor
                def _(pe):
                    for k in range(4):
                        pe.wait_ge(xn_done.sem, xn_done.at(4 * (k // 2) + 4))
                        for j in range(4):
                            t = 4 * (k // 2) + j
                            mm = pe.transpose(c.ps[:, k, j * P:(j + 1) * P],
                                              c.xn[:, t, (k % 2) * P:(k % 2 + 1) * P], c.ident[:, :])
                        mm.then_inc(tr_done.sem, 1)

            @block.sync
            def _(sp):
                sp.wait_ge(xn_done.sem, xn_done.at(TT))
                if want_t:
                    sp.wait_ge(ev_done.sem, ev_done.at(4))

        for s, n in ((stats_done, TT), (mv_done, TT), (var_done, 1), (std_done, 1), (rstd_done, 1),
                     (xn_done, TT), (tr_done, 4 if want_t else 0), (ev_done, 4 if want_t else 0)):
            s.done(n)



def lora_fold(c):
    nc, io = c.nc, c.io
    wT, lb, la = c.lora
    loaded, prod, fold = c.counter("lora_in"), c.counter("lora_prod"), c.counter("lora_fold")
    with nc.Block() as block:

        @block.sync
        def _(sp):
            for k in range(3):
                sp.dma_start(c.fw[:, k, :], io["f_w"][k]).then_inc(c.fw_in[k].sem, 16)
            sp.wait_ge(fold.sem, 4)

        @block.gpsimd
        def _(pool):
            clear_keys(c, pool, (2,))

        @block.tensor
        def _(pe):
            pe.wait_ge(loaded.sem, 96)
            for w in range(4):
                for t in range(DT):
                    mm = pe.matmul(c.ps[:, w, t * DIM:(t + 1) * DIM], lb[:, w, t * P:(t + 1) * P],
                                   la[:, w, :], start=True, stop=True)
                mm.then_inc(prod.sem, 1)

        @block.vector
        def _(dve):
            for w in range(4):
                dve.wait_ge(prod.sem, w + 1)
                dve.scalar_tensor_tensor(wT[:, w, :, :], c.ps[:, w, :].rearrange("p (t o) -> p t o", t=DT),
                                         0.5, wT[:, w, :, :], ALU.mult, ALU.add).then_inc(fold.sem, 1)
    c.cleared.done(4)
    return wT


def store_part(sp, w, part, dst, parts, stored):
    for k, p in enumerate(((0, 0, 0, 1, 1, 2), (0, 1, 2, 0, 1, 0))[w]):
        if p == part:
            sp.dma_start(dst[:, k], parts[:, part, :]).then_inc(stored.sem, 16)



def qkv_stage(c, st, name, wq, wk, wv, bias_io, scr_q, scr_k):
    nc, io = c.nc, c.io
    v = st.enter_context(nc.sbuf_tensor(f"{name}_v", [P, TT, DIM], F32))
    with ExitStack() as tmp:
        parts = tmp.enter_context(nc.sbuf_tensor(f"{name}_parts", [P, 2, DT, 3, TOK], BF16))
        rest = tmp.enter_context(nc.sbuf_tensor(f"{name}_rest", [P, 2, BANK], F32))
        bcol = tmp.enter_context(nc.sbuf_tensor(f"{name}_bcol", [P, 2, DT], F32))
        bv = tmp.enter_context(nc.sbuf_tensor(f"{name}_bv", [P, DIM], F32))
        bias_in, proj = c.counter("qkv_bias"), c.counter("qkv_proj")
        hi_done, rest_done, mid_done, lo_done = (c.counter("qkv_hi"), c.counter("qkv_rest"),
                                                 c.counter("qkv_mid"), c.counter("qkv_lo"))
        vproj, v_done, stored = c.counter("qkv_vproj"), c.counter("qkv_v"), c.counter("qkv_stored")
        groups = [(w, ot, half) for w in range(2) for ot in range(DT) for half in range(HALF)]
        NG = len(groups)

        with nc.Block() as block:

            @block.sync
            def _(sp):
                sp.dma_start(bcol[:, :, :], io[bias_io + "_col"]).then_inc(bias_in.sem, 16)
                sp.dma_start(bv[:, :], io[bias_io][2:3, :].broadcast_to([P, DIM])).then_inc(bias_in.sem, 16)
                for k in range(2 * DT):
                    w, ot = divmod(k, DT)
                    for part, done in enumerate((hi_done, mid_done, lo_done)):
                        sp.wait_ge(done.sem, done.at(HALF * (k + 1)))
                        store_part(sp, w, part, (scr_q, scr_k)[w][8 * ot:8 * ot + 8], parts[:, w, ot, :, :],
                                   stored)
                sp.wait_ge(stored.sem, stored.at(16 * TERMS * 2 * DT))
                sp.wait_ge(v_done.sem, v_done.at(TT // 2))

            @block.gpsimd
            def _(pool):
                for g, (w, ot, half) in enumerate(groups):
                    cols = slice(half * BANK, (half + 1) * BANK)
                    pool.wait_ge(mid_done.sem, mid_done.at(g + 1))
                    pool.tensor_tensor(parts[:, w, ot, 2, cols], rest[:, g % 2, :], parts[:, w, ot, 1, cols],
                                       ALU.subtract).then_inc(lo_done.sem, 1)

            @block.tensor
            def _(pe):
                for g, (w, ot, half) in enumerate(groups):
                    if g >= 4:
                        pe.wait_ge(rest_done.sem, rest_done.at(g - 3))
                    for dt in range(DT):
                        mm = pe.matmul(c.ps[:, g % 4, :], (wq, wk)[w][:, dt, ot * P:(ot + 1) * P],
                                       c.xnT[:, dt, half * BANK:(half + 1) * BANK],
                                       start=(dt == 0), stop=(dt == DT - 1))
                    mm.then_inc(proj.sem, 1)
                for t in range(TT):
                    for dt in range(DT):
                        mm = pe.matmul(c.ps[:, 4 + t // 2, (t % 2) * DIM:(t % 2 + 1) * DIM],
                                       c.xnT[:, dt, t * P:(t + 1) * P], wv[:, dt, :],
                                       start=(dt == 0), stop=(dt == DT - 1))
                    if t % 2:
                        mm.then_inc(vproj.sem, 1)

            @block.scalar
            def _(act):
                act.wait_ge(bias_in.sem, bias_in.at(32))
                for g, (w, ot, half) in enumerate(groups + [(None, None, None)]):
                    if g < NG:
                        act.wait_ge(proj.sem, proj.at(g + 1))
                        act.activation(parts[:, w, ot, 0, half * BANK:(half + 1) * BANK], c.ps[:, g % 4, :],
                                       ACT.Identity, bias=bcol[:, w, ot:ot + 1]).then_inc(hi_done.sem, 1)
                    if g >= 1:
                        w, ot, half = groups[g - 1]
                        act.wait_ge(rest_done.sem, rest_done.at(g))
                        act.activation(parts[:, w, ot, 1, half * BANK:(half + 1) * BANK],
                                       rest[:, (g - 1) % 2, :], ACT.Copy).then_inc(mid_done.sem, 1)

            @block.vector
            def _(dve):
                dve.wait_ge(bias_in.sem, bias_in.at(32))
                for g, (w, ot, half) in enumerate(groups):
                    dve.wait_ge(hi_done.sem, hi_done.at(g + 1))
                    if g >= 2:
                        dve.wait_ge(lo_done.sem, lo_done.at(g - 1))
                    dve.scalar_tensor_tensor(rest[:, g % 2, :], c.ps[:, g % 4, :], bcol[:, w, ot:ot + 1],
                                             parts[:, w, ot, 0, half * BANK:(half + 1) * BANK],
                                             ALU.add, ALU.subtract).then_inc(rest_done.sem, 1)
                for k in range(TT // 2):
                    dve.wait_ge(vproj.sem, vproj.at(k + 1))
                    dve.tensor_tensor(v[:, 2 * k:2 * k + 2, :],
                                      c.ps[:, 4 + k, :].rearrange("p (t o) -> p t o", t=2),
                                      bv[:, :].unsqueeze(1).broadcast_to([P, 2, DIM]), ALU.add)\
                        .then_inc(v_done.sem, 1)

        bias_in.done(32)
        for s in (proj, hi_done, rest_done, mid_done, lo_done):
            s.done(NG)
        vproj.done(TT // 2)
        v_done.done(TT // 2)
        stored.done(16 * TERMS * 2 * DT)
    return v



def attention_stage(c, name, hd, shared_k, scale, v, scr_q, scr_k, av_all, alibi=False):
    nc, io = c.nc, c.io
    rows = TERMS * hd
    s_rows = P - 2
    per_seq = 8 if shared_k else 4
    n_seq = ITEMS // per_seq
    NK = 1 if shared_k else 4
    N_ITER = BATCH // n_seq
    UNITS = 3 if alibi else 4
    LAG, TLAG = 4, 3
    MAXR = 4 * QT * 2
    ST0, AV0, OUT0, EX0 = 2 * ITEMS, ITEMS, 1, 2

    with ExitStack() as st:
        def sb(n, shape, dt=F32):
            return st.enter_context(nc.sbuf_tensor(f"{name}_{n}", shape, dt))

        qs = c.qs
        ks = c.ks[:, :, 0:NK, :]
        vs = sb("vs", [P, ITEMS, QT, NK, SCOLS])
        pt = sb("pt", [P, 2, QT, 4 * SEQ])
        one8 = sb("one8", [P, 4 * QT])
        nm = sb("nm", [P, ITEMS, 4 * QT])
        nms = sb("nms", [P, ITEMS, 2, 4 * QT], BF16)
        mT = sb("mT", [MAXR, ITEMS, P], BF16)
        maskb = c.maskb if alibi else None
        filled = c.counter("at_filled")
        in_q = [c.counter(f"at_in{i}") for i in range(ITEMS)]
        m_in = [c.counter(f"at_m{i}") for i in range(ITEMS)]
        v_in = c.counter("at_v_in")
        s_done, mx_done = c.counter("at_s"), c.counter("at_mx")
        nh_done, nl_done = c.counter("at_nh"), c.counter("at_nl")
        tr_done, mt_done = c.counter("at_tr"), c.counter("at_mt")
        st_done, exp_done = c.counter("at_st"), c.counter("at_exp")
        av_done, out_done = c.counter("at_av"), c.counter("at_out")

        def seq_of(it, i):
            return it * n_seq + i // per_seq

        def ahead(step, it, i, last, *part):
            if i < ITEMS:
                step(it, i, *part)
            elif not last:
                step(it + 1, i - ITEMS, *part)

        def iterations(engine, body):
            with engine.Fori(0, N_ITER - 1) as it:
                body(it, False)
            body(N_ITER - 1, True)

        with nc.Block() as block:

            @block.sync
            def _(sp):
                with sp.Fori(0, N_ITER) as it:
                    for i in range(ITEMS):
                        n = it * ITEMS + i
                        toks = bass.ds(seq_of(it, i) * SEQ, SEQ)
                        hg = i % per_seq
                        sp.wait_ge(st_done.sem, st_done.at(2 * n + 2))
                        for dst, scr, heads in ((qs, scr_q, 4), (ks, scr_k, NK)):
                            sp.dma_start(dst[0:rows, i, :, :], scr[heads * hg:heads * (hg + 1), :, :, toks]
                                         .rearrange("h k d q -> (k d) h q")).then_inc(in_q[i].sem, 16)

            @block.gpsimd
            def _(pool):
                pool.memset(vs[:, :, :, :, :], 1.0).then_inc(filled.sem, 1)
                pool.memset(one8[:, :], 1.0).then_inc(filled.sem, 1)
                pool.wait_ge(filled.sem, filled.at(2))
                with pool.Fori(0, N_ITER) as it:
                    for i in range(ITEMS):
                        n = it * ITEMS + i
                        pool.wait_ge(av_done.sem, av_done.at(n + 1))
                        pool.wait_ge(filled.sem, filled.at(1))
                        hg = i % per_seq
                        pool.tensor_copy(vs[:, i, :, :, 0:hd],
                                         v[:, bass.ds(seq_of(it, i) * QT, QT), hg * NK * hd:(hg + 1) * NK * hd]
                                         .rearrange("p t (h d) -> p t h d", h=NK)).then_inc(v_in.sem, 1)
                        pool.wait_ge(mx_done.sem, mx_done.at(UNITS * n + UNITS))
                        pool.tensor_tensor(nms[:, i, 0, :], nm[:, i, :], one8[:, :], ALU.mult)\
                            .then_inc(nh_done.sem, 1)
                        pool.wait_ge(nh_done.sem, nh_done.at(n + 1))
                        pool.tensor_tensor(nms[:, i, 1, :], nm[:, i, :], nms[:, i, 0, :],
                                           ALU.subtract).then_inc(nl_done.sem, 1)

            @block.vector
            def _(dve):
                dve.sem_inc(st_done.sem, ST0)
                dve.sem_inc(av_done.sem, AV0)
                dve.sem_inc(out_done.sem, OUT0)
                def maximum(it, i, u):
                    n = it * ITEMS + i
                    dve.wait_ge(s_done.sem, s_done.at(UNITS * n + u + 1))
                    bank = c.ps[:, (UNITS * i + u) % 2, :]
                    by_head = nm[:, i, :].rearrange("p (h t) -> p h t", t=QT)
                    if not alibi:
                        dst, src = nm[:, i, QT * u:QT * u + QT], bank.rearrange("p (t k) -> p t k", t=QT)
                    elif u == 0:
                        dst, src = by_head[:, :, 0], bank.rearrange("p (h k) -> p h k", k=P)
                    else:
                        dst, src = by_head[:, 2 * u - 2:2 * u, 1], bank.rearrange("p (h k) -> p h k", k=SEQ)
                    dve.tensor_reduce(dst, src, AX.X, ALU.max, negate=True).then_inc(mx_done.sem, 1)

                def outputs(it, i):
                    n = it * ITEMS + i
                    dve.wait_ge(av_done.sem, av_done.at(AV0 + n + 1))
                    dve.tensor_scalar(av_all[:, i % per_seq, bass.ds(seq_of(it, i) * SEQ, SEQ)],
                                      c.ps[:, 6, 0:SEQ], 1.0, None, ALU.mult).then_inc(out_done.sem, 1)

                def body(it, last):
                    for i in range(ITEMS):
                        for u in range(UNITS):
                            ahead(maximum, it, i + LAG, last, u)
                        outputs(it, i)

                dve.sem_inc(exp_done.sem, EX0)
                for i in range(LAG):
                    for u in range(UNITS):
                        maximum(0, i, u)
                iterations(dve, body)

            @block.scalar
            def _(act):
                def max_rows(it, i):
                    n = it * ITEMS + i
                    act.wait_ge(tr_done.sem, tr_done.at(n + 1))
                    act.activation(mT[:, i, :], c.ps[0:MAXR, 7, 0:P], ACT.Copy)\
                        .then_inc(mt_done.sem, 1)
                    act.wait_ge(mt_done.sem, mt_done.at(n + 1))
                    act.dma_start(qs[s_rows:P, i, :, :], mT[:, i, :]).then_inc(m_in[i].sem, 16)

                def exponentials(it, i, kt):
                    n = it * ITEMS + i
                    act.wait_ge(av_done.sem, av_done.at(AV0 + n - 1))
                    act.wait_ge(st_done.sem, st_done.at(ST0 + 2 * n + kt + 1))
                    banks = 1 if alibi and kt == 1 else 2
                    act.activation(pt[:, i % 2, kt, 0:banks * BANK],
                                   c.ps[:, 2 + 2 * kt:2 + 2 * kt + banks, :].rearrange("p b n -> p (b n)"),
                                   ACT.Exp, scale=scale).then_inc(exp_done.sem, 1)

                def body(it, last):
                    for i in range(ITEMS):
                        ahead(exponentials, it, i + 1, last, 0)
                        ahead(max_rows, it, i + TLAG, last)
                        ahead(exponentials, it, i + 1, last, 1)

                for i in range(TLAG):
                    max_rows(0, i)
                for kt in range(QT):
                    exponentials(0, 0, kt)
                iterations(act, body)

            @block.tensor
            def _(pe):
                def is_first(it, i):
                    return isinstance(it, int) and it == 0 and i == 0

                def scores(it, i, u):
                    n = it * ITEMS + i
                    bank = (UNITS * i + u) % 2
                    if u == 0:
                        pe.wait_ge(in_q[i].sem, in_q[i].at((it + 1) * 32))
                    if not is_first(it, i) or u > 1:
                        pe.wait_ge(mx_done.sem, mx_done.at(UNITS * n + u - 1))
                    if alibi:
                        causal_scores(i, u, bank)
                        return
                    for qt in range(QT):
                        mm = pe.matmul(c.ps[:, bank, qt * SEQ:(qt + 1) * SEQ],
                                       qs[0:s_rows, i, u, qt * P:(qt + 1) * P],
                                       ks[0:s_rows, i, 0 if shared_k else u, :], start=True, stop=True)
                    mm.then_inc(s_done.sem, 1)

                def causal_scores(i, u, bank):
                    heads, qt, width = (range(4), 0, P) if u == 0 else (range(2 * u - 2, 2 * u), 1, SEQ)
                    for j, h in enumerate(heads):
                        pe.matmul(c.ps[:, bank, j * width:(j + 1) * width],
                                  qs[0:s_rows, i, h, qt * P:(qt + 1) * P], ks[0:s_rows, i, h, 0:width],
                                  start=(j == 0), stop=True, skip_group_check=True)
                    diagonal = c.ps[:, bank, :].rearrange("p (h k) -> p h k", k=width)[:, :, width - P:width]
                    pe.matmul(diagonal, c.identb[:, :],
                              maskb[:, 0, 0:len(heads) * P].rearrange("p (h k) -> p h k", k=P),
                              start=False, stop=True, skip_group_check=True).then_inc(s_done.sem, 1)

                def max_transpose(it, i):
                    n = it * ITEMS + i
                    if not is_first(it, i):
                        pe.wait_ge(mt_done.sem, mt_done.at(n))
                    pe.wait_ge(nl_done.sem, nl_done.at(n + 1))
                    pe.matmul(c.ps[0:MAXR, 7, 0:P], nms[:, i, :, :].rearrange("p a b -> p (a b)"),
                              c.identb[:, :], start=True, stop=True).then_inc(tr_done.sem, 1)

                def scores_t(it, i, kt):
                    n = it * ITEMS + i
                    if kt == 0:
                        pe.wait_ge(m_in[i].sem, m_in[i].at((it + 1) * 16))
                    pe.wait_ge(exp_done.sem, exp_done.at(EX0 + 2 * n - 1 + kt))
                    if alibi:
                        causal_scores_t(i, kt)
                        return
                    for hh in range(0, 4, 2):
                        bank = 2 + 2 * kt + hh // 2
                        if shared_k:
                            mm = pe.matmul(c.ps[:, bank, :], ks[:, i, 0, kt * P:(kt + 1) * P],
                                           qs[:, i, hh:hh + 2, :].rearrange("p h q -> p (h q)"),
                                           start=True, stop=True)
                        else:
                            for h in range(hh, hh + 2):
                                mm = pe.matmul(c.ps[:, bank, (h % 2) * SEQ:(h % 2 + 1) * SEQ],
                                               ks[:, i, h, kt * P:(kt + 1) * P], qs[:, i, h, :],
                                               start=True, stop=True)
                    mm.then_inc(st_done.sem, 1)

                def causal_scores_t(i, kt):
                    width = SEQ if kt == 0 else P
                    for first in range(0, 4, BANK // width):
                        heads = range(first, first + BANK // width)
                        bank = 2 + 2 * kt + first // 2
                        for j, h in enumerate(heads):
                            pe.matmul(c.ps[:, bank, j * width:(j + 1) * width], ks[:, i, h, kt * P:(kt + 1) * P],
                                      qs[:, i, h, SEQ - width:SEQ],
                                      start=(j == 0), stop=True, skip_group_check=True)
                        diagonal = c.ps[:, bank, :].rearrange("p (h q) -> p h q", q=width)[:, :, 0:P]
                        mm = pe.matmul(diagonal, c.identb[:, :],
                                       maskb[:, 1, 0:len(heads) * P].rearrange("p (h q) -> p h q", q=P),
                                       start=False, stop=True, skip_group_check=True)
                    mm.then_inc(st_done.sem, 1)

                def product(it, i, kt):
                    n = it * ITEMS + i
                    if kt == 0:
                        pe.wait_ge(v_in.sem, v_in.at(n + 1))
                        pe.wait_ge(out_done.sem, out_done.at(OUT0 + n))
                    pe.wait_ge(exp_done.sem, exp_done.at(EX0 + 2 * n + kt + 1))
                    width = P if alibi and kt == 1 else SEQ
                    for hh in range(4):
                        mm = pe.matmul(c.ps[SCOLS * hh:SCOLS * (hh + 1), 6, SEQ - width:SEQ],
                                       vs[:, i, kt, 0 if shared_k else hh, :],
                                       pt[:, i % 2, kt, hh * width:(hh + 1) * width],
                                       start=(kt == 0), stop=(kt == QT - 1), skip_group_check=True)
                    if kt == QT - 1:
                        mm.then_inc(av_done.sem, 1)

                for i in range(LAG):
                    for u in range(UNITS):
                        scores(0, i, u)
                    if i >= LAG - TLAG:
                        max_transpose(0, i - (LAG - TLAG))
                for kt in range(QT):
                    scores_t(0, 0, kt)

                def body(it, last):
                    for i in range(ITEMS):
                        ahead(scores, it, i + LAG, last, 0)
                        ahead(scores_t, it, i + 1, last, 0)
                        ahead(scores, it, i + LAG, last, 1)
                        product(it, i, 0)
                        ahead(max_transpose, it, i + TLAG, last)
                        ahead(scores, it, i + LAG, last, 2)
                        product(it, i, 1)
                        if UNITS == 4:
                            ahead(scores, it, i + LAG, last, 3)
                        ahead(scores_t, it, i + 1, last, 1)

                iterations(pe, body)

        n_items = N_ITER * ITEMS
        filled.done(2)
        for s in in_q:
            s.done(32 * N_ITER)
        for s in m_in:
            s.done(16 * N_ITER)
        for s in (v_in, nh_done, nl_done, tr_done, mt_done):
            s.done(n_items)
        s_done.done(UNITS * n_items)
        mx_done.done(UNITS * n_items)
        st_done.done(ST0 + 2 * n_items)
        exp_done.done(EX0 + 2 * n_items)
        av_done.done(AV0 + n_items)
        out_done.done(OUT0 + n_items)


def normalise_stage(c, st, name, groups, hd, av_all, wo, bias_io):
    nc, io = c.nc, c.io
    heads = 4 * groups
    nb = groups * P // BANK
    with ExitStack() as tmp:
        def sb(n, shape, dt=F32):
            return tmp.enter_context(nc.sbuf_tensor(f"{name}_{n}", shape, dt))

        rec = sb("rec", [P, TT, heads])
        on = sb("on", [P, TT, heads, hd])
        onT = sb("onT", [P, DT, TOK])
        bo = sb("bo", [P, DIM])
        bias_in, tr_done, rec_done, on_done = (c.counter("no_bias"), c.counter("no_tr"), c.counter("no_rec"),
                                               c.counter("no_on"))
        t2_done, onT_done, y_done, x_done = (c.counter("no_t2"), c.counter("no_onT"), c.counter("no_y"),
                                             c.counter("no_x"))
        xb_done = c.counter("no_xb")

        def out_view(t):
            b0 = nb * (t % 2)
            return c.ps[:, b0:b0 + nb, :].rearrange("p b (h s) -> p (b h) s", s=SCOLS)

        with nc.Block() as block:

            @block.tensor
            def _(pe):
                def second(t):
                    pe.wait_ge(on_done.sem, on_done.at(t + 1))
                    if t >= 2:
                        pe.wait_ge(onT_done.sem, onT_done.at(t - 1))
                    for dt in range(DT):
                        mm = pe.transpose(c.ps[:, 4 + t % 2, dt * P:(dt + 1) * P],
                                          on[:, t, :, :].rearrange("p h d -> p (h d)")[:, dt * P:(dt + 1) * P],
                                          c.ident[:, :])
                    mm.then_inc(t2_done.sem, 1)

                def project(t):
                    pe.wait_ge(onT_done.sem, onT_done.at(t + 1))
                    if t >= 2:
                        pe.wait_ge(x_done.sem, x_done.at(t - 1))
                    for dt in range(DT):
                        mm = pe.matmul(c.ps[:, 6 + t % 2, 0:DIM], onT[:, dt, t * P:(t + 1) * P],
                                       wo[:, dt, :], start=(dt == 0), stop=(dt == DT - 1))
                    mm.then_inc(y_done.sem, 1)

                for t in range(TT + 2):
                    if t < TT:
                        if t >= 2:
                            pe.wait_ge(on_done.sem, on_done.at(t - 1))
                        for g in range(groups):
                            mm = pe.transpose(c.ps[:, nb * (t % 2) + g // 4, (g % 4) * P:(g % 4 + 1) * P],
                                              av_all[:, g, t * P:(t + 1) * P], c.ident[:, :])
                        mm.then_inc(tr_done.sem, 1)
                    if wo is not None and 1 <= t <= TT:
                        second(t - 1)
                    if wo is not None and t >= 2:
                        project(t - 2)

            @block.vector
            def _(dve):
                def residual(t):
                    dve.wait_ge(y_done.sem, y_done.at(t + 1))
                    dve.tensor_tensor(c.x[:, t, :], c.ps[:, 6 + t % 2, 0:DIM], c.x[:, t, :], ALU.add)\
                        .then_inc(x_done.sem, 1)

                if wo is not None:
                    dve.wait_ge(xb_done.sem, xb_done.at(1))
                for t in range(TT):
                    dve.wait_ge(tr_done.sem, tr_done.at(t + 1))
                    dve.reciprocal(rec[:, t, :], out_view(t)[:, :, hd:hd + 1].squeeze(2)).then_inc(rec_done.sem, 1)
                    dve.wait_ge(rec_done.sem, rec_done.at(t + 1))
                    dve.tensor_tensor(on[:, t, :, :], out_view(t)[:, :, 0:hd],
                                      rec[:, t, :].unsqueeze(2).broadcast_to([P, heads, hd]), ALU.mult)\
                        .then_inc(on_done.sem, 1)
                    if wo is None:
                        dve.wait_ge(on_done.sem, on_done.at(t + 1))
                        dve.tensor_tensor(c.x[:, t, :], on[:, t, :, :].rearrange("p h d -> p (h d)"),
                                          c.x[:, t, :], ALU.add).then_inc(x_done.sem, 1)
                    elif t >= 2:
                        residual(t - 2)
                if wo is not None:
                    residual(TT - 2)
                    residual(TT - 1)

            if wo is not None:
                @block.sync
                def _(sp):
                    sp.dma_start(bo[:, :], io[bias_io][3:4, :].broadcast_to([P, DIM])).then_inc(bias_in.sem, 16)

                @block.gpsimd
                def _(pool):
                    pool.wait_ge(bias_in.sem, bias_in.at(16))
                    pool.tensor_tensor(c.x[:, :, :], c.x[:, :, :],
                                       bo[:, :].unsqueeze(1).broadcast_to([P, TT, DIM]), ALU.add)\
                        .then_inc(xb_done.sem, 1)

                @block.scalar
                def _(act):
                    for t in range(TT):
                        act.wait_ge(t2_done.sem, t2_done.at(t + 1))
                        act.activation(onT[:, :, t * P:(t + 1) * P],
                                       c.ps[:, 4 + t % 2, 0:DIM].rearrange("p (t n) -> p t n", t=DT),
                                       ACT.Copy).then_inc(onT_done.sem, 1)

        for s in (tr_done, rec_done, on_done, x_done):
            s.done(TT)
        if wo is not None:
            for s in (t2_done, onT_done, y_done):
                s.done(TT)
            bias_in.done(16)
            xb_done.done(1)


PAIRS = 8
HK, DCQ, R = 128, 192, 64


def context_stage(c, st):
    nc, io = c.nc, c.io
    kvr = st.enter_context(nc.sbuf_tensor("m_kvr", [P, TT, CTX], F32))
    kvT = st.enter_context(nc.sbuf_tensor("m_kvT", [P, TOK], F32))
    with ExitStack() as tmp:
        def sb(n, shape, dt=F32):
            return tmp.enter_context(nc.sbuf_tensor(f"mc_{n}", shape, dt))

        raw = sb("raw", [P, TT, CTX])
        rot = sb("rot", [P, TT, CTX])
        tab = sb("tab", [P, 2, QT, CTX])
        t1 = sb("t1", [P, TT, CTX])
        junk, ones = sb("junk", [P, DT * FFN]), sb("ones", [P, P])
        asum = sb("asum", [P, 3])
        summed, total, scales = c.counter("fw_sum"), c.counter("fw_total"), c.counter("fw_step")
        loaded, step, tr = c.counter("mc_in"), c.counter("mc_step"), c.counter("mc_tr")
        half = CTX // 2
        with nc.Block() as block:

            @block.sync
            def _(sp):
                src = io["ctx"].rearrange("(t p) d -> p t d", p=P)
                sp.dma_start(raw[:, :, :], src).then_inc(loaded.sem, 16)
                sp.dma_start(rot[:, :, 0:half], src[:, :, half:CTX]).then_inc(loaded.sem, 16)
                sp.dma_start(rot[:, :, half:CTX], src[:, :, 0:half]).then_inc(loaded.sem, 16)
                sp.dma_start(tab[:, :, :, :], io["rope_k"]).then_inc(loaded.sem, 16)

            @block.vector
            def _(dve):
                def by_seq(a):
                    return a.rearrange("p (b t) d -> p b (t d)", t=QT)

                def table(k):
                    return tab[:, k, :, :].rearrange("p t d -> p (t d)").unsqueeze(1)\
                        .broadcast_to([P, BATCH, QT * CTX])

                dve.memset(kvT[:, :], 0.0).then_inc(step.sem, 1)
                dve.wait_ge(loaded.sem, 64)
                dve.tensor_tensor(by_seq(t1[:, :, :]), by_seq(raw[:, :, :]), table(0), ALU.mult)\
                    .then_inc(step.sem, 1)
                dve.tensor_tensor(by_seq(rot[:, :, :]), by_seq(rot[:, :, :]), table(1), ALU.mult)\
                    .then_inc(step.sem, 1)
                dve.wait_ge(step.sem, 3)
                dve.tensor_tensor(kvr[:, :, :], t1[:, :, :], rot[:, :, :], ALU.add).then_inc(step.sem, 1)
                dve.wait_ge(tr.sem, 1)
                dve.tensor_copy(kvT[0:CTX, :], c.ps[0:CTX, 0:2, :].rearrange("p b n -> p (b n)"))\
                    .then_inc(step.sem, 1)
                dve.wait_ge(total.sem, 1)
                dve.tensor_scalar(c.fmean[:, :], c.ps[:, 3, 0:3], 1.0 / (FFN * DIM), QUANT_EPS, ALU.mult, ALU.max)\
                    .then_inc(scales.sem, 1)
                dve.wait_ge(scales.sem, 2)
                dve.reciprocal(c.finv[:, :], c.fmean[:, :]).then_inc(scales.sem, 1)
                dve.wait_ge(scales.sem, 3)
                dve.wait_ge(step.sem, 5)

            @block.gpsimd
            def _(pool):
                pool.memset(ones[:, :], 1.0).then_inc(scales.sem, 1)

            @block.scalar
            def _(act):
                for k in range(3):
                    act.wait_ge(c.fw_in[k].sem, 16)
                    if k:
                        act.wait_ge(summed.sem, k)
                    act.activation(junk[:, :], c.fw[:, k, :], ACT.Abs, accum_out=asum[:, k:k + 1])\
                        .then_inc(summed.sem, 1)

            @block.tensor
            def _(pe):
                pe.wait_ge(scales.sem, 1)
                pe.wait_ge(summed.sem, 3)
                pe.matmul(c.ps[:, 3, 0:3], ones[:, :], asum[:, :], start=True, stop=True).then_inc(total.sem, 1)
                pe.wait_ge(step.sem, 4)
                for t in range(TT):
                    mm = pe.transpose(c.ps[0:CTX, t // 4, (t % 4) * P:(t % 4 + 1) * P], kvr[:, t, :],
                                      c.ident[:, :])
                mm.then_inc(tr.sem, 1)
    return kvr, kvT


def mla_stages(c):
    nc, io = c.nc, c.io
    layer_norm(c, "ln2")
    with ExitStack() as st:
        kvr, kvT = context_stage(c, st)

        def sb(n, shape, dt=F32):
            return st.enter_context(nc.sbuf_tensor(f"m_{n}", shape, dt))

        ctxn = sb("ctxn", [P, PAIRS, TOK])
        nw = sb("nw", [P, PAIRS, DIM])
        with ExitStack() as tmp:
            mla_pairs(c, tmp, kvr, kvT, ctxn, nw)

        cp = sb("cp", [P, 2, 2, TOK], F32R)
        wp = sb("wp", [P, 2, PAIRS, DIM], F32R)
        w_hi, w_lo, high, low = (c.counter(f"at_m{k}") for k in (0, 1, 2, 4))
        y_done, x_done, used = c.counter("mo_y"), c.counter("mo_x"), c.counter("at_m3")
        with nc.Block() as block:

            @block.scalar
            def _(act):
                for p in range(PAIRS):
                    act.activation(wp[:, 0, p, :], nw[:, p, :], ACT.Copy).then_inc(w_hi.sem, 1)
                    if p >= 2:
                        act.wait_ge(used.sem, used.at(p - 1))
                    act.activation(cp[:, p % 2, 0, :], ctxn[:, p, :], ACT.Copy).then_inc(high.sem, 1)

            @block.vector
            def _(dve):
                for p in range(PAIRS):
                    dve.wait_ge(w_hi.sem, w_hi.at(p + 1))
                    dve.tensor_tensor(wp[:, 1, p, :], nw[:, p, :], wp[:, 0, p, :].bitcast(F32), ALU.subtract)\
                        .then_inc(w_lo.sem, 1)
                    dve.wait_ge(high.sem, high.at(p + 1))
                    dve.tensor_tensor(cp[:, p % 2, 1, :], ctxn[:, p, :], cp[:, p % 2, 0, :].bitcast(F32),
                                      ALU.subtract).then_inc(low.sem, 1)
                for t in range(TT):
                    dve.wait_ge(y_done.sem, t + 1)
                    dve.tensor_tensor(c.x[:, t, :], c.ps[:, t, 0:DIM], c.x[:, t, :], ALU.add)\
                        .then_inc(x_done.sem, 1)
                dve.wait_ge(x_done.sem, TT)

            @block.tensor
            def _(pe):
                for p in range(PAIRS):
                    pe.wait_ge(w_lo.sem, w_lo.at(p + 1))
                    pe.wait_ge(low.sem, low.at(p + 1))
                    for t in range(TT):
                        for k, (x, w) in enumerate(((0, 0), (0, 1), (1, 0))):
                            mm = pe.matmul(c.ps[:, t, 0:DIM], cp[:, p % 2, x, t * P:(t + 1) * P], wp[:, w, p, :],
                                           start=(p == 0 and k == 0), stop=(p == PAIRS - 1 and k == 2))
                        if p == PAIRS - 1:
                            mm.then_inc(y_done.sem, 1)
                    if p < PAIRS - 1:
                        mm.then_inc(used.sem, 1)
        for s in (w_hi, w_lo, high, low):
            s.done(PAIRS)
        used.done(PAIRS - 1)


def mla_pairs(c, st, kvr, kvT, ctxn, nw):
    nc, io = c.nc, c.io

    def sb(n, shape, dt=F32):
        return st.enter_context(nc.sbuf_tensor(f"mp_{n}", shape, dt))

    wq2, wkq = sb("wq2", [P, 2, DIM]), sb("wkq", [P, 2, DCQ])
    wr = sb("wr", [P, 2, 3, 2 * R])
    wkr = sb("wkr", [P, 2 * R])
    wkv, wo = sb("wkv", [P, 2, CTX]), sb("wo", [P, 2, DIM])
    tab = sb("tab", [P, 2, 3, SEQ])
    mp = sb("mp", [P, 2, DT, 2 * DCQ], F32R)
    xp = sb("xp", [P, 2, DT, TOK], F32R)
    qcs = sb("qcs", [P, HALF, 3, 2, BANK])
    qa = c.xn[:, :, :].rearrange("p (h t) d -> p h (t d)", h=2)
    ks = sb("ks", [P, 2, TOK])
    zero = sb("zero", [1, TOK])
    nm = sb("nm", [P, HALF, 2, BATCH // HALF, QT])
    MR = 2 * BATCH // HALF * QT
    mT = sb("mT", [MR, HALF, P])
    pt = sb("pt", [P, 2, 2, QT, SEQ])
    ones = sb("ones", [P, R])
    inv = sb("inv", [P, 2, SEQ])

    tab_in, prep, tern = c.counter("mp_tab"), c.counter("mp_prep"), c.counter("mp_tern")
    w_a, w_k, w_r, w_n = (c.counter("mp_wa"), c.counter("mp_wk"), c.counter("mp_wr"), c.counter("mp_wn"))
    kr, k_ev = c.counter("mp_kr"), c.counter("mp_k_ev")
    a_done, mp_hi, mp_done, xp_s = c.counter("mp_a"), c.counter("mp_hi"), c.counter("mp_mp"), c.counter("mp_xp")
    qb, rope, qr = c.counter("mp_qb"), c.counter("mp_rope"), c.counter("mp_qr")
    q_ev, q_ev2, z_in = c.counter("mp_q_ev"), c.counter("mp_q_ev2"), c.counter("mp_z_in")
    m_in = [c.counter(f"mp_m_in{half}") for half in range(HALF)]
    s_done, mx = c.counter("mp_s"), c.counter("mp_mx")
    tr, mt = c.counter("mp_tr"), c.counter("mp_mt")
    n_done, nw_done = c.counter("mp_n"), c.counter("mp_nw")
    stt, ex, av = c.counter("mp_st"), c.counter("mp_ex"), c.counter("mp_av")
    inv_done, out = c.counter("mp_inv"), c.counter("mp_out")
    OUT0, Z0 = 2, 1
    TILE_ORDER = (1, 0, 2)
    QB_BANKS = (2, 3, 0, 1)
    S_BANKS = (0, 1, 0, 1, 2, 3, 0, 1)

    def rows(h):
        return slice(R * h, R * h + R)

    def m_row(h):
        return slice(R * (1 - h), R * (1 - h) + 1)

    def half_cols(half):
        return slice(half * BANK, (half + 1) * BANK)

    def pairs(engine, body):
        with engine.Fori(0, PAIRS - 1) as it:
            body(it, False)
        body(PAIRS - 1, True)

    with nc.Block() as block:

        @block.sync
        def _(sp):
            def load_k(p):
                sp.dma_start(wkr[:, :], io["m_wkr"][p]).then_inc(w_k.sem, 16)

            def load_a(p):
                sp.dma_start(wq2[:, :, :], io["m_wq"][p]).then_inc(w_a.sem, 16)
                sp.dma_start(wkq[:, :, :], io["m_wkq"][p]).then_inc(w_a.sem, 16)

            def load_r(p):
                sp.dma_start(wr[:, :, :, :], io["m_wr"][p]).then_inc(w_r.sem, 16)

            def load_n(p):
                sp.dma_start(wkv[:, :, :], io["m_wkv"][p]).then_inc(w_n.sem, 16)
                sp.dma_start(wo[:, :, :], io["m_wo"][p]).then_inc(w_n.sem, 16)

            load_k(0)
            load_a(0)
            sp.dma_start(tab[:, :, :, :], io["rope_q"]).then_inc(tab_in.sem, 16)
            load_r(0)
            load_n(0)
            with sp.Fori(1, PAIRS) as it:
                sp.wait_ge(kr.sem, it * 2)
                load_k(bass.ds(it, 1))
                sp.wait_ge(a_done.sem, it * 1)
                load_a(bass.ds(it, 1))
                sp.wait_ge(qr.sem, it * 2)
                load_r(bass.ds(it, 1))
                sp.wait_ge(n_done.sem, it * 1)
                load_n(bass.ds(it, 1))
                sp.wait_ge(stt.sem, it * 4)
                for h in range(2):
                    sp.dma_start(qa[m_row(h), h, :], zero[:, :]).then_inc(z_in.sem, 16)

        @block.gpsimd
        def _(pool):
            for tile, value in ((ks[:, :, :], 0.0), (qa[:, :, :], 0.0), (ones[:, :], 1.0), (zero[:, :], 0.0)):
                pool.memset(tile, value).then_inc(prep.sem, 1)
            pool.wait_ge(prep.sem, 4)
            for h in range(2):
                pool.memset(ks[m_row(h), h, :], 1.0).then_inc(prep.sem, 1)
            pool.wait_ge(prep.sem, 6)
            for k in range(3):
                w = c.fw[:, k, :]
                pool.tensor_scalar(w, w, c.finv[:, k:k + 1], ROUND, ALU.mult, ALU.add).then_inc(tern.sem, 1)
                pool.wait_ge(tern.sem, 3 * k + 1)
                pool.tensor_scalar(w, w, -ROUND, -1.0, ALU.add, ALU.max).then_inc(tern.sem, 1)
                pool.wait_ge(tern.sem, 3 * k + 2)
                pool.tensor_scalar(c.wb[:, k, :], w, 1.0, None, ALU.min).then_inc(tern.sem, 1)
            pool.wait_ge(tern.sem, 9)

        @block.vector
        def _(dve):
            def rotate(it, k):
                half, tile = k // 3, TILE_ORDER[k % 3]
                dve.wait_ge(qb.sem, it * 6 + (k + 1))
                for cs in range(2):
                    dve.tensor_tensor(
                        qcs[:, half, tile, cs, :].rearrange("p (b q) -> p b q", q=SEQ),
                        c.ps[:, QB_BANKS[k % 4], :].rearrange("p (b q) -> p b q", q=SEQ),
                        tab[:, cs, tile, :].unsqueeze(1).broadcast_to([P, 2, SEQ]), ALU.mult)\
                        .then_inc(rope.sem, 1)

            def folded(p):
                dve.wait_ge(mp_hi.sem, p + 1)
                dve.tensor_tensor(mp[:, 1, :, :], c.ps[:, 0:2, 0:2 * DCQ], mp[:, 0, :, :].bitcast(F32),
                                  ALU.subtract).then_inc(mp_done.sem, 1)

            def queries(it, half):
                dve.wait_ge(qr.sem, it * 2 + (half + 1))
                dve.tensor_copy(qa[rows(1), 1, half_cols(half)], c.ps[rows(1), 4 + half, :])\
                    .then_inc(q_ev2.sem, 1)

            def maximum(it, k):
                b, h = k // 2, k % 2
                dve.wait_ge(s_done.sem, it * 8 + (k + 1))
                dve.tensor_reduce(nm[:, b // 2, h, b % 2, :],
                                  c.ps[:, S_BANKS[k], :].rearrange("p (t k) -> p t k", t=QT),
                                  AX.X, ALU.max, negate=True).then_inc(mx.sem, 1)

            def outputs(it, b):
                dve.wait_ge(av.sem, it * 4 + (b + 1))
                cols = slice(b * SEQ, (b + 1) * SEQ)
                dve.reciprocal(inv[:, b % 2, :], c.ps[:, 6 + b % 2, SEQ:2 * SEQ]).then_inc(inv_done.sem, 1)
                dve.wait_ge(inv_done.sem, it * 4 + (b + 1))
                dve.tensor_tensor(ctxn[:, bass.ds(it, 1), cols].squeeze(1), c.ps[:, 6 + b % 2, 0:SEQ],
                                  inv[:, b % 2, :], ALU.mult).then_inc(out.sem, 1)

            def body(it, last):
                for k in range(5):
                    rotate(it, k)
                queries(it, 0)
                rotate(it, 5)
                for k in range(4):
                    maximum(it, k)
                queries(it, 1)
                for k in range(4, 8):
                    maximum(it, k)
                dve.wait_ge(n_done.sem, it + 1)
                dve.tensor_scalar(nw[:, bass.ds(it, 1), :].squeeze(1), c.ps[:, 5, 0:DIM], 1.0, None, ALU.mult)\
                    .then_inc(nw_done.sem, 1)
                outputs(it, 0)
                if not last:
                    folded(it + 1)
                for b in range(1, BATCH):
                    outputs(it, b)

            dve.sem_inc(out.sem, OUT0)
            dve.sem_inc(z_in.sem, Z0)
            dve.wait_ge(tab_in.sem, 16)
            dve.wait_ge(prep.sem, 6)
            dve.wait_ge(xp_s.sem, 1)
            dve.tensor_tensor(xp[:, 1, :, :], c.xnT[:, :, :], xp[:, 0, :, :].bitcast(F32), ALU.subtract)\
                .then_inc(xp_s.sem, 1)
            folded(0)
            pairs(dve, body)

        @block.scalar
        def _(act):
            def keys(p):
                for half in range(HALF):
                    act.wait_ge(kr.sem, p * 2 + (half + 1))
                    for h in range(2):
                        act.activation(ks[rows(h), h, half_cols(half)], c.ps[rows(h), half, :], ACT.Copy)\
                            .then_inc(k_ev.sem, 1)

            def folded(p):
                act.wait_ge(a_done.sem, p + 1)
                act.activation(mp[:, 0, :, :], c.ps[:, 0:2, 0:2 * DCQ], ACT.Copy).then_inc(mp_hi.sem, 1)

            def queries(it, half):
                act.wait_ge(qr.sem, it * 2 + (half + 1))
                act.activation(qa[rows(0), 0, half_cols(half)], c.ps[rows(0), 4 + half, :], ACT.Copy)\
                    .then_inc(q_ev.sem, 1)

            def max_rows(it, half):
                act.wait_ge(tr.sem, it * 2 + (half + 1))
                act.activation(mT[:, half, :], c.ps[0:MR, 7, 0:P], ACT.Copy).then_inc(mt.sem, 1)
                act.wait_ge(mt.sem, it * 2 + (half + 1))
                for h in range(2):
                    act.dma_start(qa[m_row(h), h, half_cols(half)], mT[h * MR // 2:(h + 1) * MR // 2, half, :])\
                        .then_inc(m_in[half].sem, 16)

            def exponentials(it, b):
                act.wait_ge(stt.sem, it * 4 + (b + 1))
                if b >= 2:
                    act.wait_ge(av.sem, it * 4 + (b - 1))
                act.activation(pt[:, b % 2, :, :, :].rearrange("p h t q -> p (h t q)"),
                               c.ps[:, 2 + 2 * (b % 2):4 + 2 * (b % 2), :].rearrange("p b n -> p (b n)"),
                               ACT.Exp).then_inc(ex.sem, 1)

            def body(it, last):
                queries(it, 0)
                queries(it, 1)
                max_rows(it, 0)
                exponentials(it, 0)
                max_rows(it, 1)
                exponentials(it, 1)
                if not last:
                    folded(it + 1)
                exponentials(it, 2)
                exponentials(it, 3)
                if not last:
                    keys(it + 1)

            act.activation(xp[:, 0, :, :], c.xnT[:, :, :], ACT.Copy).then_inc(xp_s.sem, 1)
            folded(0)
            act.wait_ge(prep.sem, 6)
            keys(0)
            pairs(act, body)

        @block.tensor
        def _(pe):
            def keys(p):
                pe.wait_ge(w_k.sem, p * 16 + 16)
                pe.wait_ge(mp_done.sem, p + 1)
                for half in range(HALF):
                    pe.matmul(c.ps[:, half, :], wkr[:, :], kvT[:, half_cols(half)],
                              start=True, stop=True).then_inc(kr.sem, 1)

            def fold(p):
                pe.wait_ge(w_a.sem, p * 32 + 32)
                for dt in range(DT):
                    for h in range(2):
                        mm = pe.matmul(c.ps[:, dt, h * DCQ:(h + 1) * DCQ], wq2[:, h, dt * P:(dt + 1) * P],
                                       wkq[:, h, :], start=True, stop=True)
                mm.then_inc(a_done.sem, 1)

            def packed(it, k):
                half, tile = k // 3, TILE_ORDER[k % 3]
                if k == 0:
                    pe.wait_ge(mp_done.sem, it + 1)
                if k == 2:
                    pe.wait_ge(k_ev.sem, it * 4 + 4)
                if k >= 4:
                    pe.wait_ge(rope.sem, it * 12 + 2 * (k - 3))
                terms = [(dt, w, x) for dt in range(DT) for w, x in ((0, 0), (0, 1), (1, 0))]
                for dt, w, x in terms:
                    mm = pe.matmul(c.ps[:, QB_BANKS[k % 4], :], mp[:, w, dt, tile * P:(tile + 1) * P],
                                   xp[:, x, dt, half_cols(half)], start=((dt, w, x) == terms[0]),
                                   stop=((dt, w, x) == terms[-1]))
                mm.then_inc(qb.sem, 1)

            def scored_both(it, half):
                if half == 0:
                    pe.wait_ge(w_r.sem, it * 16 + 16)
                pe.wait_ge(rope.sem, it * 12 + (6 * half + 2))
                for cs in range(2):
                    pe.matmul(c.ps[:, 4 + half, :], wr[:, cs, 1, :], qcs[:, half, 1, cs, :],
                              start=(cs == 0), stop=False, skip_group_check=True)

            def scored_own(it, half):
                pe.wait_ge(rope.sem, it * 12 + (6 * half + 6))
                for cs in range(2):
                    for h, tile in ((0, 0), (1, 2)):
                        mm = pe.matmul(c.ps[rows(h), 4 + half, :], wr[:, cs, tile, rows(h)],
                                       qcs[:, half, tile, cs, :], start=False, stop=(cs == 1),
                                       skip_group_check=True)
                mm.then_inc(qr.sem, 1)

            def scores(it, k):
                b, h = k // 2, k % 2
                if k == 0:
                    pe.wait_ge(rope.sem, it * 12 + 8)
                    pe.wait_ge(z_in.sem, it * 32 + Z0)
                if k % 4 == 0:
                    pe.wait_ge(q_ev.sem, it * 2 + (k // 4 + 1))
                    pe.wait_ge(q_ev2.sem, it * 2 + (k // 4 + 1))
                if k in (2, 3):
                    pe.wait_ge(mx.sem, it * 8 + (k - 1))
                if k in (6, 7):
                    pe.wait_ge(mx.sem, it * 8 + (k - 3))
                for qt in range(QT):
                    q0 = b * SEQ + qt * P
                    mm = pe.matmul(c.ps[:, S_BANKS[k], qt * SEQ:(qt + 1) * SEQ], qa[:, h, q0:q0 + P],
                                   ks[:, h, b * SEQ:(b + 1) * SEQ], start=True, stop=True)
                mm.then_inc(s_done.sem, 1)

            def max_transpose(it, half):
                pe.wait_ge(mx.sem, it * 8 + 4 * (half + 1))
                if half == 0:
                    pe.wait_ge(out.sem, it * 4 + OUT0)
                else:
                    pe.wait_ge(mt.sem, it * 2 + 1)
                pe.transpose(c.ps[0:MR, 7, 0:P], nm[:, half, :, :, :].rearrange("p h b t -> p (h b t)"),
                             c.ident[:, :]).then_inc(tr.sem, 1)

            def output_weight(it):
                pe.wait_ge(w_n.sem, it * 32 + 32)
                for h in range(2):
                    mm = pe.matmul(c.ps[rows(h), 5, 0:DIM], wkv[:, h, :], wo[:, h, :], start=True, stop=True)
                mm.then_inc(n_done.sem, 1)

            def scores_t(it, b):
                if b % 2 == 0:
                    pe.wait_ge(m_in[b // 2].sem, it * 32 + 32)
                if b == 0:
                    pe.wait_ge(mx.sem, it * 8 + 6)
                if b == 1:
                    pe.wait_ge(nw_done.sem, it + 1)
                if b >= 2:
                    pe.wait_ge(ex.sem, it * 4 + (b - 1))
                for h in range(2):
                    for kt in range(QT):
                        mm = pe.matmul(c.ps[:, 2 + 2 * (b % 2) + h, kt * SEQ:(kt + 1) * SEQ],
                                       ks[:, h, b * SEQ + kt * P:b * SEQ + (kt + 1) * P],
                                       qa[:, h, b * SEQ:(b + 1) * SEQ], start=True, stop=True)
                mm.then_inc(stt.sem, 1)

            def product(it, b):
                pe.wait_ge(ex.sem, it * 4 + (b + 1))
                pe.wait_ge(out.sem, it * 4 + (OUT0 - 1 + b))
                if b == 1:
                    pe.wait_ge(mt.sem, it * 2 + 2)
                for part in range(2):
                    for kt in range(QT):
                        for h in range(2):
                            mm = pe.matmul(c.ps[rows(h), 6 + b % 2, part * SEQ:(part + 1) * SEQ],
                                           (kvr[:, b * QT + kt, :], ones[:, :])[part], pt[:, b % 2, h, kt, :],
                                           start=(kt == 0), stop=(kt == QT - 1))
                mm.then_inc(av.sem, 1)

            def body(it, last):
                for k in range(4):
                    packed(it, k)
                scored_both(it, 0)
                packed(it, 4)
                scored_own(it, 0)
                packed(it, 5)
                for k in range(4):
                    scores(it, k)
                scored_both(it, 1)
                scored_own(it, 1)
                max_transpose(it, 0)
                for k in range(4, 8):
                    scores(it, k)
                output_weight(it)
                scores_t(it, 0)
                max_transpose(it, 1)
                scores_t(it, 1)
                product(it, 0)
                if not last:
                    fold(it + 1)
                scores_t(it, 2)
                product(it, 1)
                scores_t(it, 3)
                if not last:
                    keys(it + 1)
                product(it, 2)
                product(it, 3)

            pe.wait_ge(prep.sem, 6)
            pe.wait_ge(xp_s.sem, 2)
            fold(0)
            keys(0)
            pairs(pe, body)


FT = FFN // P


def quantise(dve, tile, scale, out, sig, first, n):
    dve.tensor_scalar(tile, tile, scale, INT8_MAX, ALU.mult, ALU.min).then_inc(sig.sem, 1)
    dve.wait_ge(sig.sem, first + 1)
    dve.tensor_scalar(tile, tile, INT8_MIN, ROUND, ALU.max, ALU.add).then_inc(sig.sem, 1)
    dve.wait_ge(sig.sem, first + 2)
    dve.tensor_scalar(out, tile, -ROUND, None, ALU.add).then_inc(sig.sem, 1)


class AlibiRows:

    STEPS = 10

    def __init__(self, c, st, hd, scale):
        def sb(n, shape, dt=F32):
            return st.enter_context(c.nc.sbuf_tensor(f"al_{n}", shape, dt))

        self.c, self.rows, self.scale = c, TERMS * hd, scale
        self.slope = sb("slope", [16, 2])
        self.wide = sb("wide", [16, 3, SEQ])
        self.pos = sb("pos", [16, SEQ])
        self.parts = sb("parts", [16, 9, SEQ], BF16)
        self.maskf = sb("maskf", [P, 2, BANK])
        self.step, self.loaded, self.filled = c.counter("at_alibi"), c.counter("at_alibi_in"), c.counter("at_fill_in")

    def moves(self, sp):
        c, loaded = self.c, self.loaded
        sp.dma_start(self.slope[:, 0:1], c.io["slopes"]).then_inc(loaded.sem, 16)
        sp.dma_start(self.pos[:, :], c.io["pos"].broadcast_to([16, SEQ])).then_inc(loaded.sem, 16)
        sp.dma_start(self.maskf[:, :, :], c.io["masks"]).then_inc(loaded.sem, 16)
        sp.wait_ge(self.step.sem, self.STEPS)
        sp.dma_start(c.scr_al.rearrange("k h q -> h k q"), self.parts[:, :, :]).then_inc(loaded.sem, 16)
        sp.wait_ge(loaded.sem, 64)
        sp.wait_ge(c.cleared.sem, c.cleared.at(4))
        per_seq = 4
        for i in range(0, ITEMS, per_seq):
            for dst, first in ((c.qs, 0), (c.ks, 3)):
                sp.dma_start(dst[self.rows:self.rows + 6, i:i + per_seq],
                             c.scr_al[first:first + 6].rearrange("k (s h) q -> k s h q", s=per_seq))\
                    .then_inc(self.filled.sem, 16)
        sp.wait_ge(self.filled.sem, 32 * ITEMS // per_seq)

    def split(self, dve):
        parts, wide, step = self.parts, self.wide, self.step
        dve.wait_ge(self.loaded.sem, 48)
        dve.tensor_copy(self.c.maskb[:, :, :], self.maskf[:, :, :]).then_inc(step.sem, 1)
        dve.tensor_copy(parts[:, 3:6, :], self.pos[:, :].unsqueeze(1).broadcast_to([16, 3, SEQ])).then_inc(step.sem, 1)
        dve.tensor_scalar(self.slope[:, 1:2], self.slope[:, 0:1], 1.0 / self.scale, None, ALU.mult)\
            .then_inc(step.sem, 1)
        dve.wait_ge(step.sem, 3)
        dve.tensor_copy(wide[:, 0, :], self.slope[:, 1:2].broadcast_to([16, SEQ])).then_inc(step.sem, 1)
        for k in range(3):
            dve.wait_ge(step.sem, 4 + 2 * k)
            dve.tensor_copy(parts[:, k, :], wide[:, k, :]).then_inc(step.sem, 1)
            if k < 2:
                dve.wait_ge(step.sem, 5 + 2 * k)
                dve.tensor_tensor(wide[:, k + 1, :], wide[:, k, :], parts[:, k, :], ALU.subtract).then_inc(step.sem, 1)
        dve.wait_ge(step.sem, 9)
        dve.tensor_scalar(parts[:, 6:9, :], parts[:, 0:3, :], -1.0, None, ALU.mult).then_inc(step.sem, 1)
        dve.wait_ge(step.sem, 10)


def ffn_stages(c):
    nc, io = c.nc, c.io
    with ExitStack() as st:
        wb, mean = c.wb, c.fmean
        layer_norm(c, "ln3", want_t=False)

        def sb(n, shape, dt=F32):
            return st.enter_context(nc.sbuf_tensor(f"f_{n}", shape, dt))

        amax, qsc = sb("amax", [P, TT]), sb("qsc", [P, TT])
        deq = sb("deq", [P, 2, TT])
        xq = sb("xq", [P, TT, DIM], BF16)
        xqT = sb("xqT", [P, DT, TOK], BF16)
        h = sb("h", [P, TT, FFN])
        sg = sb("sg", [P, 2, FFN])
        a_s, q_s, tr, ev = c.counter("f_a"), c.counter("f_q"), c.counter("f_tr"), c.counter("f_ev")
        gu, silu, hd = c.counter("f_gu"), c.counter("f_silu"), c.counter("f_h")
        sq = c.counter("f_sq")
        ssq = sb("ssq", [P, TT])
        junk = sb("junk", [P, FFN])

        def bank16(k):
            return c.ps[:, k, :].bitcast(BF16)

        alibi = AlibiRows(c, st, 16, 0.25)

        with nc.Block() as block:

            @block.sync
            def _(sp):
                w_in = c.counter("a1_w_in")
                for k in range(4):
                    sp.dma_start(c.a1_w[:, k, :, :], io["L1_WT"][k].rearrange("(t p) o -> p t o", p=P))\
                        .then_inc(w_in.sem, 16)
                alibi.moves(sp)
                sp.wait_ge(w_in.sem, 64)

            @block.vector
            def _(dve):
                dve.tensor_reduce(amax[:, :], c.xn[:, :, :], AX.X, ALU.max, apply_absolute_value=True)\
                    .then_inc(a_s.sem, 1)
                dve.wait_ge(a_s.sem, 1)
                dve.tensor_scalar(amax[:, :], amax[:, :], QUANT_EPS, None, ALU.max).then_inc(a_s.sem, 1)
                dve.wait_ge(a_s.sem, 2)
                dve.reciprocal(qsc[:, :], amax[:, :]).then_inc(a_s.sem, 1)
                dve.wait_ge(a_s.sem, 3)
                dve.tensor_scalar(qsc[:, :], qsc[:, :], INT8_MAX, None, ALU.mult).then_inc(a_s.sem, 1)
                for k in range(2):
                    dve.tensor_scalar(deq[:, k, :], amax[:, :], mean[:, k:k + 1], 1.0 / INT8_MAX,
                                      ALU.mult, ALU.mult).then_inc(a_s.sem, 1)
                dve.wait_ge(a_s.sem, 6)
                for t in range(TT):
                    dve.tensor_scalar(c.xn[:, t, :], c.xn[:, t, :], qsc[:, t:t + 1], INT8_MAX, ALU.mult, ALU.min)\
                        .then_inc(q_s.sem, 1)
                for g in range(HALF):
                    some = slice(g * TT // 2, (g + 1) * TT // 2)
                    dve.wait_ge(q_s.sem, 2 * g + TT)
                    dve.tensor_scalar(c.xn[:, some, :], c.xn[:, some, :], INT8_MIN, ROUND, ALU.max, ALU.add)\
                        .then_inc(q_s.sem, 1)
                    dve.wait_ge(q_s.sem, 2 * g + TT + 1)
                    dve.tensor_scalar(xq[:, some, :], c.xn[:, some, :], -ROUND, None, ALU.add).then_inc(q_s.sem, 1)
                alibi.split(dve)
                for t in range(TT):
                    dve.wait_ge(silu.sem, t + 1)
                    b = 4 * (t % 2) + 2
                    dve.scalar_tensor_tensor(h[:, t, :], c.ps[:, b:b + 2, :].rearrange("p b n -> p (b n)"),
                                             deq[:, 1, t:t + 1], sg[:, t % 2, :], ALU.mult, ALU.mult)\
                        .then_inc(hd.sem, 1)

            @block.tensor
            def _(pe):
                for t in range(TT):
                    if t % (TT // 2) == 0:
                        pe.wait_ge(q_s.sem, TT + 2 + 2 * (t // (TT // 2)))
                    for dt in range(DT):
                        mm = pe.transpose(bank16(dt)[:, t * P:(t + 1) * P], xq[:, t, dt * P:(dt + 1) * P],
                                          c.identb[:, :])
                mm.then_inc(tr.sem, 1)
                pe.wait_ge(ev.sem, 2)
                for t in range(TT):
                    if t >= 2:
                        pe.wait_ge(hd.sem, t - 1)
                    for k in range(2):
                        for n in range(FFN // BANK):
                            for dt in range(DT):
                                mm = pe.matmul(c.ps[:, 4 * (t % 2) + 2 * k + n, :], xqT[:, dt, t * P:(t + 1) * P],
                                               wb[:, k, dt * FFN + n * BANK:dt * FFN + (n + 1) * BANK],
                                               start=(dt == 0), stop=(dt == DT - 1))
                    mm.then_inc(gu.sem, 1)

            @block.gpsimd
            def _(pool):
                pool.memset(c.qs[:, :, :, :].bitcast(F32), 0.0).then_inc(c.cleared.sem, 1)
                pool.wait_ge(c.cleared.sem, c.cleared.at(1))
                clear_keys(c, pool)

            def square(act, t):
                act.wait_ge(hd.sem, t + 1)
                if t:
                    act.wait_ge(sq.sem, t)
                act.activation(junk[:, :], h[:, t, :], ACT.Square, accum_out=ssq[:, t:t + 1]).then_inc(sq.sem, 1)

            @block.scalar
            def _(act):
                act.wait_ge(tr.sem, 1)
                for dt in range(DT):
                    act.activation(xqT[:, dt, :], bank16(dt), ACT.Copy).then_inc(ev.sem, 1)
                for t in range(TT):
                    act.wait_ge(gu.sem, t + 1)
                    if t >= 2:
                        act.wait_ge(hd.sem, t - 1)
                    b = 4 * (t % 2)
                    act.activation(sg[:, t % 2, :], c.ps[:, b:b + 2, :].rearrange("p b n -> p (b n)"),
                                   ACT.Silu, scale=deq[:, 0, t:t + 1]).then_inc(silu.sem, 1)
                    if t >= 1:
                        square(act, t - 1)
                square(act, TT - 1)

        c.cleared.done(4)

        with ExitStack() as tmp:
            def sb2(n, shape, dt=F32):
                return tmp.enter_context(nc.sbuf_tensor(f"f2_{n}", shape, dt))

            lnw = sb2("lnw", [P, FFN])
            rstd = sb2("rstd", [P, TT])
            am, qs2 = sb2("am", [P, TT]), sb2("qs2", [P, TT])
            dd = sb2("dd", [P, TT])
            hq = sb2("hq", [P, 2, FFN], BF16)
            hqT = sb2("hqT", [P, 2, FT, P], BF16)
            lnw_in, r_s, std_s = c.counter("f2_in"), c.counter("f2_r"), c.counter("f2_std")
            v_s, n_s, m_s, k_s = c.counter("f2_v"), c.counter("f2_n"), c.counter("f2_m"), c.counter("f2_k")
            q2, tr2, ev2, y_s, x_s = (c.counter("f2_q"), c.counter("f2_tr"), c.counter("f2_ev"),
                                      c.counter("f2_y"), c.counter("f2_x"))
            with nc.Block() as block:

                @block.sync
                def _(sp):
                    sp.dma_start(lnw[:, :], io["f_ln"].broadcast_to([P, FFN])).then_inc(lnw_in.sem, 16)

                @block.scalar
                def _(act):
                    act.wait_ge(r_s.sem, 1)
                    act.activation(rstd[:, :], rstd[:, :], ACT.Sqrt).then_inc(std_s.sem, 1)

                    def normalise(t):
                        act.activation(h[:, t, :], h[:, t, :], ACT.Copy, scale=rstd[:, t:t + 1]).then_inc(v_s.sem, 1)

                    act.wait_ge(r_s.sem, 2)
                    for t in range(3):
                        normalise(t)
                    for t in range(TT):
                        act.wait_ge(tr2.sem, t + 1)
                        if t >= 2:
                            act.wait_ge(y_s.sem, t - 1)
                        act.activation(hqT[:, t % 2, :, :].rearrange("p f n -> p (f n)"), bank16(t % 2), ACT.Copy)\
                            .then_inc(ev2.sem, 1)
                        if t + 3 < TT:
                            normalise(t + 3)

                @block.gpsimd
                def _(pool):
                    pool.wait_ge(lnw_in.sem, 16)
                    for t in range(TT):
                        pool.wait_ge(v_s.sem, t + 1)
                        pool.tensor_tensor(h[:, t, :], h[:, t, :], lnw[:, :], ALU.mult).then_inc(n_s.sem, 1)

                @block.vector
                def _(dve):
                    dve.tensor_scalar(rstd[:, :], ssq[:, :], 1.0 / FFN, RMS_EPS, ALU.mult, ALU.add)\
                        .then_inc(r_s.sem, 1)
                    dve.wait_ge(std_s.sem, 1)
                    dve.reciprocal(rstd[:, :], rstd[:, :]).then_inc(r_s.sem, 1)

                    def residual(t):
                        dve.wait_ge(y_s.sem, t + 1)
                        dve.scalar_tensor_tensor(c.x[:, t, :], c.ps[:, 2 + t % 2, 0:DIM], dd[:, t:t + 1],
                                                 c.x[:, t, :], ALU.mult, ALU.add).then_inc(x_s.sem, 1)

                    for t in range(TT):
                        one = slice(t, t + 1)
                        dve.wait_ge(n_s.sem, t + 1)
                        dve.tensor_reduce(am[:, one], h[:, t, :], AX.X, ALU.max, apply_absolute_value=True)\
                            .then_inc(m_s.sem, 1)
                        dve.wait_ge(m_s.sem, t + 1)
                        dve.tensor_scalar(am[:, one], am[:, one], QUANT_EPS, None, ALU.max).then_inc(k_s.sem, 1)
                        dve.wait_ge(k_s.sem, 4 * t + 1)
                        dve.reciprocal(qs2[:, one], am[:, one]).then_inc(k_s.sem, 1)
                        dve.tensor_scalar(dd[:, one], am[:, one], mean[:, 2:3], 1.0 / INT8_MAX, ALU.mult, ALU.mult)\
                            .then_inc(k_s.sem, 1)
                        dve.wait_ge(k_s.sem, 4 * t + 2)
                        dve.tensor_scalar(qs2[:, one], qs2[:, one], INT8_MAX, None, ALU.mult).then_inc(k_s.sem, 1)
                        dve.wait_ge(k_s.sem, 4 * t + 4)
                        if t >= 2:
                            dve.wait_ge(tr2.sem, t - 1)
                        quantise(dve, h[:, t, :], qs2[:, one], hq[:, t % 2, :], q2, 3 * t, TT)
                        if t >= 1:
                            residual(t - 1)
                    residual(TT - 1)
                    dve.wait_ge(x_s.sem, TT)

                @block.tensor
                def _(pe):
                    for t in range(TT + 1):
                        if t >= 1:
                            u = t - 1
                            pe.wait_ge(ev2.sem, u + 1)
                            if u >= 2:
                                pe.wait_ge(x_s.sem, u - 1)
                            for f in range(FT):
                                mm = pe.matmul(c.ps[:, 2 + u % 2, 0:DIM], hqT[:, u % 2, f, :],
                                               wb[:, 2, f * DIM:(f + 1) * DIM],
                                               start=(f == 0), stop=(f == FT - 1))
                            mm.then_inc(y_s.sem, 1)
                        if t < TT:
                            pe.wait_ge(q2.sem, 3 * t + 3)
                            if t >= 2:
                                pe.wait_ge(ev2.sem, t - 1)
                            for f in range(FT):
                                mm = pe.transpose(bank16(t % 2)[:, f * P:(f + 1) * P],
                                                  hq[:, t % 2, f * P:(f + 1) * P], c.identb[:, :])
                            mm.then_inc(tr2.sem, 1)


def layer1_attentions(c):
    nc, io = c.nc, c.io
    with ExitStack() as st:
        with ExitStack() as own:
            w = c.a1_w
            layer_norm(c, "ln4")
            v = qkv_stage(c, own, "a1", w[:, 0], w[:, 1], w[:, 2], "L1_bias", c.scr_q, c.scr_k)
            av = own.enter_context(nc.sbuf_tensor("a1_av", [P, 4, TOK], F32))
            attention_stage(c, "a1", 16, False, 0.25, v, c.scr_q, c.scr_k, av, alibi=True)
            normalise_stage(c, own, "a1n", 4, 16, av, w[:, 3], "L1_bias")
        layer_norm(c, "ln5")
        with ExitStack() as own:
            v = own.enter_context(nc.sbuf_tensor("x1_v", [P, TT, CTX], F32))
            split_context(c, v)
            av = own.enter_context(nc.sbuf_tensor("x1_av", [P, 8, TOK], F32))
            attention_stage(c, "x1", 8, True, 8.0 ** -0.5, v, c.scr_xq, c.scr_xk, av)
            normalise_stage(c, own, "x1n", 8, 8, av, None, None)


def split_context(c, v):
    nc, io = c.nc, c.io
    with ExitStack() as tmp:
        def sb(n, shape, dt=F32):
            return tmp.enter_context(nc.sbuf_tensor(f"xs_{n}", shape, dt))

        qp = sb("qp", [P, DT, 3, TOK], BF16)
        kp = sb("kp", [CTX, 3, TOK], BF16)
        qrest, krest = sb("qrest", [P, DT, TOK]), sb("krest", [CTX, TOK])
        v_in, tr, k_s, qh, q_r, q_m, ql, stored, cleared = (
            c.counter("xs_v"), c.counter("xs_tr"), c.counter("xs_k"), c.counter("xs_qh"), c.counter("xs_qr"),
            c.counter("xs_qm"), c.counter("xs_ql"), c.counter("xs_st"), c.counter("xs_cleared"))
        kps = c.ps[0:CTX, 0:2, :].rearrange("p b n -> p (b n)")
        with nc.Block() as block:

            @block.sync
            def _(sp):
                sp.dma_start(v[:, :, :], io["ctx"].rearrange("(t p) d -> p t d", p=P)).then_inc(v_in.sem, 16)
                for part, (q_done, k_count) in enumerate(((qh, 1), (q_m, 3), (ql, 4))):
                    for dt in range(DT):
                        sp.wait_ge(q_done.sem, dt + 1)
                        store_part(sp, 0, part, c.scr_xq[16 * dt:16 * dt + 16], qp[:, dt, :, :], stored)
                    sp.wait_ge(k_s.sem, k_count)
                    store_part(sp, 1, part, c.scr_xk, kp[:, :, :], stored)
                sp.wait_ge(stored.sem, 16 * TERMS * (DT + 1))

            @block.gpsimd
            def _(pool):
                for k, (tile, first) in enumerate(((c.qs[:, :, :, :], 0), (c.ks[:, :, 0:1, :], 0),
                                                   (c.qs[:, :, :, :], 96), (c.ks[:, :, 0:1, :], 96))):
                    rows = slice(0, 96) if first == 0 else slice(96, P - 2)
                    pool.memset(tile[rows].bitcast(F32), 0.0).then_inc(cleared.sem, 1)
                    pool.wait_ge(cleared.sem, k + 1)

            @block.tensor
            def _(pe):
                pe.wait_ge(v_in.sem, 16)
                for t in range(TT):
                    mm = pe.transpose(c.ps[0:CTX, t // 4, (t % 4) * P:(t % 4 + 1) * P], v[:, t, :],
                                      c.ident[:, :])
                mm.then_inc(tr.sem, 1)

            @block.scalar
            def _(act):
                for dt in range(DT):
                    act.activation(qp[:, dt, 0, :], c.xnT[:, dt, :], ACT.Copy).then_inc(qh.sem, 1)
                act.wait_ge(tr.sem, 1)
                act.activation(kp[:, 0, :], kps, ACT.Copy).then_inc(k_s.sem, 1)
                for dt in range(DT):
                    act.wait_ge(q_r.sem, dt + 1)
                    act.activation(qp[:, dt, 1, :], qrest[:, dt, :], ACT.Copy).then_inc(q_m.sem, 1)
                act.wait_ge(k_s.sem, 2)
                act.activation(kp[:, 1, :], krest[:, :], ACT.Copy).then_inc(k_s.sem, 1)

            @block.vector
            def _(dve):
                for dt in range(DT):
                    dve.wait_ge(qh.sem, dt + 1)
                    dve.tensor_tensor(qrest[:, dt, :], c.xnT[:, dt, :], qp[:, dt, 0, :], ALU.subtract)\
                        .then_inc(q_r.sem, 1)
                dve.wait_ge(k_s.sem, 1)
                dve.tensor_tensor(krest[:, :], kps, kp[:, 0, :], ALU.subtract).then_inc(k_s.sem, 1)
                for dt in range(DT):
                    dve.wait_ge(q_m.sem, dt + 1)
                    dve.tensor_tensor(qp[:, dt, 2, :], qrest[:, dt, :], qp[:, dt, 1, :], ALU.subtract)\
                        .then_inc(ql.sem, 1)
                dve.wait_ge(k_s.sem, 3)
                dve.tensor_tensor(kp[:, 2, :], krest[:, :], kp[:, 1, :], ALU.subtract).then_inc(k_s.sem, 1)


def moe_stages(c):
    nc, io = c.nc, c.io
    layer_norm(c, "ln6")
    NX = EXPERTS + 1
    with ExitStack() as st:
        def sb(n, shape, dt=F32):
            return st.enter_context(nc.sbuf_tensor(f"x_{n}", shape, dt))

        gw = sb("gw", [P, DT, EXPERTS])
        iota = sb("iota", [P, EXPERTS])
        score = sb("score", [P, TT, EXPERTS])
        best = sb("best", [P, TT, 8])
        bidx = sb("bidx", [P, TT, 8], U32)
        bidf = sb("bidf", [P, TT, TOPK])
        hit = sb("hit", [P, TOPK, TT, EXPERTS])
        gate = sb("gate", [P, TT, NX])
        gT = sb("gT", [NX, TOK])
        g_in, logit, sc = c.counter("x_gate_in"), c.counter("x_logit"), c.counter("x_score")
        mxs, ids, st_s = c.counter("x_max"), c.counter("x_ids"), c.counter("x_step")
        gtr, gev, gst = c.counter("x_gtr"), c.counter("x_gev"), c.counter("x_gst")

        with nc.Block() as block:

            @block.sync
            def _(sp):
                sp.dma_start(gw[:, :, :], io["gate_wT"].rearrange("(t p) e -> p t e", p=P)).then_inc(g_in.sem, 16)
                sp.dma_start(iota[:, :], io["iota"].broadcast_to([P, EXPERTS])).then_inc(g_in.sem, 16)
                sp.wait_ge(gev.sem, 1)
                sp.dma_start(c.scr_g, gT[:, :]).then_inc(gst.sem, 16)
                sp.wait_ge(gst.sem, 16)

            @block.tensor
            def _(pe):
                pe.wait_ge(g_in.sem, 32)
                for t in range(TT):
                    for dt in range(DT):
                        mm = pe.matmul(c.ps[:, 0, t * EXPERTS:(t + 1) * EXPERTS], c.xnT[:, dt, t * P:(t + 1) * P],
                                       gw[:, dt, :], start=(dt == 0), stop=(dt == DT - 1))
                mm.then_inc(logit.sem, 1)
                pe.wait_ge(st_s.sem, 7)
                for t in range(TT):
                    mm = pe.transpose(c.ps[0:NX, 1 + t // 4, (t % 4) * P:(t % 4 + 1) * P], gate[:, t, :],
                                      c.ident[:, :])
                mm.then_inc(gtr.sem, 1)

            @block.scalar
            def _(act):
                act.wait_ge(logit.sem, 1)
                act.activation(score[:, :, :].rearrange("p t e -> p (t e)"), c.ps[:, 0, 0:TT * EXPERTS],
                               ACT.Sigmoid).then_inc(sc.sem, 1)
                act.wait_ge(gtr.sem, 1)
                act.activation(gT[:, :], c.ps[0:NX, 1:3, :].rearrange("p b n -> p (b n)"), ACT.Copy)\
                    .then_inc(gev.sem, 1)

            @block.vector
            def _(dve):
                dve.memset(gate[:, :, :], 1.0).then_inc(st_s.sem, 1)
                dve.wait_ge(sc.sem, 1)
                for t in range(TT):
                    dve.max(best[:, t, :], score[:, t, :]).then_inc(mxs.sem, 1)
                for t in range(TT):
                    dve.wait_ge(mxs.sem, t + 1)
                    dve.max_index(bidx[:, t, :], best[:, t, :], score[:, t, :]).then_inc(ids.sem, 1)
                dve.wait_ge(ids.sem, TT)
                dve.tensor_copy(bidf[:, :, :], bidx[:, :, 0:TOPK]).then_inc(st_s.sem, 1)
                dve.wait_ge(st_s.sem, 2)
                for k in range(TOPK):
                    dve.tensor_tensor(hit[:, k, :, :], iota[:, :].unsqueeze(1).broadcast_to([P, TT, EXPERTS]),
                                      bidf[:, :, k:k + 1].broadcast_to([P, TT, EXPERTS]), ALU.is_equal)\
                        .then_inc(st_s.sem, 1)
                for k in range(TOPK):
                    dve.wait_ge(st_s.sem, 3 + k)
                    dve.tensor_tensor(hit[:, k, :, :], hit[:, k, :, :],
                                      best[:, :, k:k + 1].broadcast_to([P, TT, EXPERTS]), ALU.mult)\
                        .then_inc(st_s.sem, 1)
                dve.wait_ge(st_s.sem, 6)
                dve.tensor_tensor(gate[:, :, 0:EXPERTS], hit[:, 0, :, :], hit[:, 1, :, :], ALU.add)\
                    .then_inc(st_s.sem, 1)

        BUF = 3
        w13 = sb("w13", [P, BUF, 2, DT, EH])
        w2 = sb("w2", [P, BUF, DIM])
        gb = sb("gb", [P, BUF, TOK])
        w13p = sb("w13p", [P, BUF, 2, 2 * DT * EH], F32R)
        w2p = sb("w2p", [P, BUF, 2, DIM], F32R)
        xp = sb("xp", [P, 2, DT, TOK], F32R)
        hTp = sb("hTp", [P, 2, 2, BANK], F32R)
        one = sb("one", [P, 2 * DT * EH])
        h1g = sb("h1g", [P, 2, BANK])
        sg = sb("sg", [P, 2, BANK])
        h3 = sb("h3", [P, 2, BANK])
        hT = sb("hT", [P, 2, BANK])
        w_in = [c.counter(f"e_in{b}") for b in range(BUF)]
        p13, gm, sl, m3, hd = c.counter("e_p13"), c.counter("e_gm"), c.counter("e_silu"), c.counter("e_m3"), c.counter("e_h")
        down, seeded, x_s = c.counter("e_down"), c.counter("e_seed"), c.counter("e_x")
        wp_hi, wp_s, hp_hi, hp, xps = (c.counter(f"at_m{k}") for k in range(5))
        D0 = 2 * BUF
        M0 = 1
        TERMS3 = ((0, 0), (0, 1), (1, 0))
        with nc.Block() as block:

            @block.sync
            def _(sp):
                with sp.Fori(0, NX // BUF) as it:
                    for b in range(BUF):
                        e = it * BUF + b
                        sp.wait_ge(down.sem, e * 2 + 2)
                        one = bass.ds(e, 1)
                        sp.dma_start(w13[:, b], io["e_w13"][one]).then_inc(w_in[b].sem, 16)
                        sp.dma_start(w2[:, b], io["e_w2"][one]).then_inc(w_in[b].sem, 16)
                        sp.dma_start(gb[:, b], c.scr_g[one, :].broadcast_to([P, TOK])).then_inc(w_in[b].sem, 16)

            @block.vector
            def _(dve):
                dve.sem_inc(down.sem, D0)
                dve.sem_inc(m3.sem, M0)
                dve.wait_ge(xps.sem, xps.at(1))
                dve.tensor_tensor(xp[:, 1, :, :], c.xnT[:, :, :], xp[:, 0, :, :].bitcast(F32), ALU.subtract)\
                    .then_inc(xps.sem, 1)
                with dve.Fori(0, NX // BUF) as it:
                    for k in range(2 * BUF):
                        b, half = k // 2, k % 2
                        n = it * (2 * BUF) + k
                        cols = slice(half * BANK, (half + 1) * BANK)
                        dve.wait_ge(w_in[b].sem, it * 48 + 48)
                        dve.wait_ge(p13.sem, n * 2 + 1)
                        dve.tensor_tensor(h1g[:, half, :], c.ps[:, 4 + half, :], gb[:, b, cols], ALU.mult)\
                            .then_inc(gm.sem, 1)
                        dve.wait_ge(sl.sem, n + 1)
                        dve.wait_ge(p13.sem, n * 2 + 2)
                        dve.tensor_tensor(h3[:, half, :], c.ps[:, 6 + half, :], sg[:, half, :], ALU.mult)\
                            .then_inc(m3.sem, 1)
                        dve.wait_ge(m3.sem, n + (M0 + 1))
                        dve.tensor_tensor(hT[:, half, :], h3[:, half, :], gb[:, b, cols], ALU.mult)\
                            .then_inc(hd.sem, 1)
                        dve.wait_ge(hp_hi.sem, hp_hi.at(n + 1))
                        dve.tensor_tensor(hTp[:, half, 1, :], hT[:, half, :], hTp[:, half, 0, :].bitcast(F32),
                                          ALU.subtract).then_inc(hp.sem, 1)
                for t in range(TT):
                    if t == 0:
                        dve.wait_ge(down.sem, D0 + 2 * NX)
                    dve.tensor_copy(c.x[:, t, :], c.ps[:, t // 2, (t % 2) * DIM:(t % 2 + 1) * DIM])\
                        .then_inc(x_s.sem, 1)
                dve.wait_ge(x_s.sem, TT)

            @block.scalar
            def _(act):
                act.activation(xp[:, 0, :, :], c.xnT[:, :, :], ACT.Copy).then_inc(xps.sem, 1)
                with act.Fori(0, NX // BUF) as it:
                    for k in range(2 * BUF):
                        n = it * (2 * BUF) + k
                        act.wait_ge(gm.sem, n + 1)
                        act.activation(sg[:, k % 2, :], h1g[:, k % 2, :], ACT.Silu).then_inc(sl.sem, 1)
                        act.wait_ge(down.sem, n + (D0 - 1))
                        act.wait_ge(hd.sem, n + 1)
                        act.activation(hTp[:, k % 2, 0, :], hT[:, k % 2, :], ACT.Copy).then_inc(hp_hi.sem, 1)

            @block.gpsimd
            def _(pool):
                pool.memset(one[:, :], 1.0).then_inc(seeded.sem, 1)
                pool.wait_ge(seeded.sem, 1)
                with pool.Fori(0, NX // BUF) as it:
                    for b in range(BUF):
                        e = it * BUF + b
                        pool.wait_ge(w_in[b].sem, it * 48 + 48)
                        for k, (parts, w) in enumerate((
                                (w13p[:, b], w13[:, b, :, :, :].rearrange("p j t h -> p (j t h)")),
                                (w2p[:, b], w2[:, b, :]))):
                            pool.tensor_tensor(parts[:, 0, :], w, one[:, 0:w.shape[1]], ALU.mult)\
                                .then_inc(wp_hi.sem, 1)
                            pool.wait_ge(wp_hi.sem, wp_hi.at(e * 2 + (k + 1)))
                            pool.tensor_tensor(parts[:, 1, :], w, parts[:, 0, :].bitcast(F32), ALU.subtract)\
                                .then_inc(wp_s.sem, 1)

            @block.tensor
            def _(pe):
                for k in range(TT // 2):
                    pe.matmul(c.ps[:, k, :], c.ident[:, :], c.x[:, 2 * k:2 * k + 2, :].rearrange("p t d -> p (t d)"),
                              start=True, stop=True)

                pe.wait_ge(xps.sem, xps.at(2))

                def up(it, k):
                    b, half = k // 2, k % 2
                    n = it * (2 * BUF) + k
                    if half == 0:
                        pe.wait_ge(wp_s.sem, wp_s.at((it * BUF + b) * 2 + 1))
                    if not (isinstance(it, int) and it == 0 and k == 0):
                        pe.wait_ge(m3.sem, n + (M0 - 1))
                    for j in range(2):
                        terms = [(dt, w, x) for dt in range(DT) for w, x in TERMS3]
                        for dt, w, x in terms:
                            at = (j * DT + dt) * EH
                            mm = pe.matmul(c.ps[:, 4 + 2 * j + half, :], w13p[:, b, w, at:at + EH],
                                           xp[:, x, dt, half * BANK:(half + 1) * BANK],
                                           start=((dt, w, x) == terms[0]), stop=((dt, w, x) == terms[-1]))
                        mm.then_inc(p13.sem, 1)

                def add(it, k):
                    b, half = k // 2, k % 2
                    n = it * (2 * BUF) + k
                    pe.wait_ge(hp.sem, hp.at(n + 1))
                    if half == 0:
                        pe.wait_ge(wp_s.sem, wp_s.at((it * BUF + b) * 2 + 2))
                    for j in range(4):
                        t = 4 * half + j
                        for h, w in TERMS3:
                            mm = pe.matmul(c.ps[:, t // 2, (t % 2) * DIM:(t % 2 + 1) * DIM],
                                           hTp[:, half, h, j * P:(j + 1) * P], w2p[:, b, w, :],
                                           start=False, stop=True, skip_group_check=True)
                    mm.then_inc(down.sem, 1)

                def body(it, last):
                    for k in range(2 * BUF):
                        if k + 1 < 2 * BUF:
                            up(it, k + 1)
                        elif not last:
                            up(it + 1, 0)
                        add(it, k)

                up(0, 0)
                with pe.Fori(0, NX // BUF - 1) as it:
                    body(it, False)
                body(NX // BUF - 1, True)


def store_stage(c, out):
    nc = c.nc
    stored = c.counter("qkv_stored")
    with nc.Block() as block:

        @block.sync
        def _(sp):
            sp.dma_start(out.rearrange("(t p) d -> p t d", p=P), c.x[:, :, :]).then_inc(stored.sem, 16)
            sp.wait_ge(stored.sem, stored.at(16))


def build_program(nc, io, out):
    with ExitStack() as ctx:
        c = Chip(nc, ctx, io)
        permanent_buffers(c)
        c.scr_q = nc.dram_tensor("scr_q", (16, TERMS, 16, TOK), BF16, kind="Internal").ap()
        c.scr_k = nc.dram_tensor("scr_k", (16, TERMS, 16, TOK), BF16, kind="Internal").ap()
        c.scr_xq = nc.dram_tensor("scr_xq", (32, TERMS, 8, TOK), BF16, kind="Internal").ap()
        c.scr_xk = nc.dram_tensor("scr_xk", (8, TERMS, 8, TOK), BF16, kind="Internal").ap()
        c.scr_g = nc.dram_tensor("scr_g", (EXPERTS + 1, TOK), F32, kind="Internal").ap()
        c.scr_al = nc.dram_tensor("scr_al", (9, 16, SEQ), BF16, kind="Internal").ap()

        with ExitStack() as st:
            stack_slots(c, st, "a0")
            rank = io["L0_B"].shape[1]
            c.lora = (st.enter_context(nc.sbuf_tensor("lora_wT", [P, 4, DT, DIM], F32)),
                      st.enter_context(nc.sbuf_tensor("lora_b", [rank, 4, DIM], F32)),
                      st.enter_context(nc.sbuf_tensor("lora_aT", [rank, 4, DIM], F32)))
            load_stage(c)
            layer_norm(c, "ln1", beside=lambda pool: clear_keys(c, pool, (0, 1)))
            wT = lora_fold(c)
            v = qkv_stage(c, st, "a0", wT[:, 0], wT[:, 1], wT[:, 2], "L0_bias", c.scr_q, c.scr_k)
            av = st.enter_context(nc.sbuf_tensor("a0_av", [P, 4, TOK], F32))
            attention_stage(c, "a0", 16, False, 0.25, v, c.scr_q, c.scr_k, av)
            normalise_stage(c, st, "a0n", 4, 16, av, wT[:, 3], "L0_bias")
        mla_stages(c)
        with ExitStack() as st:
            stack_slots(c, st, "a1")
            c.maskb = st.enter_context(nc.sbuf_tensor("a1_maskb", [P, 2, BANK], BF16))
            c.a1_w = st.enter_context(nc.sbuf_tensor("a1_w", [P, 4, DT, DIM], F32))
            ffn_stages(c)
            layer1_attentions(c)
        moe_stages(c)
        store_stage(c, out)



def _constants():
    q = np.arange(SEQ)
    causal = np.where(q[None, :P] <= q[:P, None], 0.0, NEG).astype(np.float32)
    masks = np.stack([np.concatenate([causal] * 4, 1), np.concatenate([causal.T] * 4, 1)], 1)
    pos = q.astype(np.float32).reshape(1, SEQ)

    def rope(length, dim):
        inv = (np.float32(1.0) / np.float32(10000.0) ** (np.arange(0, dim, 2, dtype=np.float32) / np.float32(dim)))
        f = np.arange(length, dtype=np.float32)[:, None] * inv.astype(np.float32)[None, :]
        return np.repeat(np.sin(f), 2, -1).astype(np.float32), np.repeat(np.cos(f), 2, -1).astype(np.float32)

    sin_q, cos_q = rope(SEQ, DCQ)
    hq = DCQ // 2
    sin_moved = np.concatenate([sin_q[:, hq:], -sin_q[:, :hq]], 1)
    rope_q = np.stack([np.concatenate([t.T, t.T]).reshape(3, P, SEQ) for t in (cos_q, sin_moved)])
    sin_k, cos_k = rope(SEQ, CTX)
    hk = CTX // 2
    sin_signed = np.concatenate([-sin_k[:, :hk], sin_k[:, hk:]], 1)
    rope_k = np.stack([t.reshape(QT, P, CTX) for t in (cos_k, sin_signed)])
    return dict(ident=np.eye(P, dtype=np.float32), masks=masks, pos=pos,
                rope_q=rope_q.transpose(2, 0, 1, 3), rope_k=rope_k.transpose(2, 0, 1, 3))


def _columns(rows):
    return rows.reshape(len(rows), DT, P).transpose(2, 0, 1)


def _layout(inputs):
    k = _constants()
    c = np.ascontiguousarray
    a = {n: np.asarray(v) for n, v in inputs.items()}
    io = {
        "x": c(a["x"].reshape(TOK, DIM)),
        "ident": k["ident"], "masks": c(k["masks"]), "pos": c(k["pos"]),
        "L0_WT": np.stack([a[f"L0_attn_W{n}"].T for n in "qkvo"]),
        "L0_B": np.stack([a[f"L0_attn_B{n}"] for n in "qkvo"]),
        "L0_AT": np.stack([a[f"L0_attn_A{n}"].T for n in "qkvo"]),
        "L0_bias": np.stack([a[f"L0_attn_b{n}"] for n in "qkvo"]),
        "L0_bias_col": _columns(np.stack([a["L0_attn_bq"], a["L0_attn_bk"]])),
        "slopes": c(a["L1_attn_alibi_slopes"].reshape(16, 1)),
    }
    wqr = a["L0_xattn_W_qr"]
    wr = np.zeros((PAIRS, 2, 2 * DCQ, 2, R), np.float32)
    for h in range(2):
        for cs, moved in enumerate((wqr, np.roll(wqr, -(DCQ // 2), 1))):
            wr[:, cs, h * DCQ:(h + 1) * DCQ, h] = moved[h::2]
    wkr = np.zeros((PAIRS, P, 2, R), np.float32)
    for h in range(2):
        wkr[:, 0:CTX, h] = a["L0_xattn_W_kr"][h::2]
    pairs = lambda w, r: w.reshape(PAIRS, 2, P, r).transpose(0, 2, 1, 3)
    io.update({
        "ctx": a["ctx_512"].reshape(TOK, CTX),
        "rope_q": k["rope_q"], "rope_k": k["rope_k"],
        "m_wq": pairs(a["L0_xattn_Wq"], DIM), "m_wkq": pairs(a["L0_xattn_w_kc_q"], DCQ),
        "m_wr": wr.reshape(PAIRS, 2, 3, P, 2 * R).transpose(0, 3, 1, 2, 4),
        "m_wkr": wkr.reshape(PAIRS, P, 2 * R),
        "m_wkv": pairs(a["L0_xattn_w_kc_kv"], CTX), "m_wo": pairs(a["L0_xattn_Wo"].T, DIM),
    })
    tiles = lambda w: w.reshape(-1, P, w.shape[-1]).transpose(1, 0, 2).reshape(P, -1)
    qkv = a["L1_attn_qkv_w"].reshape(3, DIM, DIM)
    bias = np.concatenate([a["L1_attn_qkv_b"].reshape(3, DIM), a["L1_attn_out_b"][None]])
    w1 = np.concatenate([a["L1_ffn_w1"], a["L1_ffn_ws1"][None]])
    w3 = np.concatenate([a["L1_ffn_w3"], a["L1_ffn_ws3"][None]])
    w2 = np.concatenate([a["L1_ffn_w2"], a["L1_ffn_ws2"][None]])
    io.update({
        "f_w": np.stack([tiles(a["L0_ffn_w_gate"].T), tiles(a["L0_ffn_w_up"].T), tiles(a["L0_ffn_w_down"].T)]),
        "f_ln": a["L0_ffn_ln_weight"].reshape(1, FFN),
        "L1_WT": np.concatenate([qkv, a["L1_attn_out_w"][None]]).transpose(0, 2, 1),
        "L1_bias": bias, "L1_bias_col": _columns(bias[0:2]),
        "gate_wT": a["L1_ffn_gate_w"].T, "iota": np.arange(EXPERTS, dtype=np.float32).reshape(1, EXPERTS),
        "e_w13": np.stack([w1, w3], 1).reshape(EXPERTS + 1, 2, EH, DT, P).transpose(0, 4, 1, 3, 2),
        "e_w2": w2.transpose(0, 2, 1),
    })
    return {n: c(v) for n, v in io.items()}


def kernel(**inputs):
    import concourse.bacc as bacc
    from concourse.bass_utils import run_bass_kernel_spmd

    nc = bacc.Bacc("TRN2", target_bir_lowering=False, num_devices=1)
    arrays = _layout(inputs)
    io = {n: nc.dram_tensor(f"in_{n}", v.shape, mybir.dt.from_np(v.dtype), kind="ExternalInput").ap()
          for n, v in arrays.items()}
    out = nc.dram_tensor("out_x", (TOK, DIM), F32, kind="ExternalOutput").ap()
    build_program(nc, io, out)
    r = run_bass_kernel_spmd(nc, [{f"in_{n}": v for n, v in arrays.items()}], core_ids=[0])
    return r.results[0]["out_x"].reshape(BATCH, SEQ, DIM)
```
